# Optimizing a Trainium2 kernel written in Bass

```python
import numpy as np
import jax
import jax.numpy as jnp

def _softmax(x, axis=-1):
    return jax.nn.softmax(x, axis=axis)

def _gelu(x):
    return jax.nn.gelu(x, approximate=True)

def _silu(x):
    return jax.nn.silu(x)

def _sigmoid(x):
    return jax.nn.sigmoid(x)

def _layernorm(x, axis=-1, eps=1e-05):
    m = jnp.mean(x, axis=axis, keepdims=True)
    v = jnp.var(x, axis=axis, keepdims=True)
    return (x - m) / jnp.sqrt(v + eps)

def _scatter_add(tgt, idx, src, axis=0):
    return tgt.at[idx].add(src)

def _segment_sum(src, seg, n):
    return jax.ops.segment_sum(src, seg, n)
kernel_name = 'mk_seq_postln_d1_jaxref_r8_d1e773'

def setup_inputs(seed: int=0):
    np.random.seed(seed)
    _w = jnp.asarray

    def _L0_attn_setup():
        import jax, jax.numpy as jnp
        import numpy as np
        DIM = 256
        N_HEADS = 16
        KV_RANK = 64
        NOPE = 128
        ROPE = 64
        VDIM = 128
        QK_HEAD = NOPE + ROPE
        THETA = 10000.0
        EPS = 1e-06
        SCALE = QK_HEAD ** (-0.5)
        NEG_INF = -1e+30

        def precompute_freqs(seq_len, head_dim, theta=THETA):
            freqs = 1.0 / theta ** (np.arange(0, head_dim, 2, dtype=np.float32) / head_dim)
            ang = np.outer(np.arange(seq_len, dtype=np.float32), freqs)
            return (jnp.asarray(np.cos(ang)), jnp.asarray(np.sin(ang)))

        def apply_rope(x, cos, sin):
            x2 = x.reshape(*x.shape[:-1], -1, 2)
            x0, x1 = (x2[..., 0], x2[..., 1])
            c = cos[None, :, None, :]
            s = sin[None, :, None, :]
            r0 = x0 * c - x1 * s
            r1 = x0 * s + x1 * c
            return jnp.stack([r0, r1], axis=-1).reshape(x.shape)

        def rmsnorm(x, w, eps=EPS):
            rms = jnp.sqrt(jnp.mean(x * x, axis=-1, keepdims=True) + eps)
            return x / rms * w
        key = jax.random.key(seed)
        ks = jax.random.split(key, 5)
        B, S = (2, 256)
        sc = lambda n: 1.0 / np.sqrt(n)
        return {'x': jax.random.normal(ks[0], (B, S, DIM), jnp.float32), 'wq': jax.random.normal(ks[1], (N_HEADS * QK_HEAD, DIM), jnp.float32) * sc(DIM), 'wkv_a': jax.random.normal(ks[2], (KV_RANK + ROPE, DIM), jnp.float32) * sc(DIM), 'wkv_b': jax.random.normal(ks[3], (N_HEADS * (NOPE + VDIM), KV_RANK), jnp.float32) * sc(KV_RANK), 'wo': jax.random.normal(ks[4], (DIM, N_HEADS * VDIM), jnp.float32) * sc(N_HEADS * VDIM), 'kv_norm_w': jnp.ones((KV_RANK,), jnp.float32)}
    _L0_attn_in = _L0_attn_setup()

    def _L0_ffn_setup():
        import jax, jax.numpy as jnp
        import numpy as np
        TOP_K = 6
        CAP_FACTOR = 2

        def _moe_block(x2d, wg_router, w_gate, w_up, w_down, ws_gate, ws_up, ws_down):
            T, D = x2d.shape
            E = wg_router.shape[0]
            scores = jax.nn.softmax(x2d @ wg_router.T, axis=-1)
            topk_w, topk_idx = jax.lax.top_k(scores, TOP_K)
            topk_w = topk_w / (jnp.sum(topk_w, axis=-1, keepdims=True) + 1e-20)
            flat_idx = topk_idx.reshape(-1)
            oh = jax.nn.one_hot(flat_idx, E, dtype=jnp.int32)
            pos = jnp.cumsum(oh, axis=0) - 1
            pos_in_e = jnp.take_along_axis(pos, flat_idx[:, None], axis=1)[:, 0]
            C = CAP_FACTOR * (T * TOP_K // E)
            valid = pos_in_e < C
            safe_pos = jnp.where(valid, pos_in_e, 0)
            tok_id = jnp.repeat(jnp.arange(T), TOP_K)
            vmask = valid[:, None].astype(x2d.dtype)
            x_rep = x2d[tok_id] * vmask
            xe = jnp.zeros((E, C, D), x2d.dtype).at[flat_idx, safe_pos].add(x_rep)
            g = jnp.einsum('ecd,edf->ecf', xe, w_gate)
            u = jnp.einsum('ecd,edf->ecf', xe, w_up)
            ye = jnp.einsum('ecf,efd->ecd', jax.nn.silu(g) * u, w_down)
            y_tok = ye[flat_idx, safe_pos] * vmask
            y = jnp.sum(y_tok.reshape(T, TOP_K, D) * topk_w[..., None], axis=1)
            sh = jax.nn.silu(x2d @ ws_gate) * (x2d @ ws_up) @ ws_down
            return y + sh
        key = jax.random.key(seed)
        ks = jax.random.split(key, 9)
        B, S, D, F, E = (1, 256, 256, 176, 32)
        FS = F * 2
        s = 0.02
        return {'hidden_states': jax.random.normal(ks[0], (B, S, D), jnp.float32), 'wg_router': jax.random.normal(ks[1], (E, D), jnp.float32) * s, 'w_gate': jax.random.normal(ks[2], (E, D, F), jnp.float32) * s, 'w_up': jax.random.normal(ks[3], (E, D, F), jnp.float32) * s, 'w_down': jax.random.normal(ks[4], (E, F, D), jnp.float32) * s, 'ws_gate': jax.random.normal(ks[5], (D, FS), jnp.float32) * s, 'ws_up': jax.random.normal(ks[6], (D, FS), jnp.float32) * s, 'ws_down': jax.random.normal(ks[7], (FS, D), jnp.float32) * s}
    _L0_ffn_in = _L0_ffn_setup()
    _d = {'L0_attn_x': _L0_attn_in['x'], 'L0_attn_wq': _L0_attn_in['wq'], 'L0_attn_wkv_a': _L0_attn_in['wkv_a'], 'L0_attn_wkv_b': _L0_attn_in['wkv_b'], 'L0_attn_wo': _L0_attn_in['wo'], 'L0_attn_kv_norm_w': _L0_attn_in['kv_norm_w'], 'L0_ffn_wg_router': _L0_ffn_in['wg_router'], 'L0_ffn_w_gate': _L0_ffn_in['w_gate'], 'L0_ffn_w_up': _L0_ffn_in['w_up'], 'L0_ffn_w_down': _L0_ffn_in['w_down'], 'L0_ffn_ws_gate': _L0_ffn_in['ws_gate'], 'L0_ffn_ws_up': _L0_ffn_in['ws_up'], 'L0_ffn_ws_down': _L0_ffn_in['ws_down']}
    _x0 = _d['L0_attn_x']
    _d['L0_attn_x'] = jax.random.normal(jax.random.fold_in(jax.random.key(seed), 1), (4, 512, 256), dtype=_x0.dtype)
    del _x0
    return _d

def reference(L0_attn_x, L0_attn_wq, L0_attn_wkv_a, L0_attn_wkv_b, L0_attn_wo, L0_attn_kv_norm_w, L0_ffn_wg_router, L0_ffn_w_gate, L0_ffn_w_up, L0_ffn_w_down, L0_ffn_ws_gate, L0_ffn_ws_up, L0_ffn_ws_down):

    def _L0_attn_ref(x, wq, wkv_a, wkv_b, wo, kv_norm_w):
        import jax, jax.numpy as jnp
        import numpy as np
        DIM = 256
        N_HEADS = 16
        KV_RANK = 64
        NOPE = 128
        ROPE = 64
        VDIM = 128
        QK_HEAD = NOPE + ROPE
        THETA = 10000.0
        EPS = 1e-06
        SCALE = QK_HEAD ** (-0.5)
        NEG_INF = -1e+30

        def precompute_freqs(seq_len, head_dim, theta=THETA):
            freqs = 1.0 / theta ** (np.arange(0, head_dim, 2, dtype=np.float32) / head_dim)
            ang = np.outer(np.arange(seq_len, dtype=np.float32), freqs)
            return (jnp.asarray(np.cos(ang)), jnp.asarray(np.sin(ang)))

        def apply_rope(x, cos, sin):
            x2 = x.reshape(*x.shape[:-1], -1, 2)
            x0, x1 = (x2[..., 0], x2[..., 1])
            c = cos[None, :, None, :]
            s = sin[None, :, None, :]
            r0 = x0 * c - x1 * s
            r1 = x0 * s + x1 * c
            return jnp.stack([r0, r1], axis=-1).reshape(x.shape)

        def rmsnorm(x, w, eps=EPS):
            rms = jnp.sqrt(jnp.mean(x * x, axis=-1, keepdims=True) + eps)
            return x / rms * w
        B, S, _ = x.shape
        cos, sin = precompute_freqs(S, ROPE)
        q = (x @ wq.T).reshape(B, S, N_HEADS, QK_HEAD)
        q_nope, q_pe = (q[..., :NOPE], q[..., NOPE:])
        q_pe = apply_rope(q_pe, cos, sin)
        kv = x @ wkv_a.T
        kv_lat, k_pe = (kv[..., :KV_RANK], kv[..., KV_RANK:])
        k_pe = apply_rope(k_pe[:, :, None, :], cos, sin)[:, :, 0, :]
        wkv_b_h = wkv_b.reshape(N_HEADS, NOPE + VDIM, KV_RANK)
        q_lat = jnp.einsum('bshd,hdc->bshc', q_nope, wkv_b_h[:, :NOPE])
        kv_cache = rmsnorm(kv_lat, kv_norm_w)
        scores = (jnp.einsum('bshc,btc->bsht', q_lat, kv_cache) + jnp.einsum('bshr,btr->bsht', q_pe, k_pe)) * SCALE
        causal = jnp.tril(jnp.ones((S, S), bool))
        scores = jnp.where(causal[None, :, None, :], scores, NEG_INF)
        attn = jax.nn.softmax(scores, axis=-1)
        out_lat = jnp.einsum('bsht,btc->bshc', attn, kv_cache)
        out = jnp.einsum('bshc,hdc->bshd', out_lat, wkv_b_h[:, NOPE:])
        return out.reshape(B, S, N_HEADS * VDIM) @ wo.T

    def _L0_ffn_ref(hidden_states, wg_router, w_gate, w_up, w_down, ws_gate, ws_up, ws_down):
        import jax, jax.numpy as jnp
        import numpy as np
        TOP_K = 6
        CAP_FACTOR = 2

        def _moe_block(x2d, wg_router, w_gate, w_up, w_down, ws_gate, ws_up, ws_down):
            T, D = x2d.shape
            E = wg_router.shape[0]
            scores = jax.nn.softmax(x2d @ wg_router.T, axis=-1)
            topk_w, topk_idx = jax.lax.top_k(scores, TOP_K)
            topk_w = topk_w / (jnp.sum(topk_w, axis=-1, keepdims=True) + 1e-20)
            flat_idx = topk_idx.reshape(-1)
            oh = jax.nn.one_hot(flat_idx, E, dtype=jnp.int32)
            pos = jnp.cumsum(oh, axis=0) - 1
            pos_in_e = jnp.take_along_axis(pos, flat_idx[:, None], axis=1)[:, 0]
            C = CAP_FACTOR * (T * TOP_K // E)
            valid = pos_in_e < C
            safe_pos = jnp.where(valid, pos_in_e, 0)
            tok_id = jnp.repeat(jnp.arange(T), TOP_K)
            vmask = valid[:, None].astype(x2d.dtype)
            x_rep = x2d[tok_id] * vmask
            xe = jnp.zeros((E, C, D), x2d.dtype).at[flat_idx, safe_pos].add(x_rep)
            g = jnp.einsum('ecd,edf->ecf', xe, w_gate)
            u = jnp.einsum('ecd,edf->ecf', xe, w_up)
            ye = jnp.einsum('ecf,efd->ecd', jax.nn.silu(g) * u, w_down)
            y_tok = ye[flat_idx, safe_pos] * vmask
            y = jnp.sum(y_tok.reshape(T, TOP_K, D) * topk_w[..., None], axis=1)
            sh = jax.nn.silu(x2d @ ws_gate) * (x2d @ ws_up) @ ws_down
            return y + sh
        B, S, D = hidden_states.shape
        x2d = hidden_states.reshape(-1, D)
        out = _moe_block(x2d, wg_router, w_gate, w_up, w_down, ws_gate, ws_up, ws_down)
        return out.reshape(B, S, D)
    x = L0_attn_x
    x = _layernorm(x + _L0_attn_ref(x, L0_attn_wq, L0_attn_wkv_a, L0_attn_wkv_b, L0_attn_wo, L0_attn_kv_norm_w), axis=-1)
    x = _layernorm(x + _L0_ffn_ref(x, L0_ffn_wg_router, L0_ffn_w_gate, L0_ffn_w_up, L0_ffn_w_down, L0_ffn_ws_gate, L0_ffn_ws_up, L0_ffn_ws_down), axis=-1)
    return x

_drawn_inputs = setup_inputs


def setup_inputs(seed=0):
    import zlib

    import numpy as np

    out = dict(_drawn_inputs(seed))
    spreads = {'L0_attn_kv_norm_w': (1.0, 0.2)}
    factors = {'L0_ffn_wg_router': 8.0,
     'L0_ffn_w_gate': 8.0,
     'L0_ffn_w_up': 8.0,
     'L0_ffn_w_down': 8.0,
     'L0_ffn_ws_gate': 2.891,
     'L0_ffn_ws_up': 2.864,
     'L0_ffn_ws_down': 2.857}
    for name, (base, spread) in spreads.items():
        noise = np.random.default_rng([zlib.crc32(name.encode()), seed]).standard_normal(out[name].shape)
        drawn = base * np.exp(spread * noise) if base else spread * noise
        out[name] = jnp.asarray(drawn.astype(out[name].dtype))
    for name, factor in factors.items():
        out[name] = (out[name] * factor).astype(out[name].dtype)
    return out
```

```python
from contextlib import ExitStack

import concourse.bass as bass
from concourse import mybir

F32 = mybir.dt.float32
BF16 = mybir.dt.bfloat16
U32 = mybir.dt.uint32
I32 = mybir.dt.int32
ALU = mybir.AluOpType
ACT = mybir.ActivationFunctionType
AX = mybir.AxisListType

P = 128
B, S, D = 4, 512, 256
H, NOPE, ROPE, LAT, VDIM = 16, 128, 64, 64, 128
QK = NOPE + ROPE
SCALE = float(QK) ** -0.5
HALF = ROPE // 2
KD = D // P
TILES = S // P
PAIRS = H // 2
UNITS = PAIRS * TILES
E, TOPK, F = 32, 6, 176
FS = 2 * F
FH = F // 2
CAP = 2 * (B * S * TOPK // E)
CAPB = CAP // P
NBLK = 128
WCOLS = KD * 2 * F + 2 * D
DROPPED = float(1 << 20)
EPS_RMS, EPS_LN = 1e-6, 1e-5
STAGE_EXPERTS = 14
HEAD_EXPERTS = 14
GROUP = 2
SHC = [(0, 128), (128, 128), (256, 96)]

CONSTS = {}


def const_layout():
    at = 0
    for name, n in (("ident", P), ("mask", P), ("before", P), ("ones", P), ("cos2", TILES * ROPE),
                    ("sin2", TILES * ROPE), ("iota_e", E), ("e_cap", E), ("j_128", CAPB),
                    ("part", 1), ("ids", TILES), ("seq_len", TILES), ("tri", E * E)):
        CONSTS[name] = (at, n)
        at += n
    return at


NCONST = const_layout()


def layer_kernel(nc, x, wq, wkv_a, wkv_b, wo, kv_w, w_router, w_gate, w_up, w_down, ws_gate, ws_up,
                 ws_down, consts, out):
    x1_dram = nc.dram_tensor("x1_rows", (B * S, D), F32, kind="Internal").ap()
    acc_dram = nc.dram_tensor("acc_rows", (B * S, D), F32, kind="Internal").ap()
    y_dram = nc.dram_tensor("expert_rows", (NBLK * P, D), F32, kind="Internal").ap()
    table_dram = nc.dram_tensor("slot_table", (E * CAP, 1), F32, kind="Internal").ap()

    out_rows = out.rearrange("b s d -> (b s) d")

    with ExitStack() as ctx:
        def sb(name, shape, dt=F32):
            return ctx.enter_context(nc.sbuf_tensor(name, shape, dt))

        def sem(name):
            return ctx.enter_context(nc.semaphore(name))

        WREG = sb("expert_weights", [P, E * WCOLS])
        at = [0, STAGE_EXPERTS * WCOLS]

        def stage(n, *dims):
            v = WREG[:, at[0]:at[0] + n]
            at[0] += n
            assert at[0] <= at[1]
            names = "abc"[:len(dims)]
            if len(dims) == 1:
                return v
            spec = " ".join(names)
            return v.rearrange(f"p ({spec}) -> p {spec}", **dict(zip(names, dims)))

        wq_nope = stage(H * D, H, D)
        wq_rope = stage(PAIRS * D, PAIRS, D)
        wkvb = stage(2 * H * LAT, 2 * H, LAT)
        wo_raw = stage(2 * H * VDIM, KD, H * VDIM)
        wkva = stage(D, D)
        wo_t = stage(H * D, H, D)
        at[0], at[1] = HEAD_EXPERTS * WCOLS, E * WCOLS
        w_query = stage(KD * H * P, KD, H * P)
        o_all = stage(TILES * H * LAT, TILES, H * LAT)
        x_in = stage(TILES * D, TILES, D)
        xT = stage(KD * S, KD, S)
        keyT = stage(S, S)
        k_all = stage(TILES * P, TILES, P)
        probs = [stage(2 * S, 2, S) for _ in range(2)]
        probsT = [stage(S, TILES, P) for _ in range(2)]
        w_value_out = stage(PAIRS * D, PAIRS, D)
        oT = [stage(PAIRS * P, PAIRS, P) for _ in range(2)]
        acc = stage(TILES * D, TILES, D)
        wsgu = stage(KD * 2 * FS, KD, 2 * FS)
        wsd = stage(len(SHC) * D, len(SHC), D)
        rope_a = stage(2 * ROPE, 2, ROPE)
        rope_b = stage(2 * ROPE, 2, ROPE)

        cst = sb("cst", [P, NCONST])

        def const(name, *dims):
            a, n = CONSTS[name]
            v = cst[:, a:a + n]
            if dims:
                v = v.rearrange("p (a b) -> p a b", a=dims[0], b=dims[1])
            return v

        ident = const("ident")
        cos2, sin2 = const("cos2", TILES, ROPE), const("sin2", TILES, ROPE)
        tri = const("tri", E, E)
        ident_bf = sb("ident_bf", [P, P], BF16)
        mask_bf = sb("mask_bf", [P, P], BF16)
        kvw = sb("kvw", [P, LAT])
        wkvaT = sb("wkvaT", [P, KD, P])
        wr_raw = sb("wr_raw", [E, D])
        wrT = sb("wrT", [P, KD, E])
        q_raw = [sb(f"q_raw{u}", [P, 2, P]) for u in range(2)]
        qT = [sb(f"qT{u}", [P, 2, P]) for u in range(2)]
        kv_raw = sb("kv_raw", [P, TILES, P])
        k_a = sb("k_a", [P, TILES, ROPE])
        k_b = sb("k_b", [P, TILES, ROPE])
        k_c = sb("k_c", [P, TILES, LAT])
        key = sb("key", [P, TILES, P])
        neg_max = [sb(f"neg_max{u}", [P, 2]) for u in range(2)]
        row_sum = [sb(f"row_sum{u}", [P, 2]) for u in range(2)]
        row_inv = [sb(f"row_inv{u}", [P, 2]) for u in range(2)]
        stat = sb("stat", [P, 8 * TILES])
        bn6 = sb("bn6", [P, TILES, 6])
        mv = sb("mv", [P, TILES, 2])
        ln_s = sb("ln_s", [P, 3, TILES])
        x1 = sb("x1", [P, TILES, D])
        x1T = sb("x1T", [P, KD, S])
        sh_s = [sb(f"sh_s{u}", [P, FS]) for u in range(2)]
        sh_hT = sb("sh_hT", [P, len(SHC), P])
        rt_e = sb("rt_e", [P, TILES, E])
        rt_p = sb("rt_p", [P, TILES, E])
        rt_m = sb("rt_m", [P, 4, TILES])
        top = sb("top", [P, TILES, 8])
        top_ix = sb("top_ix", [P, TILES, 8], U32)
        top_f = sb("top_f", [P, TILES, 8])
        onehot = sb("onehot", [P, TILES, TOPK, E], BF16)
        picked = sb("picked", [P, TILES, TOPK, E])
        chosen = sb("chosen", [P, TILES, E])
        run = sb("run", [P, E])
        run_add = sb("run_add", [P, E])
        slot_e = sb("slot_e", [P, TILES, E])
        slot_inv = sb("slot_inv", [P, TILES, E])
        slot = sb("slot", [P, TILES, TOPK])
        slot_u = sb("slot_u", [P, TILES * TOPK], U32)
        ids_now = sb("ids_now", [P, TILES])
        weight = sb("weight", [P, TILES, TOPK])
        valid = sb("valid", [P, TILES, TOPK])
        NT = B * TILES
        all_slot = sb("all_slot", [P, NT, TOPK])
        all_weight = sb("all_weight", [P, NT, TOPK])
        all_onehot = sb("all_onehot", [P, NT, TOPK, E], BF16)
        bl = sb("bl", [P, 8, E])
        bl_gt = picked[:, 0, :, :].rearrange("p k e -> p (k e)").rearrange("p (e j) -> p e j", j=CAPB)
        bl_tri = x1T[:, :, :].rearrange("p k s -> p (k s)").rearrange("p (a b) -> p a b", b=E)
        bcol = sb("bcol", [P, 8])
        row_u = sb("row_u", [P, 1], U32)
        rows = sb("rows", [P, P])
        exp_i = sb("exp_i", [1, P], I32)
        tok_u = sb("tok_u", [P, NBLK], U32)
        y_row = sb("y_row", [P, NT, TOPK])
        y_row_u = sb("y_row_u", [P, NT, TOPK], U32)
        delta = sb("delta", [P, NT, TOPK])
        gidx = sb("gidx", [P, 2], U32)
        xg = [x1[:, 0, :], x1[:, 1, :]]
        xgT = [x1[:, 2, :], x1[:, 3, :]]
        hid = [sh_s[u][:, 0:F] for u in range(2)]
        hidT = [kv_raw[0:FH, 0:2, :].rearrange("p a b -> p (a b)"),
                kv_raw[0:FH, 2:4, :].rearrange("p a b -> p (a b)")]
        silu_g = [sh_s[u][:, F:2 * F] for u in range(2)]
        y_out = [t[:, :, :].rearrange("p i c -> p (i c)") for t in (k_a, k_b)]
        cidx = [sb(f"cidx{u}", [P, TOPK], U32) for u in range(2)]
        got = [WREG[:, u * TOPK * D:(u + 1) * TOPK * D].rearrange("p (k d) -> p k d", k=TOPK) for u in range(2)]
        cacc = [WREG[:, (2 * TOPK + u) * D:(2 * TOPK + u + 1) * D] for u in range(2)]
        cout = [WREG[:, (2 * TOPK + 2 + u) * D:(2 * TOPK + 3 + u) * D] for u in range(2)]
        cw = sb("cw", [P, TOPK])
        cs = sb("cs", [P, 4])
        credit = sb("credit", [P, 8])

        bank = [ctx.enter_context(nc.psum_tensor(f"bank{i}", [P, 512], F32)) for i in range(8)]

        s_const = sem("const_loaded")
        s_raw = sem("raw_loaded")
        s_small = sem("small_weights_loaded")
        s_zero = sem("zero_source_ready")
        s_table0 = sem("table_zeroed")
        s_bf = sem("bf_consts_ready")
        s_prep_mm = sem("prep_round_in_psum")
        s_prep_even = sem("prep_even_round_stored")
        s_prep_odd = sem("prep_odd_round_stored")
        s_x = sem("x_loaded")
        s_xt_mm = sem("xT_in_psum")
        s_xt_a = sem("xT_half0_stored")
        s_xt_d = sem("xT_half1_stored")
        s_kv_mm = sem("kv_in_psum")
        s_kv = sem("kv_copied")
        s_ms = sem("kv_mean_square_ready")
        s_rms = sem("kv_rms_ready")
        s_key = sem("key_ready")
        s_key_mm = sem("keyT_in_psum")
        s_keyT = sem("keyT_stored")
        s_proj = sem("q_in_psum")
        s_qcopy = sem("q_copied")
        s_rope = sem("q_rotated")
        s_rope_c = sem("rope_step")
        s_qt_mm = sem("qT_in_psum")
        s_qT = sem("qT_stored")
        s_score = sem("scores_in_psum")
        s_max = sem("max_ready")
        s_exp = sem("exp_done")
        s_pt0 = sem("probsT0_in_psum")
        s_pt1 = sem("probsT1_in_psum")
        s_pt0s = sem("probsT0_stored")
        s_pt1s = sem("probsT1_stored")
        s_pv = sem("pv_done")
        s_inv = sem("row_inverse_ready")
        s_norm = sem("head_output_stored")
        s_ot_mm = sem("oT_in_psum")
        s_ota = sem("oT_low_stored")
        s_otb = sem("oT_high_stored")
        s_y = sem("attention_y_in_psum")
        s_res = sem("residual_added")
        s_var = sem("ln_variance_ready")
        s_std = sem("ln_std_ready")
        s_x1 = sem("x1_ready")
        s_x1_st = sem("x1_rows_stored")
        s_x1t_mm = sem("x1T_in_psum")
        s_x1t_a = sem("x1T_half0_stored")
        s_x1t_d = sem("x1T_half1_stored")
        s_log = sem("logits_in_psum")
        s_logd = sem("logits_shifted")
        s_rexp = sem("router_exp_ready")
        s_cho = sem("chosen_ready")
        s_pos = sem("places_in_psum")
        s_slot = sem("slots_ready")
        s_ids = sem("ids_ready")
        s_scat = sem("ids_scattered")
        s_gu = sem("shared_gate_up_in_psum")
        s_silu = sem("shared_silu_ready")
        s_sh = sem("shared_hidden_ready")
        s_sht_mm = sem("shared_hiddenT_in_psum")
        s_sht = sem("shared_hiddenT_stored")
        s_sd = sem("shared_down_in_psum")
        s_acc = sem("acc_ready")
        s_acc_st = sem("acc_rows_stored")
        s_run = sem("counts_final")
        s_cnt = sem("counts_in_psum")
        s_row = sem("block_rows_ready")
        s_rows = sem("block_slots_gathered")
        s_bt = sem("block_tables_in_psum")
        s_blk = sem("block_tables_ready")
        s_yrow = sem("result_rows_ready")
        s_w = sem("expert_weights_loaded")
        s_gix = sem("gather_index_ready")
        s_g = [sem(f"tokens_gathered{u}") for u in range(2)]
        s_mx_mm = sem("block_xT_in_psum")
        s_mxT = sem("block_xT_stored")
        s_mgu = sem("block_gate_up_in_psum")
        s_msilu = sem("block_silu_ready")
        s_mh = sem("block_hidden_ready")
        s_mht_mm = sem("block_hiddenT_in_psum")
        s_mhT = sem("block_hiddenT_stored")
        s_mdn = sem("block_down_in_psum")
        s_my = sem("block_y_copied")
        s_yst = [sem(f"block_y_stored{u}") for u in range(2)]
        s_cix = sem("combine_index_ready")
        s_cg = [sem(f"results_gathered{u}") for u in range(2)]
        s_cld = [sem(f"acc_loaded{u}") for u in range(2)]
        s_cvar = sem("out_variance_ready")
        s_cstd = sem("out_std_ready")
        s_cout = sem("out_tile_ready")
        s_cst = [sem(f"out_stored{u}") for u in range(2)]
        s_cfree = sem("combine_buffers_free")
        s_link = sem("vector_step")
        s_link2 = sem("vector_step_blocks")
        s_link3 = sem("vector_step_combine")

        N_RAW = 6
        N_SMALL = 7
        PREP_ROUNDS = 22
        LOADS = (E // GROUP) * 6
        SCAT = TILES * TOPK * 16
        LINKS = 21
        LINKS_C = 9

        w_view = WREG[:, :].rearrange("p (e c) -> p e c", e=E)

        def load_experts(eng, g):
            e0 = g * GROUP
            for k in range(KD):
                for j, w in enumerate((w_gate, w_up)):
                    at0 = k * 2 * F + j * F
                    eng.dma_start(w_view[:, e0:e0 + GROUP, at0:at0 + F],
                                  w[e0:e0 + GROUP, k * P:(k + 1) * P, :].rearrange("e p f -> p e f")).then_inc(s_w, 16)
            for j in range(2):
                at0 = KD * 2 * F + j * D
                eng.dma_start(w_view[0:FH, e0:e0 + GROUP, at0:at0 + D],
                              w_down[e0:e0 + GROUP, j * FH:(j + 1) * FH, :].rearrange("e p d -> p e d")).then_inc(s_w, 16)

        block = ctx.enter_context(nc.Block())

        @block.sync
        def _(sp):
            sp.dma_start(cst[:, :], consts).then_inc(s_const, 16)
            wq_h = wq.rearrange("(h r) d -> h r d", r=QK)
            sp.dma_start(wq_nope, wq_h[:, 0:NOPE, :].rearrange("h r d -> r h d")).then_inc(s_raw, 16)
            sp.dma_start(wkvb, wkv_b.rearrange("(h r) c -> r h c", r=P)).then_inc(s_raw, 16)
            for o in range(2):
                sp.dma_start(wq_rope[o * ROPE:(o + 1) * ROPE, :, :],
                             wq.rearrange("(a o r) d -> o r a d", o=2, r=QK)[o, NOPE:QK, :, :]).then_inc(s_raw, 16)
            sp.dma_start(wkva, wkv_a).then_inc(s_raw, 16)
            sp.dma_start(wo_raw, wo.rearrange("(k p) n -> p k n", p=P)).then_inc(s_raw, 16)
            sp.dma_start(kvw[:, :], kv_w.rearrange("(a c) -> a c", a=1).to_broadcast([P, LAT])).then_inc(s_small, 16)
            sp.dma_start(wr_raw[:, :], w_router).then_inc(s_small, 16)
            sp.dma_start(wsgu[:, :, 0:FS], ws_gate.rearrange("(k p) f -> p k f", p=P)).then_inc(s_small, 16)
            sp.dma_start(wsgu[:, :, FS:2 * FS], ws_up.rearrange("(k p) f -> p k f", p=P)).then_inc(s_small, 16)
            for c, (f0, fn) in enumerate(SHC):
                sp.dma_start(wsd[0:fn, c, :], ws_down[f0:f0 + fn, :]).then_inc(s_small, 16)
            sp.wait_ge(s_zero, 1)
            sp.dma_start(table_dram.rearrange("(p n) a -> p (n a)", p=P),
                         x1[:, 0, 0:E * CAP // P]).then_inc(s_table0, 16)

            def load_x(b):
                sp.dma_start(x_in, x[bass.ds(b, 1), :, :].squeeze(0).rearrange("(i p) d -> p i d", p=P)).then_inc(s_x, 16)

            def store_sequence(b):
                sp.wait_ge(s_x1, b + 1)
                sp.dma_start(x1_dram[bass.ds(b * S, S), :].rearrange("(i p) d -> p i d", p=P),
                             x1[:, :, :]).then_inc(s_x1_st, 16)
                sp.wait_ge(s_acc, TILES * (b + 1))
                sp.dma_start(acc_dram[bass.ds(b * S, S), :].rearrange("(i p) d -> p i d", p=P),
                             acc).then_inc(s_acc_st, 16)

            load_x(0)
            sp.wait_ge(s_prep_even, 11)
            sp.wait_ge(s_prep_odd, 11)
            for g in range(HEAD_EXPERTS // GROUP):
                load_experts(sp, g)
            with sp.Fori(0, B - 1) as b:
                sp.wait_ge(s_res, TILES * (b + 1))
                load_x(b + 1)
                store_sequence(b)
            store_sequence(B - 1)
            sp.wait_ge(s_acc_st, 16 * B)
            for g in range(HEAD_EXPERTS // GROUP, E // GROUP):
                load_experts(sp, g)

            with sp.Fori(0, NBLK // 2) as it:
                for u in range(2):
                    sp.wait_ge(s_my, 2 * it + u + 2)
                    sp.dma_start(y_dram[bass.ds((2 * it + u) * P, P), :], y_out[u]).then_inc(s_yst[u], 16)
            with sp.Fori(0, NT // 2) as it:
                for u in range(2):
                    t = 2 * it + u
                    sp.wait_ge(s_cfree, t)
                    sp.wait_ge(s_mdn, NBLK)
                    sp.dma_start(cacc[u], acc_dram[bass.ds(t * P, P), :]).then_inc(s_cld[u], 16)
                for u in range(2):
                    t = 2 * it + u
                    sp.wait_ge(s_cout, t + 1)
                    sp.dma_start(out_rows[bass.ds(t * P, P), :], cout[u]).then_inc(s_cst[u], 16)
            for u in range(2):
                sp.wait_ge(s_cst[u], 16 * (NT // 2))
                sp.wait_ge(s_yst[u], 16 * (NBLK // 2))
            sp.wait_ge(s_x1_st, 16 * B)
            sp.wait_ge(s_acc_st, 16 * B)
            sp.wait_ge(s_table0, 16)
            sp.wait_ge(s_scat, SCAT * B)

        @block.tensor
        def _(pe):
            def round_free(r):
                if r >= 8:
                    pe.wait_ge(s_prep_even if r % 2 == 0 else s_prep_odd, (r - 8) // 2 + 1)

            pe.wait_ge(s_const, 16)
            pe.wait_ge(s_raw, 16 * N_RAW)
            for k in range(KD):
                for g in range(2):
                    for j in range(8):
                        h = 8 * g + j
                        mm = pe.matmul(bank[2 * k + g][:, j * LAT:(j + 1) * LAT], wq_nope[:, h, k * P:(k + 1) * P],
                                       wkvb[:, 2 * h, :], start=True, stop=True)
                    mm.then_inc(s_prep_mm, 1)
            for k in range(KD):
                for g in range(2):
                    for j in range(4):
                        mm = pe.transpose(bank[4 + 2 * k + g][:, j * P:(j + 1) * P],
                                          wq_rope[:, 4 * g + j, k * P:(k + 1) * P], ident)
                    mm.then_inc(s_prep_mm, 1)
            round_free(8)
            for k in range(KD):
                mm = pe.transpose(bank[0][:, k * P:(k + 1) * P], wkva[:, k * P:(k + 1) * P], ident)
            mm.then_inc(s_prep_mm, 1)
            for r in range(9, 17):
                round_free(r)
                for j in range(2):
                    h = 2 * (r - 9) + j
                    for k in range(KD):
                        mm = pe.transpose(bank[r % 8][:, (2 * j + k) * P:(2 * j + k + 1) * P],
                                          wo_raw[:, k, h * VDIM:(h + 1) * VDIM], ident)
                mm.then_inc(s_prep_mm, 1)
            pe.wait_ge(s_prep_even, 9)
            pe.wait_ge(s_prep_odd, 8)
            for r in range(17, 21):
                for j in range(2):
                    for o in range(2):
                        h = 4 * (r - 17) + 2 * j + o
                        mm = pe.matmul(bank[r % 8][o * LAT:(o + 1) * LAT, j * D:(j + 1) * D], wkvb[:, 2 * h + 1, :],
                                       wo_t[:, h, :], start=True, stop=True)
                mm.then_inc(s_prep_mm, 1)
            round_free(21)
            pe.wait_ge(s_small, 16 * N_SMALL)
            for k in range(KD):
                mm = pe.transpose(bank[5][:, k * E:(k + 1) * E], wr_raw[:, k * P:(k + 1) * P], ident[0:E, 0:E])
            mm.then_inc(s_prep_mm, 1)
            pe.wait_ge(s_prep_even, 11)
            pe.wait_ge(s_prep_odd, 11)
            pe.wait_ge(s_bf, 2)

            S_BANK = [(bank[0], bank[1]), (bank[2], bank[3])]
            PT_BANK, O_BANK, Q_BANK, QT_BANK = bank[4], bank[5], bank[6], bank[7]

            def project(n, pair, i):
                pe.wait_ge(s_qcopy, n)
                for k in range(KD):
                    mm = pe.matmul(Q_BANK[:, 0:2 * P], xT[:, k, i * P:(i + 1) * P],
                                   w_query[:, k, bass.ds(pair * 2 * P, 2 * P)], start=(k == 0), stop=(k == KD - 1))
                mm.then_inc(s_proj, 1)

            def turn_query(n, slot_):
                pe.wait_ge(s_rope, n + 1)
                pe.wait_ge(s_qT, n)
                for h in range(2):
                    mm = pe.transpose(QT_BANK[:, h * P:(h + 1) * P], q_raw[slot_][:, h, :], ident)
                mm.then_inc(s_qt_mm, 1)

            def scores(n, i):
                u = i % 2
                keys = (i + 1) * P
                pe.wait_ge(s_qT, n + 1)
                pe.wait_ge(s_exp, 2 * n)
                for h in range(2):
                    pe.matmul(S_BANK[u][h][:, 0:keys], qT[u][:, h, :], keyT[:, 0:keys], start=True, stop=False)
                    mm = pe.matmul(S_BANK[u][h][:, i * P:keys], ident_bf[:, :], mask_bf[:, :], start=False, stop=True)
                mm.then_inc(s_score, 1)

            def turn_probs(n, i, h):
                pe.wait_ge(s_exp, 2 * n + h + 3)
                if h == 0:
                    pe.wait_ge(s_pt1s, n)
                else:
                    pe.wait_ge(s_pt0s, n + 1)
                for j in range(i + 1):
                    mm = pe.transpose(PT_BANK[:, j * P:(j + 1) * P], probs[i % 2][:, h, j * P:(j + 1) * P], ident)
                mm.then_inc(s_pt1 if h else s_pt0, 1)

            def values(n, i, h):
                if h == 0:
                    pe.wait_ge(s_norm, n)
                    pe.wait_ge(s_pt0s, n + 1)
                else:
                    pe.wait_ge(s_pt1s, n + 1)
                for j in range(i + 1):
                    mm = pe.matmul(O_BANK[:, h * LAT:(h + 1) * LAT], probsT[h][:, j, :], k_all[:, j, ROPE:P],
                                   start=(j == 0), stop=(j == i))
                if h == 1:
                    mm.then_inc(s_pv, 1)

            def step(b, p, i, first_local):
                n = UNITS * b + TILES * p + i
                last = first_local + i
                if last + 1 < UNITS:
                    scores(n + 1, (i + 1) % TILES)
                turn_probs(n, i, 0)
                if last + 2 < UNITS:
                    turn_query(n + 2, i % 2)
                turn_probs(n, i, 1)
                values(n, i, 0)
                if last + 3 < UNITS:
                    project(n + 3, p + (i + 3) // TILES, (i + 3) % TILES)
                values(n, i, 1)

            with pe.Fori(0, B) as b:
                pe.wait_ge(s_x, 16 * (b + 1))
                pe.wait_ge(s_acc, TILES * b)
                for k in range(KD):
                    for i in range(TILES):
                        mm = pe.transpose(bank[k][:, i * P:(i + 1) * P], x_in[:, i, k * P:(k + 1) * P], ident)
                    mm.then_inc(s_xt_mm, 1)
                pe.wait_ge(s_xt_a, b + 1)
                pe.wait_ge(s_xt_d, b + 1)
                for i in range(TILES):
                    for k in range(KD):
                        mm = pe.matmul(bank[2][:, i * P:(i + 1) * P], xT[:, k, i * P:(i + 1) * P], wkvaT[:, k, :],
                                       start=(k == 0), stop=(k == KD - 1))
                mm.then_inc(s_kv_mm, 1)
                n0 = UNITS * b
                project(n0, 0, 0)
                project(n0 + 1, 0, 1)
                turn_query(n0, 0)
                project(n0 + 2, 0, 2)
                turn_query(n0 + 1, 1)
                pe.wait_ge(s_key, b + 1)
                for i in range(TILES):
                    mm = pe.transpose(bank[3][:, i * P:(i + 1) * P], key[:, i, :], ident)
                mm.then_inc(s_key_mm, 1)
                pe.wait_ge(s_keyT, b + 1)
                scores(n0, 0)
                with pe.Fori(0, PAIRS - 1) as p:
                    for i in range(TILES):
                        step(b, p, i, 0)
                for i in range(TILES):
                    step(b, PAIRS - 1, i, UNITS - TILES)

                def turn_out(i):
                    m = TILES * b + i
                    u = i % 2
                    if i >= 2:
                        pe.wait_ge(s_ota, m - 1)
                        pe.wait_ge(s_otb, m - 1)
                    for kk in range(PAIRS):
                        mm = pe.transpose(bank[2 * u + kk // 4][:, (kk % 4) * P:(kk % 4 + 1) * P],
                                          o_all[:, i, kk * P:(kk + 1) * P], ident)
                        if kk % 4 == 3:
                            mm.then_inc(s_ot_mm, 1)

                def project_out(i):
                    m = TILES * b + i
                    pe.wait_ge(s_ota, m + 1)
                    pe.wait_ge(s_otb, m + 1)
                    if i >= 2:
                        pe.wait_ge(s_res, m - 1)
                    for kk in range(PAIRS):
                        mm = pe.matmul(bank[4 + i % 2][:, 0:D], oT[i % 2][:, kk, :], w_value_out[:, kk, :],
                                       start=(kk == 0), stop=(kk == PAIRS - 1))
                    mm.then_inc(s_y, 1)

                pe.wait_ge(s_norm, UNITS * (b + 1))
                turn_out(0)
                turn_out(1)
                project_out(0)
                turn_out(2)
                project_out(1)
                turn_out(3)
                project_out(2)
                project_out(3)

                pe.wait_ge(s_x1, b + 1)
                for k in range(KD):
                    for i in range(TILES):
                        mm = pe.transpose(bank[k][:, i * P:(i + 1) * P], x1[:, i, k * P:(k + 1) * P], ident)
                    mm.then_inc(s_x1t_mm, 1)
                pe.wait_ge(s_x1t_a, b + 1)
                pe.wait_ge(s_x1t_d, b + 1)
                for i in range(TILES):
                    for k in range(KD):
                        mm = pe.matmul(bank[2][:, i * E:(i + 1) * E], x1T[:, k, i * P:(i + 1) * P], wrT[:, k, :],
                                       start=(k == 0), stop=(k == KD - 1))
                mm.then_inc(s_log, 1)

                def gate_up(i):
                    m = TILES * b + i
                    if i >= 2:
                        pe.wait_ge(s_sh, m - 1)
                    for half in range(2):
                        for k in range(KD):
                            mm = pe.matmul(bank[4 + 2 * (i % 2) + half][:, 0:FS], x1T[:, k, i * P:(i + 1) * P],
                                           wsgu[:, k, half * FS:(half + 1) * FS], start=(k == 0), stop=(k == KD - 1))
                    mm.then_inc(s_gu, 1)

                def turn_hidden(i):
                    m = TILES * b + i
                    pe.wait_ge(s_sh, m + 1)
                    pe.wait_ge(s_sht, m)
                    for c, (f0, fn) in enumerate(SHC):
                        mm = pe.transpose(bank[0][0:fn, c * P:(c + 1) * P], sh_s[i % 2][:, f0:f0 + fn], ident)
                    mm.then_inc(s_sht_mm, 1)

                def down(i):
                    m = TILES * b + i
                    pe.wait_ge(s_sht, m + 1)
                    pe.wait_ge(s_acc, m)
                    for c, (f0, fn) in enumerate(SHC):
                        mm = pe.matmul(bank[1][:, 0:D], sh_hT[0:fn, c, :], wsd[0:fn, c, :],
                                       start=(c == 0), stop=(c == len(SHC) - 1))
                    mm.then_inc(s_sd, 1)

                gate_up(0)
                gate_up(1)
                pe.wait_ge(s_cho, b + 1)
                for i in range(TILES):
                    o = bank[3][:, i * E:(i + 1) * E]
                    pe.matmul(o, const("ones"), run[:, :], start=True, stop=False)
                    for j in range(i):
                        pe.matmul(o, const("ones"), chosen[:, j, :], start=False, stop=False)
                    mm = pe.matmul(o, const("before"), chosen[:, i, :], start=False, stop=True)
                mm.then_inc(s_pos, 1)
                turn_hidden(0)
                down(0)
                gate_up(2)
                turn_hidden(1)
                down(1)
                gate_up(3)
                turn_hidden(2)
                down(2)
                turn_hidden(3)
                down(3)

            pe.wait_ge(s_run, 1)
            pe.matmul(bank[2][:, 0:E], const("ones"), run[:, :], start=True, stop=True).then_inc(s_cnt, 1)
            pe.wait_ge(s_row, 1)
            pe.matmul(bank[4][0:1, 0:P], bcol[:, 0:1], ident, start=True, stop=True).then_inc(s_bt, 1)
            pe.wait_ge(s_rows, 16)
            pe.transpose(bank[5][:, 0:P], rows[:, :], ident).then_inc(s_bt, 1)

            XT_B, GU_B, HT_B, Y_B = bank[0:2], bank[2:4], bank[4:6], bank[6:8]

            def block_xT(m, it, u):
                pe.wait_ge(s_g[u], 16 * (it + 1))
                pe.wait_ge(s_mxT, m)
                for k in range(KD):
                    mm = pe.transpose(XT_B[u][:, k * P:(k + 1) * P], xg[u][:, k * P:(k + 1) * P], ident)
                mm.then_inc(s_mx_mm, 1)

            def block_gate_up(m, u):
                e = pe.value_load(exp_i[0:1, bass.ds(m, 1)], min_val=0, max_val=E - 1)
                pe.wait_ge(s_mxT, m + 2)
                pe.wait_ge(s_mh, m)
                for k in range(KD):
                    mm = pe.matmul(GU_B[u][:, 0:2 * F], xgT[u][:, k * P:(k + 1) * P],
                                   WREG[:, bass.ds(e * WCOLS + k * 2 * F, 2 * F)], start=(k == 0), stop=(k == KD - 1))
                mm.then_inc(s_mgu, 1)

            def block_hT(m, u):
                pe.wait_ge(s_mh, m + 2)
                pe.wait_ge(s_mhT, m)
                for j in range(2):
                    mm = pe.transpose(HT_B[u][0:FH, j * P:(j + 1) * P], hid[u][:, j * FH:(j + 1) * FH], ident)
                mm.then_inc(s_mht_mm, 1)

            def block_down(m, u):
                e = pe.value_load(exp_i[0:1, bass.ds(m, 1)], min_val=0, max_val=E - 1)
                pe.wait_ge(s_mhT, m + 2)
                pe.wait_ge(s_my, m)
                for j in range(2):
                    mm = pe.matmul(Y_B[u][:, 0:D], hidT[u][:, j * P:(j + 1) * P],
                                   WREG[0:FH, bass.ds(e * WCOLS + KD * 2 * F + j * D, D)],
                                   start=(j == 0), stop=(j == 1))
                mm.then_inc(s_mdn, 1)

            pe.wait_ge(s_blk, 2)
            pe.wait_ge(s_w, 16 * LOADS)
            block_xT(0, 0, 0)
            block_xT(1, 0, 1)
            block_gate_up(0, 0)
            with pe.Fori(0, NBLK // 2 - 1) as it:
                for u in range(2):
                    m = 2 * it + u
                    block_gate_up(m + 1, 1 - u)
                    block_hT(m, u)
                    block_xT(m + 2, it + 1, u)
                    block_down(m, u)
            block_gate_up(NBLK - 1, 1)
            for u in range(2):
                block_hT(NBLK - 2 + u, u)
                block_down(NBLK - 2 + u, u)

        @block.scalar
        def _(act):
            w_q = w_query.rearrange("p k (h c) -> p k h c", c=P)

            def prep(r):
                act.wait_ge(s_prep_mm, r + 1)

            for r in (0, 2):
                prep(r)
                act.copy(w_q[:, r // 2, 0:8, ROPE:P], bank[r][:, :].rearrange("p (h c) -> p h c", c=LAT)).then_inc(s_prep_even, 1)
            for r in (4, 6):
                prep(r)
                act.copy(w_q[:, (r - 4) // 2, 0:8, 0:ROPE].rearrange("p h (t j) -> p h j t", t=2),
                         bank[r][:, :].rearrange("p (h j t) -> p h j t", h=8, t=2)).then_inc(s_prep_even, 1)
            prep(8)
            kv = bank[0][:, 0:KD * P].rearrange("p (k c) -> p k c", k=KD)
            act.copy(wkvaT[:, :, ROPE:P], kv[:, :, 0:LAT])
            act.copy(wkvaT[:, :, 0:ROPE].rearrange("p k (t j) -> p k j t", t=2),
                     kv[:, :, LAT:P].rearrange("p k (j t) -> p k j t", t=2)).then_inc(s_prep_even, 1)
            for r in (10, 12, 14, 16):
                prep(r)
                act.copy(wo_t[:, 2 * (r - 9):2 * (r - 9) + 2, :],
                         bank[r % 8][:, :].rearrange("p (j d) -> p j d", j=2)).then_inc(s_prep_even, 1)
            for r in (18, 20):
                prep(r)
                act.copy(w_value_out[:, 2 * (r - 17):2 * (r - 17) + 2, :],
                         bank[r % 8][:, :].rearrange("p (j d) -> p j d", j=2)).then_inc(s_prep_even, 1)

            def copy_query(n, i):
                act.wait_ge(s_proj, n + 1)
                act.copy(q_raw[i % 2][:, :, :], bank[6][:, 0:2 * P].rearrange("p (h c) -> p h c", h=2)).then_inc(s_qcopy, 1)

            def exps(n, i):
                u = i % 2
                act.wait_ge(s_max, n + 1)
                for h in range(2):
                    act.activation(probs[u][:, h, 0:(i + 1) * P], bank[2 * u + h][:, 0:(i + 1) * P], ACT.Exp,
                                   bias=neg_max[u][:, h:h + 1], scale=1.0,
                                   accum_out=row_sum[u][:, h:h + 1]).then_inc(s_exp, 1)

            def step(b, p, i, first_local):
                n = UNITS * b + TILES * p + i
                last = first_local + i
                act.wait_ge(s_pt0, n + 1)
                act.copy(probsT[0][:, 0:i + 1, :],
                         bank[4][:, 0:(i + 1) * P].rearrange("p (j t) -> p j t", t=P)).then_inc(s_pt0s, 1)
                if last + 1 < UNITS:
                    exps(n + 1, (i + 1) % TILES)
                if last + 3 < UNITS:
                    copy_query(n + 3, i + 3)

            with act.Fori(0, B) as b:
                act.wait_ge(s_xt_mm, 2 * b + 1)
                act.copy(xT[:, 0, :], bank[0][:, :]).then_inc(s_xt_a, 1)
                act.wait_ge(s_kv_mm, b + 1)
                act.copy(kv_raw[:, :, :], bank[2][:, :].rearrange("p (i c) -> p i c", c=P)).then_inc(s_kv, 1)
                n0 = UNITS * b
                copy_query(n0, 0)
                copy_query(n0 + 1, 1)
                act.wait_ge(s_ms, b + 1)
                act.activation(stat[:, 8:12], stat[:, 4:8], ACT.Sqrt).then_inc(s_rms, 1)
                copy_query(n0 + 2, 2)
                act.wait_ge(s_key_mm, b + 1)
                act.copy(keyT, bank[3][:, :]).then_inc(s_keyT, 1)
                exps(n0, 0)
                with act.Fori(0, PAIRS - 1) as p:
                    for i in range(TILES):
                        step(b, p, i, 0)
                for i in range(TILES):
                    step(b, PAIRS - 1, i, UNITS - TILES)
                for i in range(TILES):
                    m = TILES * b + i
                    act.wait_ge(s_ot_mm, 2 * m + 1)
                    act.copy(oT[i % 2][:, 0:4, :],
                             bank[2 * (i % 2)][:, :].rearrange("p (j t) -> p j t", t=P)).then_inc(s_ota, 1)
                act.wait_ge(s_var, b + 1)
                act.activation(ln_s[:, 1, :], ln_s[:, 0, :], ACT.Sqrt).then_inc(s_std, 1)
                act.wait_ge(s_x1t_mm, 2 * b + 1)
                act.copy(x1T[:, 0, :], bank[0][:, :]).then_inc(s_x1t_a, 1)
                act.wait_ge(s_logd, b + 1)
                act.activation(rt_e[:, :, :], rt_p[:, :, :], ACT.Exp).then_inc(s_rexp, 1)
                for i in range(TILES):
                    m = TILES * b + i
                    act.wait_ge(s_gu, m + 1)
                    if i >= 2:
                        act.wait_ge(s_sht_mm, m - 1)
                    else:
                        act.wait_ge(s_sht_mm, TILES * b)
                    act.activation(sh_s[i % 2][:, :], bank[4 + 2 * (i % 2)][:, 0:FS], ACT.Silu).then_inc(s_silu, 1)

            def block_silu(m, u):
                act.wait_ge(s_mgu, m + 1)
                act.activation(silu_g[u], bank[2 + u][:, 0:F], ACT.Silu).then_inc(s_msilu, 1)

            def block_y(m, it, u):
                act.wait_ge(s_mdn, m + 1)
                act.wait_ge(s_yst[u], 16 * it)
                act.copy(y_out[u], bank[6 + u][:, 0:D]).then_inc(s_my, 1)

            block_silu(0, 0)
            with act.Fori(0, NBLK // 2 - 1) as it:
                for u in range(2):
                    block_silu(2 * it + u + 1, 1 - u)
                    block_y(2 * it + u, it, u)
            block_silu(NBLK - 1, 1)
            for u in range(2):
                block_y(NBLK - 2 + u, NBLK // 2 - 1, u)
            with act.Fori(0, NT) as t:
                act.wait_ge(s_cvar, t + 1)
                act.activation(cs[:, 3:4], cs[:, 2:3], ACT.Sqrt).then_inc(s_cstd, 1)

        @block.vector
        def _(dve):
            class Links:

                def __init__(self, s, per):
                    self.s, self.per, self.n, self.base = s, per, 0, 0

                def start(self, base):
                    self.n, self.base = 0, base

                def __call__(self, ins):
                    self.n += 1
                    ins.then_inc(self.s, 1)
                    dve.wait_ge(self.s, self.base + self.n)

                def end(self):
                    assert self.per is None or self.n == self.per, self.n

            dve.memset(credit[:, 0:1], 0.0).then_inc(s_exp, 2)
            for j, s in enumerate((s_mxT, s_mh, s_mhT, s_my, s_cfree)):
                dve.memset(credit[:, j + 1:j + 2], 0.0).then_inc(s, 1)
            dve.memset(x1[:, 0, :], 0.0).then_inc(s_zero, 1)
            dve.memset(run[:, :], 0.0)
            dve.wait_ge(s_const, 16)
            dve.tensor_copy(ident_bf[:, :], ident).then_inc(s_bf, 1)
            dve.tensor_copy(mask_bf[:, :], const("mask")).then_inc(s_bf, 1)

            w_q = w_query.rearrange("p k (h c) -> p k h c", c=P)

            def prep(r):
                dve.wait_ge(s_prep_mm, r + 1)

            for r in (1, 3):
                prep(r)
                dve.tensor_copy(w_q[:, r // 2, 8:16, ROPE:P],
                                bank[r][:, :].rearrange("p (h c) -> p h c", c=LAT)).then_inc(s_prep_odd, 1)
            for r in (5, 7):
                prep(r)
                dve.tensor_copy(w_q[:, (r - 4) // 2, 8:16, 0:ROPE].rearrange("p h (t j) -> p h j t", t=2),
                                bank[r][:, :].rearrange("p (h j t) -> p h j t", h=8, t=2)).then_inc(s_prep_odd, 1)
            for r in (9, 11, 13, 15):
                prep(r)
                dve.tensor_copy(wo_t[:, 2 * (r - 9):2 * (r - 9) + 2, :],
                                bank[r % 8][:, :].rearrange("p (j d) -> p j d", j=2)).then_inc(s_prep_odd, 1)
            for r in (17, 19):
                prep(r)
                dve.tensor_copy(w_value_out[:, 2 * (r - 17):2 * (r - 17) + 2, :],
                                bank[r % 8][:, :].rearrange("p (j d) -> p j d", j=2)).then_inc(s_prep_odd, 1)
            prep(21)
            dve.tensor_copy(wrT[:, :, :], bank[5][:, 0:KD * E].rearrange("p (k e) -> p k e", k=KD)).then_inc(s_prep_odd, 1)

            link = Links(s_link, LINKS)

            def store_qT(n, i):
                dve.wait_ge(s_qt_mm, n + 1)
                dve.tensor_copy(qT[i % 2][:, :, :], bank[7][:, 0:2 * P].rearrange("p (h t) -> p h t", h=2)).then_inc(s_qT, 1)

            def maxima(n, i):
                u = i % 2
                dve.wait_ge(s_score, n + 1)
                for h in range(2):
                    ins = dve.tensor_reduce(neg_max[u][:, h:h + 1], bank[2 * u + h][:, 0:(i + 1) * P], AX.X, ALU.max,
                                            negate=True)
                ins.then_inc(s_max, 1)

            def normalise(n, p, i):
                u = i % 2
                dve.wait_ge(s_pv, n + 1)
                dve.reciprocal(row_inv[u][:, :], row_sum[u][:, :]).then_inc(s_inv, 1)
                dve.wait_ge(s_inv, n + 1)
                dve.tensor_tensor(o_all[:, i, bass.ds(p * 2 * LAT, 2 * LAT)].rearrange("p (h c) -> p h c", h=2),
                                  bank[5][:, 0:2 * LAT].rearrange("p (h c) -> p h c", h=2),
                                  row_inv[u][:, :].unsqueeze(2).broadcast_to([P, 2, LAT]), ALU.mult).then_inc(s_norm, 1)

            def step(b, p, i, first_local):
                n = UNITS * b + TILES * p + i
                last = first_local + i
                if last + 1 < UNITS:
                    maxima(n + 1, (i + 1) % TILES)
                if last + 2 < UNITS:
                    store_qT(n + 2, i)
                dve.wait_ge(s_pt1, n + 1)
                dve.tensor_copy(probsT[1][:, 0:i + 1, :],
                                bank[4][:, 0:(i + 1) * P].rearrange("p (j t) -> p j t", t=P)).then_inc(s_pt1s, 1)
                normalise(n, p, i)

            def bc(ap, shape):
                return ap.broadcast_to(shape)

            with dve.Fori(0, B) as b:
                link.start(b * LINKS)
                dve.wait_ge(s_xt_mm, 2 * b + 2)
                dve.tensor_copy(xT[:, 1, :], bank[1][:, :]).then_inc(s_xt_d, 1)
                dve.wait_ge(s_kv, b + 1)
                dve.tensor_tensor(k_a[:, :, :], kv_raw[:, :, 0:ROPE], cos2, ALU.mult)
                dve.tensor_tensor(k_b[:, :, :], kv_raw[:, :, 0:ROPE], sin2, ALU.mult)
                link(dve.tensor_tensor(k_c[:, :, :], kv_raw[:, :, ROPE:P], kv_raw[:, :, ROPE:P], ALU.mult))
                dve.tensor_tensor(k_all[:, :, 0:HALF], k_a[:, :, 0:HALF], k_b[:, :, HALF:ROPE], ALU.subtract)
                dve.tensor_tensor(k_all[:, :, HALF:ROPE], k_a[:, :, HALF:ROPE], k_b[:, :, 0:HALF], ALU.add)
                link(dve.tensor_reduce(stat[:, 0:4], k_c[:, :, :], AX.X, ALU.add))
                dve.tensor_scalar(stat[:, 4:8], stat[:, 0:4], 1.0 / LAT, EPS_RMS, ALU.mult, ALU.add).then_inc(s_ms, 1)
                n0 = UNITS * b
                store_qT(n0, 0)
                dve.wait_ge(s_rms, b + 1)
                link(dve.reciprocal(stat[:, 12:16], stat[:, 8:12]))
                link(dve.tensor_tensor(k_c[:, :, :], kv_raw[:, :, ROPE:P],
                                       bc(stat[:, 12:16].unsqueeze(2), [P, TILES, LAT]), ALU.mult))
                link(dve.tensor_tensor(k_all[:, :, ROPE:P], k_c[:, :, :],
                                       bc(kvw[:, :].unsqueeze(1), [P, TILES, LAT]), ALU.mult))
                dve.tensor_scalar(key[:, :, :], k_all, SCALE, None, ALU.mult).then_inc(s_key, 1)
                store_qT(n0 + 1, 1)
                maxima(n0, 0)
                with dve.Fori(0, PAIRS - 1) as p:
                    for i in range(TILES):
                        step(b, p, i, 0)
                for i in range(TILES):
                    step(b, PAIRS - 1, i, UNITS - TILES)

                def store_oT(i):
                    dve.wait_ge(s_ot_mm, 2 * (TILES * b + i) + 2)
                    dve.tensor_copy(oT[i % 2][:, 4:8, :],
                                    bank[2 * (i % 2) + 1][:, :].rearrange("p (j t) -> p j t", t=P)).then_inc(s_otb, 1)

                def residual(i):
                    dve.wait_ge(s_y, TILES * b + i + 1)
                    if i == 0:
                        dve.wait_ge(s_x1_st, 16 * b)
                        dve.wait_ge(s_table0, 16)
                    dve.tensor_tensor(x1[:, i, :], bank[4 + i % 2][:, 0:D], x_in[:, i, :], ALU.add).then_inc(s_res, 1)

                store_oT(0)
                store_oT(1)
                residual(0)
                store_oT(2)
                residual(1)
                store_oT(3)
                residual(2)
                residual(3)
                dve.wait_ge(s_res, TILES * (b + 1))
                for i in range(TILES):
                    ins = dve.bn_stats(bn6[:, i, :], x1[:, i, :])
                dve.drain()
                for i in range(TILES):
                    ins = dve.bn_aggr(mv[:, i, :], bn6[:, i, :])
                link(ins)
                dve.tensor_scalar(ln_s[:, 0, :], mv[:, :, 1], EPS_LN, None, ALU.add).then_inc(s_var, 1)
                dve.wait_ge(s_std, b + 1)
                link(dve.reciprocal(ln_s[:, 2, :], ln_s[:, 1, :]))
                for i in range(TILES):
                    ins = dve.tensor_scalar(x1[:, i, :], x1[:, i, :], mv[:, i, 0:1], ln_s[:, 2, i:i + 1],
                                            ALU.subtract, ALU.mult)
                ins.then_inc(s_x1, 1)
                dve.wait_ge(s_x1t_mm, 2 * b + 2)
                dve.tensor_copy(x1T[:, 1, :], bank[1][:, :]).then_inc(s_x1t_d, 1)

                logits = bank[2][:, 0:TILES * E].rearrange("p (i e) -> p i e", e=E)
                dve.wait_ge(s_log, b + 1)
                link(dve.tensor_reduce(rt_m[:, 0, :], logits, AX.X, ALU.max))
                dve.tensor_tensor(rt_p[:, :, :], logits, bc(rt_m[:, 0, :].unsqueeze(2), [P, TILES, E]),
                                  ALU.subtract).then_inc(s_logd, 1)
                dve.wait_ge(s_rexp, b + 1)
                link(dve.tensor_reduce(rt_m[:, 1, :], rt_e[:, :, :], AX.X, ALU.add))
                link(dve.reciprocal(rt_m[:, 2, :], rt_m[:, 1, :]))
                dve.tensor_tensor(rt_p[:, :, :], rt_e[:, :, :], bc(rt_m[:, 2, :].unsqueeze(2), [P, TILES, E]), ALU.mult)
                dve.drain()
                for i in range(TILES):
                    ins = dve.max(top[:, i, :], rt_p[:, i, :])
                dve.drain()
                for i in range(TILES):
                    ins = dve.max_index(top_ix[:, i, :], top[:, i, :], rt_p[:, i, :])
                link(ins)
                dve.tensor_reduce(rt_m[:, 3, :], top[:, :, 0:TOPK], AX.X, ALU.add)
                link(dve.tensor_copy(top_f[:, :, :], top_ix[:, :, :]))
                link(dve.tensor_scalar(rt_m[:, 0, :], rt_m[:, 3, :], 1e-20, None, ALU.add))
                dve.reciprocal(rt_m[:, 1, :], rt_m[:, 0, :])
                four = [P, TILES, TOPK, E]
                iota_b = bc(const("iota_e").unsqueeze(1).unsqueeze(1), four)
                link(dve.tensor_tensor(onehot[:, :, :, :], iota_b, bc(top_f[:, :, 0:TOPK].unsqueeze(3), four),
                                       ALU.is_equal))
                dve.tensor_reduce(chosen[:, :, :], onehot[:, :, :, :].rearrange("p i k e -> p i e k"), AX.X,
                                  ALU.add).then_inc(s_cho, 1)
                link(dve.tensor_tensor(weight[:, :, :], top[:, :, 0:TOPK],
                                       bc(rt_m[:, 1, :].unsqueeze(2), [P, TILES, TOPK]), ALU.mult))
                places = bank[3][:, 0:TILES * E].rearrange("p (i e) -> p i e", e=E)
                dve.wait_ge(s_pos, b + 1)
                dve.tensor_scalar(slot_inv[:, :, :], places, float(CAP), DROPPED, ALU.is_ge, ALU.mult)
                dve.tensor_tensor(slot_e[:, :, :], places, bc(const("e_cap").unsqueeze(1), [P, TILES, E]), ALU.add)
                link(dve.tensor_reduce(run_add[:, :], chosen[:, :, :].rearrange("p i e -> p e i"), AX.X, ALU.add))
                dve.tensor_tensor(run[:, :], run[:, :], run_add[:, :], ALU.add)
                link(dve.tensor_tensor(slot_e[:, :, :], slot_e[:, :, :], slot_inv[:, :, :], ALU.add))
                link(dve.tensor_tensor(picked[:, :, :, :], onehot[:, :, :, :], bc(slot_e[:, :, :].unsqueeze(2), four),
                                       ALU.mult))
                link(dve.tensor_reduce(slot[:, :, :], picked[:, :, :, :], AX.X, ALU.add))
                dve.wait_ge(s_scat, SCAT * b)
                dve.tensor_copy(slot_u[:, :], slot[:, :, :].rearrange("p i k -> p (i k)")).then_inc(s_slot, 1)
                dve.tensor_copy(all_slot[:, bass.ds(TILES * b, TILES), :], slot[:, :, :])
                link(dve.tensor_scalar(valid[:, :, :], slot[:, :, :], DROPPED / 2, None, ALU.is_lt))
                dve.tensor_tensor(all_weight[:, bass.ds(TILES * b, TILES), :], weight[:, :, :], valid[:, :, :], ALU.mult)
                link(dve.tensor_copy(all_onehot[:, bass.ds(TILES * b, TILES), :, :], onehot[:, :, :, :]))

                def hidden(i):
                    m = TILES * b + i
                    dve.wait_ge(s_silu, m + 1)
                    dve.tensor_tensor(sh_s[i % 2][:, :], sh_s[i % 2][:, :], bank[5 + 2 * (i % 2)][:, 0:FS],
                                      ALU.mult).then_inc(s_sh, 1)

                def store_hT(i):
                    m = TILES * b + i
                    dve.wait_ge(s_sht_mm, m + 1)
                    dve.tensor_copy(sh_hT[:, 0:2, :], bank[0][:, 0:2 * P].rearrange("p (c t) -> p c t", c=2))
                    dve.tensor_copy(sh_hT[0:SHC[2][1], 2, :], bank[0][0:SHC[2][1], 2 * P:3 * P]).then_inc(s_sht, 1)

                def add_shared(i):
                    m = TILES * b + i
                    dve.wait_ge(s_sd, m + 1)
                    if i == 0:
                        dve.wait_ge(s_acc_st, 16 * b)
                    dve.tensor_tensor(acc[:, i, :], bank[1][:, 0:D], x1[:, i, :], ALU.add).then_inc(s_acc, 1)

                hidden(0)
                hidden(1)
                store_hT(0)
                add_shared(0)
                hidden(2)
                store_hT(1)
                add_shared(1)
                hidden(3)
                store_hT(2)
                add_shared(2)
                store_hT(3)
                add_shared(3)
                link.end()

            cnt, nblk, before, upto, base_m, tmp = (bl[:, j, :] for j in range(6))
            link = Links(s_link2, None)
            link.start(0)
            dve.wait_ge(s_link, LINKS * B)
            dve.memset(credit[:, 6:7], 0.0).then_inc(s_run, 1)
            dve.wait_ge(s_cnt, 1)
            link(dve.tensor_scalar(cnt, bank[2][:, 0:E], float(CAP), None, ALU.min))
            link(dve.tensor_tensor(bl_gt, bc(cnt.unsqueeze(2), [P, E, CAPB]),
                                   bc(const("j_128").unsqueeze(1), [P, E, CAPB]), ALU.is_gt))
            link(dve.tensor_reduce(nblk, bl_gt, AX.X, ALU.add))
            link(dve.tensor_tensor(bl_tri, bc(nblk.unsqueeze(1), [P, E, E]), tri, ALU.mult))
            link(dve.tensor_reduce(before, bl_tri, AX.X, ALU.add))
            link(dve.tensor_tensor(upto, before, nblk, ALU.add))
            link(dve.tensor_scalar(tmp, upto, const("part"), None, ALU.is_le))
            link(dve.tensor_reduce(bcol[:, 1:2], tmp, AX.X, ALU.add))
            link(dve.tensor_scalar(bcol[:, 0:1], bcol[:, 1:2], float(E - 1), None, ALU.min))
            link(dve.tensor_scalar(tmp, const("iota_e"), bcol[:, 0:1], None, ALU.is_equal))
            link(dve.tensor_tensor(tmp, tmp, before, ALU.mult))
            link(dve.tensor_reduce(bcol[:, 2:3], tmp, AX.X, ALU.add))
            link(dve.tensor_tensor(bcol[:, 3:4], const("part"), bcol[:, 2:3], ALU.subtract))
            link(dve.tensor_scalar(bcol[:, 4:5], bcol[:, 3:4], float(CAPB - 1), None, ALU.min))
            link(dve.scalar_tensor_tensor(out=bcol[:, 5:6], in0=bcol[:, 0:1], scalar=float(CAPB), in1=bcol[:, 4:5],
                                          op0=ALU.mult, op1=ALU.add))
            dve.tensor_copy(row_u[:, :], bcol[:, 5:6]).then_inc(s_row, 1)
            link(dve.tensor_scalar(tmp, before, float(P), None, ALU.mult))
            link(dve.tensor_tensor(base_m, tmp, const("e_cap"), ALU.subtract))
            dve.wait_ge(s_bt, 1)
            dve.tensor_copy(exp_i[:, :], bank[4][0:1, 0:P]).then_inc(s_blk, 1)
            dve.wait_ge(s_bt, 2)
            dve.tensor_copy(tok_u[:, :], bank[5][:, 0:P]).then_inc(s_blk, 1)
            four = [P, TILES, TOPK, E]
            for q in range(B):
                link(dve.tensor_tensor(picked[:, :, :, :], all_onehot[:, q * TILES:(q + 1) * TILES, :, :],
                                       bc(base_m.unsqueeze(1).unsqueeze(1), four), ALU.mult))
                link(dve.tensor_reduce(delta[:, q * TILES:(q + 1) * TILES, :], picked[:, :, :, :], AX.X, ALU.add))
            link(dve.tensor_tensor(delta[:, :, :], delta[:, :, :], all_slot[:, :, :], ALU.add))
            link(dve.tensor_scalar(y_row[:, :, :], all_slot[:, :, :], DROPPED / 2, None, ALU.is_lt))
            link(dve.tensor_tensor(y_row[:, :, :], y_row[:, :, :], delta[:, :, :], ALU.mult))
            dve.tensor_copy(y_row_u[:, :, :], y_row[:, :, :]).then_inc(s_yrow, 1)

            def block_xT(m, u):
                dve.wait_ge(s_mx_mm, m + 1)
                dve.tensor_copy(xgT[u], bank[u][:, 0:D]).then_inc(s_mxT, 1)

            def block_hidden(m, u):
                dve.wait_ge(s_msilu, m + 1)
                dve.tensor_tensor(hid[u], silu_g[u], bank[2 + u][:, F:2 * F], ALU.mult).then_inc(s_mh, 1)

            def block_hT(m, u):
                dve.wait_ge(s_mht_mm, m + 1)
                dve.tensor_copy(hidT[u], bank[4 + u][0:FH, 0:2 * P]).then_inc(s_mhT, 1)

            block_xT(0, 0)
            block_xT(1, 1)
            block_hidden(0, 0)
            with dve.Fori(0, NBLK // 2 - 1) as it:
                for u in range(2):
                    m = 2 * it + u
                    block_hT(m, u)
                    block_xT(m + 2, u)
                    block_hidden(m + 1, 1 - u)
            block_hT(NBLK - 2, 0)
            block_hidden(NBLK - 1, 1)
            block_hT(NBLK - 1, 1)

            link = Links(s_link3, LINKS_C)
            with dve.Fori(0, NT // 2) as it:
                for u in range(2):
                    t = 2 * it + u
                    link.start(t * LINKS_C)
                    link(dve.tensor_copy(cw[:, :], all_weight[:, bass.ds(t, 1), :].squeeze(1)))
                    dve.wait_ge(s_cld[u], 16 * (it + 1))
                    dve.wait_ge(s_cg[u], 16 * TOPK * (it + 1))
                    for k in range(TOPK):
                        link(dve.scalar_tensor_tensor(out=cacc[u], in0=got[u][:, k, :], scalar=cw[:, k:k + 1],
                                                      in1=cacc[u], op0=ALU.mult, op1=ALU.add))
                    dve.bn_stats(bn6[:, 0, :], cacc[u])
                    dve.drain()
                    link(dve.bn_aggr(cs[:, 0:2], bn6[:, 0, :]))
                    dve.tensor_scalar(cs[:, 2:3], cs[:, 1:2], EPS_LN, None, ALU.add).then_inc(s_cvar, 1)
                    dve.wait_ge(s_cstd, t + 1)
                    link(dve.reciprocal(credit[:, 7:8], cs[:, 3:4]))
                    dve.wait_ge(s_cst[u], 16 * it)
                    dve.tensor_scalar(cout[u], cacc[u], cs[:, 0:1], credit[:, 7:8], ALU.subtract,
                                      ALU.mult).then_inc(s_cout, 1)
                    dve.wait_ge(s_cout, t + 1)
                    dve.memset(bcol[:, 7:8], 0.0).then_inc(s_cfree, 1)
                    link.end()

        @block.gpsimd
        def _(pool):
            pool.wait_ge(s_const, 16)
            pool.tensor_copy(ids_now[:, :], const("ids")).then_inc(s_ids, 1)
            pool.wait_ge(s_ids, 1)

            def rotate(n, b, i):
                s = i % 2
                c = bc2(cos2[:, i % TILES, :])
                q = q_raw[s]
                pool.wait_ge(s_rope, n)
                pool.wait_ge(s_qcopy, n + 1)
                pool.tensor_tensor(rope_a[:, :, :], q[:, :, 0:ROPE], c, ALU.mult)
                pool.tensor_tensor(rope_b[:, :, :], q[:, :, 0:ROPE], bc2(sin2[:, i % TILES, :]), ALU.mult).then_inc(s_rope_c, 1)
                pool.wait_ge(s_rope_c, n + 1)
                pool.tensor_tensor(q[:, :, 0:HALF], rope_a[:, :, 0:HALF], rope_b[:, :, HALF:ROPE], ALU.subtract)
                pool.tensor_tensor(q[:, :, HALF:ROPE], rope_a[:, :, HALF:ROPE], rope_b[:, :, 0:HALF], ALU.add).then_inc(s_rope, 1)

            def bc2(ap):
                return ap.unsqueeze(1).broadcast_to([P, 2, ROPE])

            with pool.Fori(0, B) as b:
                for i in range(3):
                    rotate(UNITS * b + i, b, i)
                with pool.Fori(0, PAIRS - 1) as p:
                    for i in range(TILES):
                        rotate(UNITS * b + TILES * p + i + 3, b, i + 3)
                rotate(UNITS * b + UNITS - 1, b, 3)
                pool.wait_ge(s_scat, SCAT * b)
                pool.wait_ge(s_slot, b + 1)
                pool.tensor_tensor(ids_now[:, :], ids_now[:, :], const("seq_len"), ALU.add).then_inc(s_ids, 1)
                pool.drain()
                pool.wait_ge(s_table0, 16)
                for i in range(TILES):
                    for k in range(TOPK):
                        c = i * TOPK + k
                        pool.indirect_dma_start(table_dram, bass.IndirectOffsetOnAxis(slot_u[:, c:c + 1], 0),
                                                ids_now[:, i:i + 1], None, bounds_check=E * CAP - 1,
                                                oob_is_err=False).then_inc(s_scat, 16)
            pool.wait_ge(s_row, 1)
            pool.wait_ge(s_scat, SCAT * B)
            pool.indirect_dma_start(rows[:, :], None, table_dram.rearrange("(r c) a -> r (c a)", c=P),
                                    bass.IndirectOffsetOnAxis(row_u[:, 0:1], 0)).then_inc(s_rows, 16)
            pool.wait_ge(s_x1_st, 16 * B)
            pool.wait_ge(s_acc, TILES * B)
            pool.wait_ge(s_blk, 2)
            with pool.Fori(0, NBLK // 2) as it:
                for u in range(2):
                    m = 2 * it + u
                    pool.wait_ge(s_mxT, m)
                    pool.wait_ge(s_g[u], 16 * it)
                    pool.tensor_copy(gidx[:, u:u + 1], tok_u[:, bass.ds(m, 1)]).then_inc(s_gix, 1)
                    pool.drain()
                    pool.indirect_dma_start(xg[u], None, x1_dram,
                                            bass.IndirectOffsetOnAxis(gidx[:, u:u + 1], 0)).then_inc(s_g[u], 16)
            pool.wait_ge(s_yrow, 1)
            for u in range(2):
                pool.wait_ge(s_yst[u], 16 * (NBLK // 2))
            with pool.Fori(0, NT // 2) as it:
                for u in range(2):
                    t = 2 * it + u
                    pool.wait_ge(s_cg[u], 16 * TOPK * it)
                    pool.wait_ge(s_cfree, t)
                    pool.tensor_copy(cidx[u][:, :], y_row_u[:, bass.ds(t, 1), :].squeeze(1)).then_inc(s_cix, 1)
                    pool.drain()
                    for k in range(TOPK):
                        pool.indirect_dma_start(got[u][:, k, :], None, y_dram,
                                                bass.IndirectOffsetOnAxis(cidx[u][:, k:k + 1], 0)).then_inc(s_cg[u], 16)


_INS = ["L0_attn_x", "L0_attn_wq", "L0_attn_wkv_a", "L0_attn_wkv_b", "L0_attn_wo", "L0_attn_kv_norm_w",
        "L0_ffn_wg_router", "L0_ffn_w_gate", "L0_ffn_w_up", "L0_ffn_w_down", "L0_ffn_ws_gate", "L0_ffn_ws_up",
        "L0_ffn_ws_down"]


def shape_constants():
    import numpy as np

    freqs = 1.0 / 10000.0 ** (np.arange(0, ROPE, 2, dtype=np.float32) / ROPE)
    ang = np.outer(np.arange(S, dtype=np.float32), freqs)
    p = np.arange(P)

    def rope(t):
        t = t.reshape(TILES, P, HALF).transpose(1, 0, 2)
        return np.concatenate([t, t], axis=2).reshape(P, TILES * ROPE)

    def rows(v):
        return np.broadcast_to(v, (P, v.size))

    e = np.arange(E)
    parts = {
        "ident": np.eye(P),
        "mask": np.where(p[None, :] > p[:, None], -1e30, 0.0),
        "before": (p[:, None] < p[None, :]),
        "ones": np.ones((P, P)),
        "cos2": rope(np.cos(ang)),
        "sin2": rope(np.sin(ang)),
        "iota_e": rows(e),
        "e_cap": rows(e * CAP),
        "j_128": rows(np.arange(CAPB) * P),
        "part": p[:, None],
        "ids": p[:, None] + P * np.arange(TILES)[None, :] - S,
        "seq_len": np.full((P, TILES), S),
        "tri": rows((e[None, :] < e[:, None]).reshape(-1)),
    }
    return np.concatenate([parts[k].astype(np.float32) for k in CONSTS], axis=1)


def kernel(**inputs):
    import numpy as np
    import concourse.bacc as bacc
    from concourse.bass_utils import run_bass_kernel_spmd

    nc = bacc.Bacc("TRN2", target_bir_lowering=False, num_devices=1)
    arrays, args = {}, []
    for name in _INS:
        arrays[name] = np.ascontiguousarray(inputs[name])
    arrays["shape_constants"] = np.ascontiguousarray(shape_constants())
    for name, a in arrays.items():
        args.append(nc.dram_tensor(name, a.shape, mybir.dt.from_np(a.dtype), kind="ExternalInput").ap())
    out = nc.dram_tensor("out", (B, S, D), F32, kind="ExternalOutput").ap()
    layer_kernel(nc, *args, out)
    r = run_bass_kernel_spmd(nc, [arrays], core_ids=[0])
    return r.results[0]["out"]
```

```python
from contextlib import ExitStack

import concourse.bass as bass
from concourse import mybir

F32 = mybir.dt.float32
BF16 = mybir.dt.bfloat16
U32 = mybir.dt.uint32
I32 = mybir.dt.int32
ALU = mybir.AluOpType
ACT = mybir.ActivationFunctionType
AX = mybir.AxisListType

P = 128
B, S, D = 4, 512, 256
H, NOPE, ROPE, LAT, VDIM = 16, 128, 64, 64, 128
QK = NOPE + ROPE
SCALE = float(QK) ** -0.5
HALF = ROPE // 2
KD = D // P
TILES = S // P
PAIRS = H // 2
UNITS = PAIRS * TILES
E, TOPK, F = 32, 6, 176
FS = 2 * F
FH = F // 2
CAP = 2 * (B * S * TOPK // E)
CAPB = CAP // P
NBLK = 128
WCOLS = KD * 2 * F + 2 * D
ROWS = B * S + P
DROPPED = float(1 << 20)
EPS_RMS, EPS_LN = 1e-6, 1e-5
STAGE_EXPERTS = 14
HEAD_EXPERTS = 14
AHEAD = 6
GROUP = 2
SHC = [(0, 128), (128, 128), (256, 96)]

CONSTS = {}


def const_layout():
    at = 0
    for name, n in (("ident", P), ("mask", P), ("before", P), ("ones", P), ("cos2", TILES * ROPE),
                    ("sin2", TILES * ROPE), ("iota_e", E), ("e_cap", E), ("j_128", CAPB),
                    ("part", 1), ("ids", TILES), ("seq_len", TILES), ("tri", E * E)):
        CONSTS[name] = (at, n)
        at += n
    return at


NCONST = const_layout()


def layer_kernel(nc, x, wq, wkv_a, wkv_b, wo, kv_w, w_router, w_gate, w_up, w_down, ws_gate, ws_up,
                 ws_down, consts, empty_table, out):
    x1_dram = nc.dram_tensor("x1_rows", (ROWS, D), F32, kind="Internal").ap()
    sum_dram = [nc.dram_tensor(f"sum_rows{u}", (ROWS, D), F32, kind="Internal").ap() for u in range(2)]
    table_dram = nc.dram_tensor("slot_table", (E * CAP, 2), F32, kind="Internal").ap()

    out_rows = out.rearrange("b s d -> (b s) d")

    with ExitStack() as ctx:
        def sb(name, shape, dt=F32):
            return ctx.enter_context(nc.sbuf_tensor(name, shape, dt))

        def sem(name):
            return ctx.enter_context(nc.semaphore(name))

        WREG = sb("expert_weights", [P, E * WCOLS])
        at = [0, STAGE_EXPERTS * WCOLS]

        def stage(n, *dims):
            v = WREG[:, at[0]:at[0] + n]
            at[0] += n
            assert at[0] <= at[1]
            names = "abc"[:len(dims)]
            if len(dims) == 1:
                return v
            spec = " ".join(names)
            return v.rearrange(f"p ({spec}) -> p {spec}", **dict(zip(names, dims)))

        wq_nope = stage(H * D, H, D)
        wq_rope = stage(PAIRS * D, PAIRS, D)
        wkvb = stage(2 * H * LAT, 2 * H, LAT)
        wo_raw = stage(2 * H * VDIM, KD, H * VDIM)
        wkva = stage(D, D)
        wo_t = stage(H * D, H, D)
        at[0], at[1] = HEAD_EXPERTS * WCOLS, E * WCOLS
        w_query = stage(KD * H * P, KD, H * P)
        o_all = stage(TILES * H * LAT, TILES, H * LAT)
        x_in = stage(TILES * D, TILES, D)
        xT = stage(KD * S, KD, S)
        keyT = stage(S, S)
        k_all = stage(TILES * P, TILES, P)
        probs = [stage(2 * S, 2, S) for _ in range(2)]
        probsT = [stage(S, TILES, P) for _ in range(2)]
        w_value_out = stage(PAIRS * D, PAIRS, D)
        oT = [stage(PAIRS * P, PAIRS, P) for _ in range(2)]
        acc = stage(TILES * D, TILES, D)
        wsgu = stage(KD * 2 * FS, KD, 2 * FS)
        wsd = stage(len(SHC) * D, len(SHC), D)
        rope_a = stage(2 * ROPE, 2, ROPE)
        rope_b = stage(2 * ROPE, 2, ROPE)

        cst = sb("cst", [P, NCONST])

        def const(name, *dims):
            a, n = CONSTS[name]
            v = cst[:, a:a + n]
            if dims:
                v = v.rearrange("p (a b) -> p a b", a=dims[0], b=dims[1])
            return v

        ident = const("ident")
        cos2, sin2 = const("cos2", TILES, ROPE), const("sin2", TILES, ROPE)
        tri = const("tri", E, E)
        ident_bf = sb("ident_bf", [P, P], BF16)
        mask_bf = sb("mask_bf", [P, P], BF16)
        kvw = sb("kvw", [P, LAT])
        wkvaT = sb("wkvaT", [P, KD, P])
        wr_raw = sb("wr_raw", [E, D])
        wrT = sb("wrT", [P, KD, E])
        q_raw = [sb(f"q_raw{u}", [P, 2, P]) for u in range(2)]
        qT = [sb(f"qT{u}", [P, 2, P]) for u in range(2)]
        kv_raw = sb("kv_raw", [P, TILES, P])
        k_a = sb("k_a", [P, TILES, ROPE])
        k_b = sb("k_b", [P, TILES, ROPE])
        k_c = sb("k_c", [P, TILES, LAT])
        key = sb("key", [P, TILES, P])
        neg_max = [sb(f"neg_max{i}", [P, 2]) for i in range(TILES)]
        row_sum = [sb(f"row_sum{i}", [P, 2]) for i in range(TILES)]
        row_inv = [sb(f"row_inv{i}", [P, 2]) for i in range(TILES)]
        x_res = sb("x_res", [P, TILES, D])
        stat = sb("stat", [P, 8 * TILES])
        bn6 = sb("bn6", [P, TILES, 6])
        mv = sb("mv", [P, TILES, 2])
        ln_s = sb("ln_s", [P, 3, TILES])
        x1 = sb("x1", [P, TILES, D])
        x1T = sb("x1T", [P, KD, S])
        sh_s = [sb(f"sh_s{u}", [P, FS]) for u in range(2)]
        sh_hT = sb("sh_hT", [P, len(SHC), P])
        rt_e = sb("rt_e", [P, TILES, E])
        rt_p = sb("rt_p", [P, TILES, E])
        rt_m = sb("rt_m", [P, 4, TILES])
        top = sb("top", [P, TILES, 8])
        top_ix = sb("top_ix", [P, TILES, 8], U32)
        top_f = sb("top_f", [P, TILES, 8])
        onehot = sb("onehot", [P, TILES, TOPK, E], BF16)
        picked = sb("picked", [P, TILES, TOPK, E])
        chosen = sb("chosen", [P, TILES, E])
        run = sb("run", [P, E])
        run_add = sb("run_add", [P, E])
        slot_e = sb("slot_e", [P, TILES, E])
        slot_inv = sb("slot_inv", [P, TILES, E])
        slot = sb("slot", [P, TILES, TOPK])
        slot_u = sb("slot_u", [P, TILES * TOPK], U32)
        ids_now = sb("ids_now", [P, TILES])
        entry = sb("entry", [P, TILES, TOPK, 2])
        bl = sb("bl", [P, 5, E])
        bl_gt = picked[:, 0, :, :].rearrange("p k e -> p (k e)").rearrange("p (e j) -> p e j", j=CAPB)
        bl_tri = x1T[:, :, :].rearrange("p k s -> p (k s)").rearrange("p (a b) -> p a b", b=E)
        bcol = sb("bcol", [P, 8])
        row_u = sb("row_u", [P, 1], U32)
        rows = sb("rows", [P, P, 2])
        exp_i = sb("exp_i", [1, P], I32)
        tok_u = sb("tok_u", [P, NBLK + AHEAD + 2], U32)
        slot_w = sb("slot_w", [P, NBLK])
        first_ix = sb("first_ix", [P, AHEAD], U32)
        block_ix = sb("block_ix", [P, 8, 2], U32)
        xg = [x1[:, r, :] for r in range(4)]
        xgT = [x1T[:, 0, u * D:(u + 1) * D] for u in range(2)]
        hid = [sh_s[u][:, 0:F] for u in range(2)]
        hidT = [kv_raw[0:FH, 2 * u:2 * u + 2, :].rearrange("p a b -> p (a b)") for u in range(2)]
        silu_g = [sh_s[u][:, F:2 * F] for u in range(2)]
        y_out = ([t[:, :, :].rearrange("p i c -> p (i c)") for t in (k_a, k_b)] +
                 [key[:, 2 * u:2 * u + 2, :].rearrange("p i c -> p (i c)") for u in range(2)])
        sums = [[WREG[:, (2 * q + j) * TILES * D:(2 * q + j + 1) * TILES * D].rearrange("p (i d) -> p i d", d=D)
                 for j in range(2)] for q in range(B)]
        out_mv = sb("out_mv", [P, B, TILES, 2])
        out_s = sb("out_s", [P, B, 3, TILES])
        credit = sb("credit", [P, 10])

        bank = [ctx.enter_context(nc.psum_tensor(f"bank{i}", [P, 512], F32)) for i in range(8)]

        s_const = sem("const_loaded")
        s_raw_nope = sem("raw_nope_and_kv_b_loaded")
        s_raw_rope = sem("raw_rope_and_kv_a_loaded")
        s_raw_wo = sem("raw_wo_loaded")
        s_small = sem("small_weights_loaded")
        s_zero = sem("zero_source_ready")
        s_table0 = sem("table_emptied")
        s_bf = sem("bf_consts_ready")
        s_prep_mm = sem("prep_round_in_psum")
        s_prep_even = sem("prep_even_round_stored")
        s_prep_odd = sem("prep_odd_round_stored")
        s_x = sem("x_loaded")
        s_xt_mm = sem("xT_in_psum")
        s_xt_a = sem("xT_half0_stored")
        s_xt_d = sem("xT_half1_stored")
        s_kv_mm = sem("kv_in_psum")
        s_kv = sem("kv_copied")
        s_ms = sem("kv_mean_square_ready")
        s_rms = sem("kv_rms_ready")
        s_key = sem("key_ready")
        s_key_mm = sem("keyT_in_psum")
        s_keyT = sem("keyT_stored")
        s_proj = sem("q_in_psum")
        s_qcopy = sem("q_copied")
        s_rope = sem("q_rotated")
        s_rope_c = sem("rope_step")
        s_qt_mm = sem("qT_in_psum")
        s_qT = sem("qT_stored")
        s_score = sem("scores_in_psum")
        s_max = sem("max_ready")
        s_exp = sem("exp_done")
        s_pt0 = sem("probsT0_in_psum")
        s_pt1 = sem("probsT1_in_psum")
        s_pt0s = sem("probsT0_stored")
        s_pt1s = sem("probsT1_stored")
        s_pv = sem("pv_done")
        s_inv = sem("row_inverse_ready")
        s_norm = sem("head_output_stored")
        s_ot_mm = sem("oT_in_psum")
        s_ota = sem("oT_low_stored")
        s_otb = sem("oT_high_stored")
        s_y = sem("attention_y_in_psum")
        s_res = sem("residual_added")
        s_var = sem("ln_variance_ready")
        s_std = sem("ln_std_ready")
        s_x1 = sem("x1_ready")
        s_x1_st = sem("x1_rows_stored")
        s_x1t_mm = sem("x1T_in_psum")
        s_x1t_a = sem("x1T_half0_stored")
        s_x1t_d = sem("x1T_half1_stored")
        s_log = sem("logits_in_psum")
        s_logd = sem("logits_shifted")
        s_rexp = sem("router_exp_ready")
        s_cho = sem("chosen_ready")
        s_pos = sem("places_in_psum")
        s_slot = sem("slots_ready")
        s_ids = sem("ids_ready")
        s_scat = sem("ids_scattered")
        s_gu = sem("shared_gate_up_in_psum")
        s_silu = sem("shared_silu_ready")
        s_sh = sem("shared_hidden_ready")
        s_sht_mm = sem("shared_hiddenT_in_psum")
        s_sht = sem("shared_hiddenT_stored")
        s_sd = sem("shared_down_in_psum")
        s_acc = sem("acc_ready")
        s_acc_st = sem("acc_rows_stored")
        s_run = sem("counts_final")
        s_cnt = sem("counts_in_psum")
        s_row = sem("block_rows_ready")
        s_xr = sem("residual_x_loaded")
        s_rows = sem("block_slots_gathered")
        s_bt = sem("block_tables_in_psum")
        s_blk = sem("block_tables_ready")
        s_w = sem("expert_weights_loaded")
        s_g = [sem(f"tokens_gathered{u}") for u in range(4)]
        s_ix = sem("block_indices_copied")
        s_mx_mm = sem("block_xT_in_psum")
        s_mxT = sem("block_xT_stored")
        s_mgu = sem("block_gate_up_in_psum")
        s_msilu = sem("block_silu_ready")
        s_mh = sem("block_hidden_ready")
        s_mht_mm = sem("block_hiddenT_in_psum")
        s_mhT = sem("block_hiddenT_stored")
        s_mdn = sem("block_down_in_psum")
        s_my = sem("block_y_copied")
        s_add = [sem(f"results_added{u}") for u in range(2)]
        s_spare = sem("spare_rows_zeroed")
        s_cld = [sem(f"sums_loaded{q}") for q in range(B)]
        s_sum = sem("sums_ready")
        s_cvar = sem("out_variance_ready")
        s_cstd = sem("out_std_ready")
        s_cout = sem("out_tiles_ready")
        s_cst = sem("out_stored")
        s_bn = sem("row_statistics_ready")
        s_slots_read = sem("places_read")
        s_link_key = sem("vector_step_keys")
        s_link = sem("vector_step")
        s_link2 = sem("vector_step_blocks")
        s_link3 = sem("vector_step_combine")

        N_SMALL = 7
        PREP_ROUNDS = 22
        LOADS = (E // GROUP) * 6
        SCAT = TILES * TOPK * 16
        KEY_LINKS = 5
        LINKS = 15

        w_view = WREG[:, :].rearrange("p (e c) -> p e c", e=E)

        def load_experts(eng, g):
            e0 = g * GROUP
            for k in range(KD):
                for j, w in enumerate((w_gate, w_up)):
                    at0 = k * 2 * F + j * F
                    eng.dma_start(w_view[:, e0:e0 + GROUP, at0:at0 + F],
                                  w[e0:e0 + GROUP, k * P:(k + 1) * P, :].rearrange("e p f -> p e f")).then_inc(s_w, 16)
            for j in range(2):
                at0 = KD * 2 * F + j * D
                eng.dma_start(w_view[0:FH, e0:e0 + GROUP, at0:at0 + D],
                              w_down[e0:e0 + GROUP, j * FH:(j + 1) * FH, :].rearrange("e p d -> p e d")).then_inc(s_w, 16)

        block = ctx.enter_context(nc.Block())

        @block.sync
        def _(sp):
            sp.dma_start(cst[:, :], consts).then_inc(s_const, 16)
            wq_h = wq.rearrange("(h r) d -> h r d", r=QK)
            sp.dma_start(wkvb, wkv_b.rearrange("(h r) c -> r h c", r=P)).then_inc(s_raw_nope, 16)
            sp.dma_start(wq_nope, wq_h[:, 0:NOPE, :].rearrange("h r d -> r h d")).then_inc(s_raw_nope, 16)
            for o in range(2):
                sp.dma_start(wq_rope[o * ROPE:(o + 1) * ROPE, :, :],
                             wq.rearrange("(a o r) d -> o r a d", o=2, r=QK)[o, NOPE:QK, :, :]).then_inc(s_raw_rope, 16)
            sp.dma_start(wkva, wkv_a).then_inc(s_raw_rope, 16)
            sp.dma_start(wo_raw, wo.rearrange("(k p) n -> p k n", p=P)).then_inc(s_raw_wo, 16)
            sp.dma_start(kvw[:, :], kv_w.rearrange("(a c) -> a c", a=1).to_broadcast([P, LAT])).then_inc(s_small, 16)
            sp.dma_start(wr_raw[:, :], w_router).then_inc(s_small, 16)
            sp.dma_start(wsgu[:, :, 0:FS], ws_gate.rearrange("(k p) f -> p k f", p=P)).then_inc(s_small, 16)
            sp.dma_start(wsgu[:, :, FS:2 * FS], ws_up.rearrange("(k p) f -> p k f", p=P)).then_inc(s_small, 16)
            for c, (f0, fn) in enumerate(SHC):
                sp.dma_start(wsd[0:fn, c, :], ws_down[f0:f0 + fn, :]).then_inc(s_small, 16)
            sp.dma_start(table_dram, empty_table).then_inc(s_table0, 16)
            sp.wait_ge(s_zero, 1)
            zeros = x1[:, 0:1, :]
            sp.dma_start(x1_dram[B * S:ROWS, :], x1[:, 0, :]).then_inc(s_spare, 16)
            sp.dma_start(sum_dram[0][B * S:ROWS, :], x1[:, 0, :]).then_inc(s_spare, 16)
            sp.dma_start(sum_dram[1].rearrange("(i p) d -> p i d", p=P),
                         zeros.broadcast_to([P, ROWS // P, D])).then_inc(s_spare, 16)

            def load_x(b):
                sp.dma_start(x_in, x[bass.ds(b, 1), :, :].squeeze(0).rearrange("(i p) d -> p i d", p=P)).then_inc(s_x, 16)

            def load_residual(b):
                sp.dma_start(x_res[:, :, :],
                             x[bass.ds(b, 1), :, :].squeeze(0).rearrange("(i p) d -> p i d", p=P)).then_inc(s_xr, 16)

            def store_sequence(b):
                sp.wait_ge(s_x1, b + 1)
                sp.dma_start(x1_dram[bass.ds(b * S, S), :].rearrange("(i p) d -> p i d", p=P),
                             x1[:, :, :]).then_inc(s_x1_st, 16)
                sp.wait_ge(s_acc, TILES * (b + 1))
                sp.dma_start(sum_dram[0][bass.ds(b * S, S), :].rearrange("(i p) d -> p i d", p=P),
                             acc).then_inc(s_acc_st, 16)

            load_x(0)
            sp.wait_ge(s_prep_even, 11)
            sp.wait_ge(s_prep_odd, 11)
            for g in range(HEAD_EXPERTS // GROUP):
                load_experts(sp, g)
            load_residual(0)
            with sp.Fori(0, B - 1) as b:
                sp.wait_ge(s_xt_mm, 2 * (b + 1))
                load_x(b + 1)
                sp.wait_ge(s_res, TILES * (b + 1))
                load_residual(b + 1)
                store_sequence(b)
            store_sequence(B - 1)
            sp.wait_ge(s_acc_st, 16 * B)
            for g in range(HEAD_EXPERTS // GROUP, E // GROUP):
                load_experts(sp, g)

            for u in range(2):
                sp.wait_ge(s_add[u], 16 * (NBLK // 2))
            sp.wait_ge(s_mdn, NBLK)

            for q in range(B):
                for j in range(2):
                    sp.dma_start(sums[q][j], sum_dram[j][q * S:(q + 1) * S, :].rearrange("(i p) d -> p i d", p=P)).then_inc(s_cld[q], 16)
            for q in range(B):
                sp.wait_ge(s_cout, q + 1)
                sp.dma_start(out_rows[q * S:(q + 1) * S, :].rearrange("(i p) d -> p i d", p=P), sums[q][0]).then_inc(s_cst, 16)
            sp.wait_ge(s_cst, 16 * B)
            sp.wait_ge(s_x1_st, 16 * B)
            sp.wait_ge(s_acc_st, 16 * B)
            sp.wait_ge(s_table0, 16)
            sp.wait_ge(s_spare, 48)
            sp.wait_ge(s_scat, SCAT * B)

        @block.tensor
        def _(pe):
            def round_free(r):
                if r >= 8:
                    pe.wait_ge(s_prep_even if r % 2 == 0 else s_prep_odd, (r - 8) // 2 + 1)

            pe.wait_ge(s_const, 16)
            pe.wait_ge(s_raw_nope, 32)
            for k in range(KD):
                for g in range(2):
                    for j in range(8):
                        h = 8 * g + j
                        mm = pe.matmul(bank[2 * k + g][:, j * LAT:(j + 1) * LAT], wq_nope[:, h, k * P:(k + 1) * P],
                                       wkvb[:, 2 * h, :], start=True, stop=True)
                    mm.then_inc(s_prep_mm, 1)
            pe.wait_ge(s_raw_rope, 48)
            for k in range(KD):
                for g in range(2):
                    for j in range(4):
                        mm = pe.transpose(bank[4 + 2 * k + g][:, j * P:(j + 1) * P],
                                          wq_rope[:, 4 * g + j, k * P:(k + 1) * P], ident)
                    mm.then_inc(s_prep_mm, 1)
            round_free(8)
            for k in range(KD):
                mm = pe.transpose(bank[0][:, k * P:(k + 1) * P], wkva[:, k * P:(k + 1) * P], ident)
            mm.then_inc(s_prep_mm, 1)
            pe.wait_ge(s_raw_wo, 16)
            for r in range(9, 17):
                round_free(r)
                for j in range(2):
                    h = 2 * (r - 9) + j
                    for k in range(KD):
                        mm = pe.transpose(bank[r % 8][:, (2 * j + k) * P:(2 * j + k + 1) * P],
                                          wo_raw[:, k, h * VDIM:(h + 1) * VDIM], ident)
                mm.then_inc(s_prep_mm, 1)
            pe.wait_ge(s_prep_even, 9)
            pe.wait_ge(s_prep_odd, 8)
            for r in range(17, 21):
                for j in range(2):
                    for o in range(2):
                        h = 4 * (r - 17) + 2 * j + o
                        mm = pe.matmul(bank[r % 8][o * LAT:(o + 1) * LAT, j * D:(j + 1) * D], wkvb[:, 2 * h + 1, :],
                                       wo_t[:, h, :], start=True, stop=True)
                mm.then_inc(s_prep_mm, 1)
            round_free(21)
            pe.wait_ge(s_small, 16 * N_SMALL)
            for k in range(KD):
                mm = pe.transpose(bank[5][:, k * E:(k + 1) * E], wr_raw[:, k * P:(k + 1) * P], ident[0:E, 0:E])
            mm.then_inc(s_prep_mm, 1)
            pe.wait_ge(s_prep_even, 11)
            pe.wait_ge(s_prep_odd, 11)
            pe.wait_ge(s_bf, 2)

            S_BANK = [(bank[0], bank[1]), (bank[2], bank[3])]
            O_BANK, Q_BANK, QT_BANK = bank[4:6], bank[6], bank[7]

            def project(n, pair, i):
                pe.wait_ge(s_qcopy, n)
                for k in range(KD):
                    mm = pe.matmul(Q_BANK[:, 0:2 * P], xT[:, k, i * P:(i + 1) * P],
                                   w_query[:, k, bass.ds(pair * 2 * P, 2 * P)], start=(k == 0), stop=(k == KD - 1))
                mm.then_inc(s_proj, 1)

            def turn_query(n, slot_):
                pe.wait_ge(s_rope, n + 1)
                pe.wait_ge(s_qT, n)
                for h in range(2):
                    mm = pe.transpose(QT_BANK[:, h * P:(h + 1) * P], q_raw[slot_][:, h, :], ident)
                mm.then_inc(s_qt_mm, 1)

            def scores(n, i):
                u = i % 2
                keys = (i + 1) * P
                pe.wait_ge(s_qT, n + 1)
                pe.wait_ge(s_pt0s, n)
                pe.wait_ge(s_pt1s, n)
                for h in range(2):
                    pe.matmul(S_BANK[u][h][:, 0:keys], qT[u][:, h, :], keyT[:, 0:keys], start=True, stop=False)
                    mm = pe.matmul(S_BANK[u][h][:, i * P:keys], ident_bf[:, :], mask_bf[:, :], start=False, stop=True)
                    mm.then_inc(s_score, 1)

            def turn_probs(n, i, h):
                pe.wait_ge(s_exp, 2 * n + h + 1)
                for j in range(i + 1):
                    mm = pe.transpose(S_BANK[i % 2][h][:, j * P:(j + 1) * P], probs[i % 2][:, h, j * P:(j + 1) * P], ident)
                mm.then_inc(s_pt1 if h else s_pt0, 1)

            def values(n, i, h):
                if h == 0:
                    pe.wait_ge(s_norm, n)
                    pe.wait_ge(s_pt0s, n + 2)
                else:
                    pe.wait_ge(s_pt1s, n + 2)
                for j in range(i + 1):
                    mm = pe.matmul(O_BANK[i % 2][:, h * LAT:(h + 1) * LAT], probsT[h][:, j, :], k_all[:, j, ROPE:P],
                                   start=(j == 0), stop=(j == i))
                if h == 1:
                    mm.then_inc(s_pv, 1)

            def step(b, p, i, first_local):
                n = UNITS * b + TILES * p + i
                last = first_local + i
                turn_probs(n, i, 0)
                turn_probs(n, i, 1)
                if last + 4 < UNITS:
                    project(n + 4, p + 1, i)
                if last + 2 < UNITS:
                    scores(n + 2, (i + 2) % TILES)
                values(n, i, 0)
                values(n, i, 1)
                if last + 3 < UNITS:
                    turn_query(n + 3, (i + 3) % 2)

            def turn_x():
                for k in range(KD):
                    for i in range(TILES):
                        mm = pe.transpose(bank[2 + k][:, i * P:(i + 1) * P], x_in[:, i, k * P:(k + 1) * P], ident)
                    mm.then_inc(s_xt_mm, 1)

            def project_kv(b):
                pe.wait_ge(s_xt_a, b + 1)
                pe.wait_ge(s_xt_d, b + 1)
                pe.wait_ge(s_res, TILES * b)
                for i in range(TILES):
                    for k in range(KD):
                        mm = pe.matmul(bank[4][:, i * P:(i + 1) * P], xT[:, k, i * P:(i + 1) * P], wkvaT[:, k, :],
                                       start=(k == 0), stop=(k == KD - 1))
                mm.then_inc(s_kv_mm, 1)

            def turn_key(b):
                pe.wait_ge(s_key, b + 1)
                for i in range(TILES):
                    mm = pe.transpose(bank[4][:, i * P:(i + 1) * P], key[:, i, :], ident)
                mm.then_inc(s_key_mm, 1)

            def first_queries(n0):
                project(n0, 0, 0)
                project(n0 + 1, 0, 1)

            def more_queries(n0):
                turn_query(n0, 0)
                project(n0 + 2, 0, 2)
                turn_query(n0 + 1, 1)
                project(n0 + 3, 0, 3)

            def first_scores(b):
                n0 = UNITS * b
                pe.wait_ge(s_keyT, b + 1)
                scores(n0, 0)
                scores(n0 + 1, 1)
                turn_query(n0 + 2, 0)

            def units(b):
                with pe.Fori(0, PAIRS - 1) as p:
                    for i in range(TILES):
                        step(b, p, i, 0)
                for i in range(TILES):
                    step(b, PAIRS - 1, i, UNITS - TILES)

            def turn_out(b, i):
                m = TILES * b + i
                u = i % 2
                if i >= 2:
                    pe.wait_ge(s_ota, m - 1)
                    pe.wait_ge(s_otb, m - 1)
                for kk in range(PAIRS):
                    mm = pe.transpose(bank[2 * u + kk // 4][:, (kk % 4) * P:(kk % 4 + 1) * P],
                                      o_all[:, i, kk * P:(kk + 1) * P], ident)
                    if kk % 4 == 3:
                        mm.then_inc(s_ot_mm, 1)

            def project_out(b, i):
                m = TILES * b + i
                pe.wait_ge(s_ota, m + 1)
                pe.wait_ge(s_otb, m + 1)
                if i >= 2:
                    pe.wait_ge(s_res, m - 1)
                for kk in range(PAIRS):
                    mm = pe.matmul(bank[4 + i % 2][:, 0:D], oT[i % 2][:, kk, :], w_value_out[:, kk, :],
                                   start=(kk == 0), stop=(kk == PAIRS - 1))
                mm.then_inc(s_y, 1)

            def gate_up(b, i):
                m = TILES * b + i
                if i >= 2:
                    pe.wait_ge(s_sh, m - 1)
                for half in range(2):
                    for k in range(KD):
                        mm = pe.matmul(bank[2 * (i % 2) + half][:, 0:FS], x1T[:, k, i * P:(i + 1) * P],
                                       wsgu[:, k, half * FS:(half + 1) * FS], start=(k == 0), stop=(k == KD - 1))
                mm.then_inc(s_gu, 1)

            def turn_hidden(b, i):
                m = TILES * b + i
                pe.wait_ge(s_sh, m + 1)
                pe.wait_ge(s_sht, m)
                for c, (f0, fn) in enumerate(SHC):
                    mm = pe.transpose(bank[4][0:fn, c * P:(c + 1) * P], sh_s[i % 2][:, f0:f0 + fn], ident)
                mm.then_inc(s_sht_mm, 1)

            def down(b, i):
                m = TILES * b + i
                pe.wait_ge(s_sht, m + 1)
                pe.wait_ge(s_acc, m)
                for c, (f0, fn) in enumerate(SHC):
                    mm = pe.matmul(bank[5][:, 0:D], sh_hT[0:fn, c, :], wsd[0:fn, c, :],
                                   start=(c == 0), stop=(c == len(SHC) - 1))
                mm.then_inc(s_sd, 1)

            def finish(b, more):
                n1 = UNITS * (b + 1)
                pe.wait_ge(s_norm, UNITS * (b + 1) + 1)
                turn_out(b, 0)
                turn_out(b, 1)
                project_out(b, 0)
                turn_out(b, 2)
                project_out(b, 1)
                turn_out(b, 3)
                project_out(b, 2)
                project_out(b, 3)
                if more:
                    pe.wait_ge(s_x, 16 * (b + 2))
                    turn_x()
                    project_kv(b + 1)
                    first_queries(n1)
                pe.wait_ge(s_x1, b + 1)
                for k in range(KD):
                    for i in range(TILES):
                        mm = pe.transpose(bank[k][:, i * P:(i + 1) * P], x1[:, i, k * P:(k + 1) * P], ident)
                    mm.then_inc(s_x1t_mm, 1)
                pe.wait_ge(s_x1t_a, b + 1)
                pe.wait_ge(s_x1t_d, b + 1)
                for i in range(TILES):
                    for k in range(KD):
                        mm = pe.matmul(bank[5][:, i * E:(i + 1) * E], x1T[:, k, i * P:(i + 1) * P], wrT[:, k, :],
                                       start=(k == 0), stop=(k == KD - 1))
                mm.then_inc(s_log, 1)
                gate_up(b, 0)
                gate_up(b, 1)
                if more:
                    more_queries(n1)
                    turn_key(b + 1)
                pe.wait_ge(s_cho, b + 1)
                for i in range(TILES):
                    o = bank[5][:, i * E:(i + 1) * E]
                    pe.matmul(o, const("ones"), run[:, :], start=True, stop=False)
                    for j in range(i):
                        pe.matmul(o, const("ones"), chosen[:, j, :], start=False, stop=False)
                    mm = pe.matmul(o, const("before"), chosen[:, i, :], start=False, stop=True)
                mm.then_inc(s_pos, 1)
                if more:
                    pe.wait_ge(s_keyT, b + 2)
                turn_hidden(b, 0)
                gate_up(b, 2)
                pe.wait_ge(s_slots_read, b + 1)
                down(b, 0)
                turn_hidden(b, 1)
                gate_up(b, 3)
                down(b, 1)
                turn_hidden(b, 2)
                down(b, 2)
                turn_hidden(b, 3)
                down(b, 3)
                if more:
                    pe.wait_ge(s_acc, TILES * (b + 1))
                    first_scores(b + 1)

            pe.wait_ge(s_x, 16)
            turn_x()
            project_kv(0)
            first_queries(0)
            more_queries(0)
            turn_key(0)
            first_scores(0)
            with pe.Fori(0, B - 1) as b:
                units(b)
                finish(b, True)
            units(B - 1)
            finish(B - 1, False)

            pe.wait_ge(s_run, 1)
            pe.matmul(bank[6][:, 0:E], const("ones"), run[:, :], start=True, stop=True).then_inc(s_cnt, 1)
            pe.wait_ge(s_row, 1)
            pe.matmul(bank[7][0:1, 0:P], bcol[:, 0:1], ident, start=True, stop=True).then_inc(s_bt, 1)
            pe.wait_ge(s_acc, TILES * B)
            pe.wait_ge(s_rows, 16)
            for j in range(2):
                mm = pe.transpose(bank[5][:, j * P:(j + 1) * P], rows[:, :, j], ident)
            mm.then_inc(s_bt, 1)

            XT_B, GU_B, HT_B, Y_B = bank[0:2], bank[2:4], bank[4:6], bank[6:8]

            def block_xT(m, it, r):
                u = r % 2
                pe.wait_ge(s_g[r], 16 * (it + 1))
                pe.wait_ge(s_mxT, m)
                for k in range(KD):
                    mm = pe.transpose(XT_B[u][:, k * P:(k + 1) * P], xg[r][:, k * P:(k + 1) * P], ident)
                mm.then_inc(s_mx_mm, 1)

            def block_expert(m):
                return pe.value_load(exp_i[0:1, bass.ds(m, 1)], min_val=0, max_val=E - 1)

            def block_gate_up(m, u, e):
                pe.wait_ge(s_mxT, m + 2)
                pe.wait_ge(s_mh, m)
                for k in range(KD):
                    mm = pe.matmul(GU_B[u][:, 0:2 * F], xgT[u][:, k * P:(k + 1) * P],
                                   WREG[:, bass.ds(e * WCOLS + k * 2 * F, 2 * F)], start=(k == 0), stop=(k == KD - 1))
                mm.then_inc(s_mgu, 1)

            def block_hT(m, u):
                pe.wait_ge(s_mh, m + 2)
                pe.wait_ge(s_mhT, m)
                for j in range(2):
                    mm = pe.transpose(HT_B[u][0:FH, j * P:(j + 1) * P], hid[u][:, j * FH:(j + 1) * FH], ident)
                mm.then_inc(s_mht_mm, 1)

            def block_down(m, u, e):
                pe.wait_ge(s_mhT, m + 2)
                pe.wait_ge(s_my, m)
                for j in range(2):
                    mm = pe.matmul(Y_B[u][:, 0:D], hidT[u][:, j * P:(j + 1) * P],
                                   WREG[0:FH, bass.ds(e * WCOLS + KD * 2 * F + j * D, D)],
                                   start=(j == 0), stop=(j == 1))
                mm.then_inc(s_mdn, 1)

            pe.wait_ge(s_blk, 2)
            pe.wait_ge(s_w, 16 * LOADS)
            block_xT(0, 0, 0)
            block_xT(1, 0, 1)
            block_gate_up(0, 0, block_expert(0))

            def block_step(m, it, r, left):
                if left > 1:
                    next_expert = block_expert(m + 1)
                if left > 2:
                    block_xT(m + 2, it + (r + 2) // 4, (r + 2) % 4)
                block_hT(m, r % 2)
                if left > 1:
                    block_gate_up(m + 1, (r + 1) % 2, next_expert)
                block_down(m, r % 2, block_expert(m))

            with pe.Fori(0, NBLK // 4 - 1) as it:
                for r in range(4):
                    block_step(4 * it + r, it, r, NBLK)
            for r in range(4):
                block_step(NBLK - 4 + r, NBLK // 4 - 1, r, 4 - r)

        @block.scalar
        def _(act):
            w_q = w_query.rearrange("p k (h c) -> p k h c", c=P)

            def prep(r):
                act.wait_ge(s_prep_mm, r + 1)

            for r in (0, 2):
                prep(r)
                act.copy(w_q[:, r // 2, 0:8, ROPE:P], bank[r][:, :].rearrange("p (h c) -> p h c", c=LAT)).then_inc(s_prep_even, 1)
            for r in (4, 6):
                prep(r)
                act.copy(w_q[:, (r - 4) // 2, 0:8, 0:ROPE].rearrange("p h (t j) -> p h j t", t=2),
                         bank[r][:, :].rearrange("p (h j t) -> p h j t", h=8, t=2)).then_inc(s_prep_even, 1)
            prep(8)
            kv = bank[0][:, 0:KD * P].rearrange("p (k c) -> p k c", k=KD)
            act.copy(wkvaT[:, :, ROPE:P], kv[:, :, 0:LAT])
            act.copy(wkvaT[:, :, 0:ROPE].rearrange("p k (t j) -> p k j t", t=2),
                     kv[:, :, LAT:P].rearrange("p k (j t) -> p k j t", t=2)).then_inc(s_prep_even, 1)
            for r in (10, 12, 14, 16):
                prep(r)
                act.copy(wo_t[:, 2 * (r - 9):2 * (r - 9) + 2, :],
                         bank[r % 8][:, :].rearrange("p (j d) -> p j d", j=2)).then_inc(s_prep_even, 1)
            for r in (18, 20):
                prep(r)
                act.copy(w_value_out[:, 2 * (r - 17):2 * (r - 17) + 2, :],
                         bank[r % 8][:, :].rearrange("p (j d) -> p j d", j=2)).then_inc(s_prep_even, 1)

            def copy_query(n, i):
                act.wait_ge(s_proj, n + 1)
                act.copy(q_raw[i % 2][:, :, :], bank[6][:, 0:2 * P].rearrange("p (h c) -> p h c", h=2)).then_inc(s_qcopy, 1)

            def exps(n, i):
                u = i % 2
                for h in range(2):
                    act.wait_ge(s_max, 2 * n + h + 1)
                    act.activation(probs[u][:, h, 0:(i + 1) * P], bank[2 * u + h][:, 0:(i + 1) * P], ACT.Exp,
                                   bias=neg_max[i][:, h:h + 1], scale=1.0,
                                   accum_out=row_sum[i][:, h:h + 1]).then_inc(s_exp, 1)

            def step(b, p, i, first_local):
                n = UNITS * b + TILES * p + i
                last = first_local + i
                act.wait_ge(s_pt0, n + 1)
                act.copy(probsT[0][:, 0:i + 1, :],
                         bank[2 * (i % 2)][:, 0:(i + 1) * P].rearrange("p (j t) -> p j t", t=P)).then_inc(s_pt0s, 1)
                if last + 1 < UNITS:
                    exps(n + 1, (i + 1) % TILES)
                if last + 4 < UNITS:
                    copy_query(n + 4, i)

            def turn_x(b):
                act.wait_ge(s_xt_mm, 2 * b + 1)
                act.copy(xT[:, 0, :], bank[2][:, :]).then_inc(s_xt_a, 1)
                act.wait_ge(s_kv_mm, b + 1)
                act.copy(kv_raw[:, :, :], bank[4][:, :].rearrange("p (i c) -> p i c", c=P)).then_inc(s_kv, 1)

            def key_rms(b):
                act.wait_ge(s_ms, b + 1)
                act.activation(stat[:, 8:12], stat[:, 4:8], ACT.Sqrt).then_inc(s_rms, 1)

            def more_queries(b):
                copy_query(UNITS * b + 2, 2)
                copy_query(UNITS * b + 3, 3)
                act.wait_ge(s_key_mm, b + 1)
                act.copy(keyT, bank[4][:, :]).then_inc(s_keyT, 1)

            def units(b):
                with act.Fori(0, PAIRS - 1) as p:
                    for i in range(TILES):
                        step(b, p, i, 0)
                for i in range(TILES):
                    step(b, PAIRS - 1, i, UNITS - TILES)

            def finish(b, more):
                n1 = UNITS * (b + 1)
                for i in range(TILES):
                    act.wait_ge(s_ot_mm, 2 * (TILES * b + i) + 1)
                    act.copy(oT[i % 2][:, 0:4, :],
                             bank[2 * (i % 2)][:, :].rearrange("p (j t) -> p j t", t=P)).then_inc(s_ota, 1)
                if more:
                    turn_x(b + 1)
                act.wait_ge(s_var, b + 1)
                act.activation(ln_s[:, 1, :], ln_s[:, 0, :], ACT.Sqrt).then_inc(s_std, 1)
                if more:
                    key_rms(b + 1)
                    copy_query(n1, 0)
                    copy_query(n1 + 1, 1)
                act.wait_ge(s_x1t_mm, 2 * b + 1)
                act.copy(x1T[:, 0, :], bank[0][:, :]).then_inc(s_x1t_a, 1)
                act.wait_ge(s_logd, b + 1)
                act.activation(rt_e[:, :, :], rt_p[:, :, :], ACT.Exp).then_inc(s_rexp, 1)

                def silu(i):
                    m = TILES * b + i
                    act.wait_ge(s_gu, m + 1)
                    act.wait_ge(s_sht_mm, m - 1 if i >= 2 else TILES * b)
                    act.activation(sh_s[i % 2][:, :], bank[2 * (i % 2)][:, 0:FS], ACT.Silu).then_inc(s_silu, 1)

                silu(0)
                silu(1)
                if more:
                    more_queries(b + 1)
                silu(2)
                silu(3)
                if more:
                    exps(n1, 0)

            turn_x(0)
            copy_query(0, 0)
            copy_query(1, 1)
            key_rms(0)
            more_queries(0)
            exps(0, 0)
            with act.Fori(0, B - 1) as b:
                units(b)
                finish(b, True)
            units(B - 1)
            finish(B - 1, False)

            def block_silu(m, u):
                act.wait_ge(s_mgu, m + 1)
                act.activation(silu_g[u], bank[2 + u][:, 0:F], ACT.Silu).then_inc(s_msilu, 1)

            def block_y(a, r):
                m = 4 * a + r
                act.wait_ge(s_mdn, m + 1)
                if not (isinstance(a, int) and a == 0):
                    act.wait_ge(s_add[r % 2], 32 * a + 16 * (r // 2) - 16)
                act.activation(y_out[r], bank[6 + r % 2][:, 0:D], ACT.Copy,
                               scale=slot_w[:, bass.ds(m, 1)]).then_inc(s_my, 1)

            act.wait_ge(s_blk, 2)
            block_silu(0, 0)
            for r in range(4):
                block_silu(r + 1, (r + 1) % 2)
                block_y(0, r)
            with act.Fori(1, NBLK // 4 - 1) as a:
                for r in range(4):
                    block_silu(4 * a + r + 1, (r + 1) % 2)
                    block_y(a, r)
            for r in range(4):
                if r < 3:
                    block_silu(NBLK - 3 + r, (r + 1) % 2)
                block_y(NBLK // 4 - 1, r)
            for q in range(B):
                act.wait_ge(s_cvar, q + 1)
                act.activation(out_s[:, q, 1, :], out_s[:, q, 0, :], ACT.Sqrt).then_inc(s_cstd, 1)

        @block.vector
        def _(dve):
            class Links:

                def __init__(self, s, per):
                    self.s, self.per, self.n, self.base = s, per, 0, 0

                def start(self, base):
                    self.n, self.base = 0, base

                def __call__(self, ins):
                    self.n += 1
                    ins.then_inc(self.s, 1)
                    dve.wait_ge(self.s, self.base + self.n)

                def end(self):
                    assert self.per is None or self.n == self.per, self.n

            for j, s in enumerate((s_pt0s, s_pt1s, s_norm, s_mxT, s_mh, s_mhT, s_my)):
                dve.memset(credit[:, j:j + 1], 0.0).then_inc(s, 1)
            dve.memset(x1[:, 0, :], 0.0).then_inc(s_zero, 1)
            dve.memset(run[:, :], 0.0)
            dve.wait_ge(s_const, 16)
            dve.tensor_copy(ident_bf[:, :], ident).then_inc(s_bf, 1)
            dve.tensor_copy(mask_bf[:, :], const("mask")).then_inc(s_bf, 1)
            dve.tensor_copy(ids_now[:, :], const("ids"))

            w_q = w_query.rearrange("p k (h c) -> p k h c", c=P)

            def prep(r):
                dve.wait_ge(s_prep_mm, r + 1)

            for r in (1, 3):
                prep(r)
                dve.tensor_copy(w_q[:, r // 2, 8:16, ROPE:P],
                                bank[r][:, :].rearrange("p (h c) -> p h c", c=LAT)).then_inc(s_prep_odd, 1)
            for r in (5, 7):
                prep(r)
                dve.tensor_copy(w_q[:, (r - 4) // 2, 8:16, 0:ROPE].rearrange("p h (t j) -> p h j t", t=2),
                                bank[r][:, :].rearrange("p (h j t) -> p h j t", h=8, t=2)).then_inc(s_prep_odd, 1)
            for r in (9, 11, 13, 15):
                prep(r)
                dve.tensor_copy(wo_t[:, 2 * (r - 9):2 * (r - 9) + 2, :],
                                bank[r % 8][:, :].rearrange("p (j d) -> p j d", j=2)).then_inc(s_prep_odd, 1)
            for r in (17, 19):
                prep(r)
                dve.tensor_copy(w_value_out[:, 2 * (r - 17):2 * (r - 17) + 2, :],
                                bank[r % 8][:, :].rearrange("p (j d) -> p j d", j=2)).then_inc(s_prep_odd, 1)
            prep(21)
            dve.tensor_copy(wrT[:, :, :], bank[5][:, 0:KD * E].rearrange("p (k e) -> p k e", k=KD)).then_inc(s_prep_odd, 1)

            link = Links(s_link, LINKS)

            def store_qT(n, i):
                dve.wait_ge(s_qt_mm, n + 1)
                dve.tensor_copy(qT[i % 2][:, :, :], bank[7][:, 0:2 * P].rearrange("p (h t) -> p h t", h=2)).then_inc(s_qT, 1)

            def maxima(n, i):
                u = i % 2
                for h in range(2):
                    dve.wait_ge(s_score, 2 * n + h + 1)
                    dve.tensor_reduce(neg_max[i][:, h:h + 1], bank[2 * u + h][:, 0:(i + 1) * P], AX.X, ALU.max,
                                      negate=True).then_inc(s_max, 1)

            def normalise(n, p, i):
                dve.wait_ge(s_pv, n + 1)
                dve.reciprocal(row_inv[i][:, :], row_sum[i][:, :]).then_inc(s_inv, 1)
                dve.wait_ge(s_inv, n + 1)
                dve.tensor_tensor(o_all[:, i, bass.ds(p * 2 * LAT, 2 * LAT)].rearrange("p (h c) -> p h c", h=2),
                                  bank[4 + i % 2][:, 0:2 * LAT].rearrange("p (h c) -> p h c", h=2),
                                  row_inv[i][:, :].unsqueeze(2).broadcast_to([P, 2, LAT]), ALU.mult).then_inc(s_norm, 1)

            def step(b, p, i, first_local):
                n = UNITS * b + TILES * p + i
                last = first_local + i
                dve.wait_ge(s_pt1, n + 1)
                dve.tensor_copy(probsT[1][:, 0:i + 1, :],
                                bank[2 * (i % 2) + 1][:, 0:(i + 1) * P].rearrange("p (j t) -> p j t", t=P)).then_inc(s_pt1s, 1)
                if last + 2 < UNITS:
                    maxima(n + 2, (i + 2) % TILES)
                normalise(n, p, i)
                if last + 3 < UNITS:
                    store_qT(n + 3, i + 3)

            def bc(ap, shape):
                return ap.broadcast_to(shape)

            key_link = Links(s_link_key, KEY_LINKS)

            def keys_first(b):
                key_link.start(b * KEY_LINKS)
                dve.wait_ge(s_xt_mm, 2 * b + 2)
                dve.tensor_copy(xT[:, 1, :], bank[3][:, :]).then_inc(s_xt_d, 1)
                dve.wait_ge(s_kv, b + 1)
                dve.tensor_tensor(k_a[:, :, :], kv_raw[:, :, 0:ROPE], cos2, ALU.mult)
                dve.tensor_tensor(k_b[:, :, :], kv_raw[:, :, 0:ROPE], sin2, ALU.mult)
                key_link(dve.tensor_tensor(k_c[:, :, :], kv_raw[:, :, ROPE:P], kv_raw[:, :, ROPE:P], ALU.mult))
                dve.tensor_tensor(k_all[:, :, 0:HALF], k_a[:, :, 0:HALF], k_b[:, :, HALF:ROPE], ALU.subtract)
                dve.tensor_tensor(k_all[:, :, HALF:ROPE], k_a[:, :, HALF:ROPE], k_b[:, :, 0:HALF], ALU.add)
                key_link(dve.tensor_reduce(stat[:, 0:4], k_c[:, :, :], AX.X, ALU.add))
                dve.tensor_scalar(stat[:, 4:8], stat[:, 0:4], 1.0 / LAT, EPS_RMS, ALU.mult, ALU.add).then_inc(s_ms, 1)

            def keys_second(b):
                dve.wait_ge(s_rms, b + 1)
                key_link(dve.reciprocal(stat[:, 12:16], stat[:, 8:12]))
                key_link(dve.tensor_tensor(k_c[:, :, :], kv_raw[:, :, ROPE:P],
                                           bc(stat[:, 12:16].unsqueeze(2), [P, TILES, LAT]), ALU.mult))
                key_link(dve.tensor_tensor(k_all[:, :, ROPE:P], k_c[:, :, :],
                                           bc(kvw[:, :].unsqueeze(1), [P, TILES, LAT]), ALU.mult))
                dve.tensor_scalar(key[:, :, :], k_all, SCALE, None, ALU.mult).then_inc(s_key, 1)
                key_link.end()

            def units(b):
                with dve.Fori(0, PAIRS - 1) as p:
                    for i in range(TILES):
                        step(b, p, i, 0)
                for i in range(TILES):
                    step(b, PAIRS - 1, i, UNITS - TILES)

            def finish(b, more):
                n1 = UNITS * (b + 1)
                link.start(b * LINKS)

                def store_oT(i):
                    dve.wait_ge(s_ot_mm, 2 * (TILES * b + i) + 2)
                    dve.tensor_copy(oT[i % 2][:, 4:8, :],
                                    bank[2 * (i % 2) + 1][:, :].rearrange("p (j t) -> p j t", t=P)).then_inc(s_otb, 1)

                def residual(i):
                    dve.wait_ge(s_y, TILES * b + i + 1)
                    if i == 0:
                        dve.wait_ge(s_x1_st, 16 * b)
                        dve.wait_ge(s_spare, 48)
                        dve.wait_ge(s_xr, 16 * (b + 1))
                    dve.tensor_tensor(x1[:, i, :], bank[4 + i % 2][:, 0:D], x_res[:, i, :], ALU.add).then_inc(s_res, 1)
                    dve.wait_ge(s_res, TILES * b + i + 1)
                    dve.bn_stats(bn6[:, i, :], x1[:, i, :]).then_inc(s_bn, 1)

                store_oT(0)
                store_oT(1)
                residual(0)
                store_oT(2)
                residual(1)
                store_oT(3)
                residual(2)
                residual(3)
                dve.drain()
                for i in range(TILES):
                    ins = dve.bn_aggr(mv[:, i, :], bn6[:, i, :])
                link(ins)
                dve.tensor_scalar(ln_s[:, 0, :], mv[:, :, 1], EPS_LN, None, ALU.add).then_inc(s_var, 1)
                if more:
                    keys_first(b + 1)
                dve.wait_ge(s_std, b + 1)
                link(dve.reciprocal(ln_s[:, 2, :], ln_s[:, 1, :]))
                for i in range(TILES):
                    ins = dve.tensor_scalar(x1[:, i, :], x1[:, i, :], mv[:, i, 0:1], ln_s[:, 2, i:i + 1],
                                            ALU.subtract, ALU.mult)
                ins.then_inc(s_x1, 1)
                if more:
                    keys_second(b + 1)
                dve.wait_ge(s_x1t_mm, 2 * b + 2)
                dve.tensor_copy(x1T[:, 1, :], bank[1][:, :]).then_inc(s_x1t_d, 1)

                logits = bank[5][:, 0:TILES * E].rearrange("p (i e) -> p i e", e=E)
                dve.wait_ge(s_log, b + 1)
                link(dve.tensor_reduce(rt_m[:, 0, :], logits, AX.X, ALU.max))
                dve.tensor_tensor(rt_p[:, :, :], logits, bc(rt_m[:, 0, :].unsqueeze(2), [P, TILES, E]),
                                  ALU.subtract).then_inc(s_logd, 1)
                dve.wait_ge(s_rexp, b + 1)
                link(dve.tensor_reduce(rt_m[:, 1, :], rt_e[:, :, :], AX.X, ALU.add))
                link(dve.reciprocal(rt_m[:, 2, :], rt_m[:, 1, :]))
                dve.tensor_tensor(rt_p[:, :, :], rt_e[:, :, :], bc(rt_m[:, 2, :].unsqueeze(2), [P, TILES, E]), ALU.mult)
                dve.drain()
                for i in range(TILES):
                    dve.max(top[:, i, :], rt_p[:, i, :])
                dve.drain()
                for i in range(TILES):
                    ins = dve.max_index(top_ix[:, i, :], top[:, i, :], rt_p[:, i, :])
                link(ins)
                dve.tensor_reduce(rt_m[:, 3, :], top[:, :, 0:TOPK], AX.X, ALU.add)
                link(dve.tensor_copy(top_f[:, :, :], top_ix[:, :, :]))
                link(dve.tensor_scalar(rt_m[:, 0, :], rt_m[:, 3, :], 1e-20, None, ALU.add))
                dve.reciprocal(rt_m[:, 1, :], rt_m[:, 0, :])
                four = [P, TILES, TOPK, E]
                iota_b = bc(const("iota_e").unsqueeze(1).unsqueeze(1), four)
                link(dve.tensor_tensor(onehot[:, :, :, :], iota_b, bc(top_f[:, :, 0:TOPK].unsqueeze(3), four),
                                       ALU.is_equal))
                dve.tensor_reduce(chosen[:, :, :], onehot[:, :, :, :].rearrange("p i k e -> p i e k"), AX.X,
                                  ALU.add).then_inc(s_cho, 1)
                dve.wait_ge(s_scat, SCAT * b)
                link(dve.tensor_scalar(ids_now[:, :], ids_now[:, :], float(S), None, ALU.add))
                link(dve.tensor_copy(entry[:, :, :, 0], bc(ids_now[:, :].unsqueeze(2), [P, TILES, TOPK])))
                def hidden(i):
                    m = TILES * b + i
                    dve.wait_ge(s_silu, m + 1)
                    dve.tensor_tensor(sh_s[i % 2][:, :], sh_s[i % 2][:, :], bank[1 + 2 * (i % 2)][:, 0:FS],
                                      ALU.mult).then_inc(s_sh, 1)

                if more:
                    store_qT(n1, 0)
                hidden(0)
                hidden(1)
                places = bank[5][:, 0:TILES * E].rearrange("p (i e) -> p i e", e=E)
                dve.wait_ge(s_pos, b + 1)
                dve.tensor_scalar(slot_inv[:, :, :], places, float(CAP), DROPPED, ALU.is_ge, ALU.mult)
                dve.tensor_tensor(slot_e[:, :, :], places, bc(const("e_cap").unsqueeze(1), [P, TILES, E]),
                                  ALU.add).then_inc(s_slots_read, 1)
                link(dve.tensor_reduce(run_add[:, :], chosen[:, :, :].rearrange("p i e -> p e i"), AX.X, ALU.add))
                dve.tensor_tensor(run[:, :], run[:, :], run_add[:, :], ALU.add)
                link(dve.tensor_tensor(slot_e[:, :, :], slot_e[:, :, :], slot_inv[:, :, :], ALU.add))
                link(dve.tensor_tensor(picked[:, :, :, :], onehot[:, :, :, :], bc(slot_e[:, :, :].unsqueeze(2), four),
                                       ALU.mult))
                link(dve.tensor_reduce(slot[:, :, :], picked[:, :, :, :], AX.X, ALU.add))
                dve.tensor_copy(slot_u[:, :], slot[:, :, :].rearrange("p i k -> p (i k)")).then_inc(s_slot, 1)
                if more:
                    store_qT(n1 + 1, 1)

                def store_hT(i):
                    m = TILES * b + i
                    dve.wait_ge(s_sht_mm, m + 1)
                    dve.tensor_copy(sh_hT[:, 0:2, :], bank[4][:, 0:2 * P].rearrange("p (c t) -> p c t", c=2))
                    dve.tensor_copy(sh_hT[0:SHC[2][1], 2, :], bank[4][0:SHC[2][1], 2 * P:3 * P]).then_inc(s_sht, 1)

                def add_shared(i):
                    m = TILES * b + i
                    dve.wait_ge(s_sd, m + 1)
                    if i == 0:
                        dve.wait_ge(s_acc_st, 16 * b)
                    dve.tensor_tensor(acc[:, i, :], bank[5][:, 0:D], x1[:, i, :], ALU.add).then_inc(s_acc, 1)

                store_hT(0)
                hidden(2)
                add_shared(0)
                store_hT(1)
                hidden(3)
                add_shared(1)
                store_hT(2)
                add_shared(2)
                store_hT(3)
                add_shared(3)
                if more:
                    first_maxima(n1)
                link.end()

            def first_maxima(n0):
                maxima(n0, 0)
                maxima(n0 + 1, 1)
                store_qT(n0 + 2, 2)

            keys_first(0)
            store_qT(0, 0)
            keys_second(0)
            store_qT(1, 1)
            first_maxima(0)
            with dve.Fori(0, B - 1) as b:
                units(b)
                finish(b, True)
            units(B - 1)
            finish(B - 1, False)

            cnt, nblk, before, upto, tmp = (bl[:, j, :] for j in range(5))
            link = Links(s_link2, None)
            link.start(0)
            dve.memset(credit[:, 7:8], 0.0).then_inc(s_run, 1)
            dve.wait_ge(s_cnt, 1)
            link(dve.tensor_scalar(cnt, bank[6][:, 0:E], float(CAP), None, ALU.min))
            link(dve.tensor_tensor(bl_gt, bc(cnt.unsqueeze(2), [P, E, CAPB]),
                                   bc(const("j_128").unsqueeze(1), [P, E, CAPB]), ALU.is_gt))
            link(dve.tensor_reduce(nblk, bl_gt, AX.X, ALU.add))
            link(dve.tensor_tensor(bl_tri, bc(nblk.unsqueeze(1), [P, E, E]), tri, ALU.mult))
            link(dve.tensor_reduce(before, bl_tri, AX.X, ALU.add))
            link(dve.tensor_tensor(upto, before, nblk, ALU.add))
            link(dve.tensor_scalar(tmp, upto, const("part"), None, ALU.is_le))
            link(dve.tensor_reduce(bcol[:, 1:2], tmp, AX.X, ALU.add))
            link(dve.tensor_scalar(bcol[:, 0:1], bcol[:, 1:2], float(E - 1), None, ALU.min))
            link(dve.tensor_scalar(tmp, const("iota_e"), bcol[:, 0:1], None, ALU.is_equal))
            link(dve.tensor_tensor(tmp, tmp, before, ALU.mult))
            link(dve.tensor_reduce(bcol[:, 2:3], tmp, AX.X, ALU.add))
            link(dve.tensor_tensor(bcol[:, 3:4], const("part"), bcol[:, 2:3], ALU.subtract))
            link(dve.tensor_scalar(bcol[:, 4:5], bcol[:, 3:4], float(CAPB - 1), None, ALU.min))
            link(dve.scalar_tensor_tensor(out=bcol[:, 5:6], in0=bcol[:, 0:1], scalar=float(CAPB), in1=bcol[:, 4:5],
                                          op0=ALU.mult, op1=ALU.add))
            dve.tensor_copy(row_u[:, :], bcol[:, 5:6]).then_inc(s_row, 1)
            dve.wait_ge(s_bt, 1)
            dve.tensor_copy(exp_i[:, :], bank[7][0:1, 0:P]).then_inc(s_blk, 1)
            dve.wait_ge(s_bt, 2)
            dve.memset(tok_u[:, NBLK:], 0)
            dve.tensor_copy(tok_u[:, 0:NBLK], bank[5][:, 0:P])
            dve.tensor_copy(slot_w[:, :], bank[5][:, P:2 * P]).then_inc(s_blk, 1)

            def block_xT(m, u):
                dve.wait_ge(s_mx_mm, m + 1)
                dve.tensor_copy(xgT[u], bank[u][:, 0:D]).then_inc(s_mxT, 1)

            def block_hidden(m, u):
                dve.wait_ge(s_msilu, m + 1)
                dve.tensor_tensor(hid[u], silu_g[u], bank[2 + u][:, F:2 * F], ALU.mult).then_inc(s_mh, 1)

            def block_hT(m, u):
                dve.wait_ge(s_mht_mm, m + 1)
                dve.tensor_copy(hidT[u], bank[4 + u][0:FH, 0:2 * P]).then_inc(s_mhT, 1)

            block_xT(0, 0)
            block_xT(1, 1)
            block_hidden(0, 0)
            with dve.Fori(0, NBLK // 2 - 1) as it:
                for u in range(2):
                    m = 2 * it + u
                    block_xT(m + 2, u)
                    block_hT(m, u)
                    block_hidden(m + 1, 1 - u)
            block_hT(NBLK - 2, 0)
            block_hidden(NBLK - 1, 1)
            block_hT(NBLK - 1, 1)

            link = Links(s_link3, None)
            link.start(0)

            def statistics(q):
                dve.wait_ge(s_sum, q + 1)
                for i in range(TILES):
                    ins = dve.bn_stats(bn6[:, i, :], sums[q][0][:, i, :])
                link(ins)
                for i in range(TILES):
                    ins = dve.bn_aggr(out_mv[:, q, i, :], bn6[:, i, :])
                link(ins)
                dve.tensor_scalar(out_s[:, q, 0, :], out_mv[:, q, :, 1], EPS_LN, None, ALU.add).then_inc(s_cvar, 1)

            def rows_out(q):
                dve.wait_ge(s_cstd, q + 1)
                link(dve.reciprocal(out_s[:, q, 2, :], out_s[:, q, 1, :]))
                for i in range(TILES):
                    ins = dve.tensor_scalar(sums[q][0][:, i, :], sums[q][0][:, i, :], out_mv[:, q, i, 0:1],
                                            out_s[:, q, 2, i:i + 1], ALU.subtract, ALU.mult)
                ins.then_inc(s_cout, 1)

            for q in range(B):
                statistics(q)
                if q > 0:
                    rows_out(q - 1)
            rows_out(B - 1)

        @block.gpsimd
        def _(pool):
            pool.wait_ge(s_const, 16)

            def rotate(n, b, i):
                s = i % 2
                c = bc2(cos2[:, i % TILES, :])
                q = q_raw[s]
                pool.wait_ge(s_rope, n)
                pool.wait_ge(s_qcopy, n + 1)
                pool.tensor_tensor(rope_a[:, :, :], q[:, :, 0:ROPE], c, ALU.mult)
                pool.tensor_tensor(rope_b[:, :, :], q[:, :, 0:ROPE], bc2(sin2[:, i % TILES, :]), ALU.mult).then_inc(s_rope_c, 1)
                pool.wait_ge(s_rope_c, n + 1)
                pool.tensor_tensor(q[:, :, 0:HALF], rope_a[:, :, 0:HALF], rope_b[:, :, HALF:ROPE], ALU.subtract)
                pool.tensor_tensor(q[:, :, HALF:ROPE], rope_a[:, :, HALF:ROPE], rope_b[:, :, 0:HALF], ALU.add).then_inc(s_rope, 1)

            def bc2(ap):
                return ap.unsqueeze(1).broadcast_to([P, 2, ROPE])

            def scatter(b):
                pool.wait_ge(s_slot, b + 1)
                pool.tensor_tensor(entry[:, :, :, 1], top[:, :, 0:TOPK],
                                   rt_m[:, 1, :].unsqueeze(2).broadcast_to([P, TILES, TOPK]), ALU.mult)
                pool.drain()
                for i in range(TILES):
                    for k in range(TOPK):
                        c = i * TOPK + k
                        pool.indirect_dma_start(table_dram, bass.IndirectOffsetOnAxis(slot_u[:, c:c + 1], 0),
                                                entry[:, i, k, :], None, bounds_check=E * CAP - 1,
                                                oob_is_err=False).then_inc(s_scat, 16)

            def units(b):
                with pool.Fori(0, PAIRS - 1) as p:
                    for i in range(TILES):
                        rotate(UNITS * b + TILES * p + i + 4, b, i)

            pool.wait_ge(s_table0, 16)
            for i in range(TILES):
                rotate(i, 0, i)
            with pool.Fori(0, B - 1) as b:
                units(b)
                for i in range(TILES):
                    rotate(UNITS * (b + 1) + i, b + 1, i)
                scatter(b)
            units(B - 1)
            scatter(B - 1)

            pool.wait_ge(s_row, 1)
            pool.wait_ge(s_scat, SCAT * B)
            pool.indirect_dma_start(rows[:, :, :].rearrange("p c a -> p (c a)"), None,
                                    table_dram.rearrange("(r c) a -> r (c a)", c=P),
                                    bass.IndirectOffsetOnAxis(row_u[:, 0:1], 0)).then_inc(s_rows, 16)
            pool.wait_ge(s_x1_st, 16 * B)
            pool.wait_ge(s_acc_st, 16 * B)
            pool.wait_ge(s_spare, 48)
            pool.wait_ge(s_blk, 2)

            def gather(m, index):
                pool.indirect_dma_start(xg[m % 4], None, x1_dram,
                                        bass.IndirectOffsetOnAxis(index, 0)).then_inc(s_g[m % 4], 16)

            pool.tensor_copy(first_ix[:, :], tok_u[:, 0:AHEAD])
            pool.tensor_copy(block_ix[:, 7, :], tok_u[:, 0:AHEAD + 1:AHEAD]).then_inc(s_ix, 1)
            pool.wait_ge(s_ix, 1)
            for m in range(AHEAD):
                if m >= 4:
                    pool.wait_ge(s_mx_mm, m - 3)
                gather(m, first_ix[:, m:m + 1])

            def block_turn(it, r, left):
                m = 8 * it + r
                pool.wait_ge(s_my, m + 2)
                pool.wait_ge(s_add[r % 2], 64 * it + 16 * (r // 2))
                pool.wait_ge(s_ix, m + 1)
                pool.tensor_copy(block_ix[:, r, :], tok_u[:, bass.ds(m + 1, 2, AHEAD)]).then_inc(s_ix, 1)
                now = (r - 1) % 8
                if left > AHEAD:
                    gather(r + AHEAD, block_ix[:, now, 1:2])
                pool.indirect_dma_start(sum_dram[r % 2], bass.IndirectOffsetOnAxis(block_ix[:, now, 0:1], 0),
                                        y_out[r % 4], None, compute_op=ALU.add).then_inc(s_add[r % 2], 16)

            with pool.Fori(0, NBLK // 8 - 1) as it:
                for r in range(8):
                    block_turn(it, r, NBLK)
            for r in range(8):
                block_turn(NBLK // 8 - 1, r, 8 - r)

            for q in range(B):
                pool.wait_ge(s_cld[q], 32)
                pool.tensor_tensor(sums[q][0], sums[q][0], sums[q][1], ALU.add).then_inc(s_sum, 1)


_INS = ["L0_attn_x", "L0_attn_wq", "L0_attn_wkv_a", "L0_attn_wkv_b", "L0_attn_wo", "L0_attn_kv_norm_w",
        "L0_ffn_wg_router", "L0_ffn_w_gate", "L0_ffn_w_up", "L0_ffn_w_down", "L0_ffn_ws_gate", "L0_ffn_ws_up",
        "L0_ffn_ws_down"]


def shape_constants():
    import numpy as np

    freqs = 1.0 / 10000.0 ** (np.arange(0, ROPE, 2, dtype=np.float32) / ROPE)
    ang = np.outer(np.arange(S, dtype=np.float32), freqs)
    p = np.arange(P)

    def rope(t):
        t = t.reshape(TILES, P, HALF).transpose(1, 0, 2)
        return np.concatenate([t, t], axis=2).reshape(P, TILES * ROPE)

    def rows(v):
        return np.broadcast_to(v, (P, v.size))

    e = np.arange(E)
    parts = {
        "ident": np.eye(P),
        "mask": np.where(p[None, :] > p[:, None], -1e30, 0.0),
        "before": (p[:, None] < p[None, :]),
        "ones": np.ones((P, P)),
        "cos2": rope(np.cos(ang)),
        "sin2": rope(np.sin(ang)),
        "iota_e": rows(e),
        "e_cap": rows(e * CAP),
        "j_128": rows(np.arange(CAPB) * P),
        "part": p[:, None],
        "ids": p[:, None] + P * np.arange(TILES)[None, :] - S,
        "seq_len": np.full((P, TILES), S),
        "tri": rows((e[None, :] < e[:, None]).reshape(-1)),
    }
    return np.concatenate([parts[k].astype(np.float32) for k in CONSTS], axis=1)


def kernel(**inputs):
    import numpy as np
    import concourse.bacc as bacc
    from concourse.bass_utils import run_bass_kernel_spmd

    nc = bacc.Bacc("TRN2", target_bir_lowering=False, num_devices=1)
    arrays, args = {}, []
    for name in _INS:
        arrays[name] = np.ascontiguousarray(inputs[name])
    arrays["shape_constants"] = np.ascontiguousarray(shape_constants())
    empty = np.zeros((E * CAP, 2), np.float32)
    empty[:, 0] = B * S + np.arange(E * CAP) % P
    arrays["empty_table"] = empty
    for name, a in arrays.items():
        args.append(nc.dram_tensor(name, a.shape, mybir.dt.from_np(a.dtype), kind="ExternalInput").ap())
    out = nc.dram_tensor("out", (B, S, D), F32, kind="ExternalOutput").ap()
    layer_kernel(nc, *args, out)
    r = run_bass_kernel_spmd(nc, [arrays], core_ids=[0])
    return r.results[0]["out"]
```

```python
from contextlib import ExitStack

import concourse.bass as bass
from concourse import mybir

F32 = mybir.dt.float32
F32R = mybir.dt.float32r
BF16 = mybir.dt.bfloat16
U32 = mybir.dt.uint32
I32 = mybir.dt.int32
ALU = mybir.AluOpType
ACT = mybir.ActivationFunctionType
AX = mybir.AxisListType

P = 128
B, S, D = 4, 512, 256
H, NOPE, ROPE, LAT, VDIM = 16, 128, 64, 64, 128
QK = NOPE + ROPE
SCALE = float(QK) ** -0.5
HALF = ROPE // 2
KD = D // P
TILES = S // P
PAIRS = H // 2
UNITS = PAIRS * TILES
E, TOPK, F = 32, 6, 176
FS = 2 * F
FH = F // 2
CAP = 2 * (B * S * TOPK // E)
CAPB = CAP // P
NBLK = 128
WCOLS = KD * 2 * F + 2 * D
ROWS = B * S + P
DROPPED = float(1 << 20)
EPS_RMS, EPS_LN = 1e-6, 1e-5
STAGE_EXPERTS = 14
HEAD_EXPERTS = 8
AHEAD = 6
ACT_TILES = TILES // 2
LATE_EXPERTS = 28
GROUP = 2
SHC = [(0, 128), (128, 128), (256, 96)]

SPLIT_AT = STAGE_EXPERTS * WCOLS

CONSTS = {}


def const_layout():
    at = 0
    for name, n in (("ident", P), ("mask", P), ("before", P), ("ones", P), ("cos2", TILES * ROPE),
                    ("sin2", TILES * ROPE), ("iota_e", E), ("e_cap", E), ("j_128", CAPB),
                    ("part", 1), ("ids", TILES), ("tri", E * E)):
        CONSTS[name] = (at, n)
        at += n
    return at


NCONST = const_layout()


def layer_kernel(nc, x, wq, wkv_a, wkv_b, wo, kv_w, w_router, w_gate, w_up, w_down, ws_gate, ws_up,
                 ws_down, consts, empty_table, out):
    x1_dram = nc.dram_tensor("x1_rows", (ROWS, D), F32, kind="Internal").ap()
    sum_dram = [nc.dram_tensor(f"sum_rows{u}", (ROWS, D), F32, kind="Internal").ap() for u in range(2)]
    table_dram = nc.dram_tensor("slot_table", (E * CAP, 2), F32, kind="Internal").ap()

    out_rows = out.rearrange("b s d -> (b s) d")

    with ExitStack() as ctx:
        def sb(name, shape, dt=F32):
            return ctx.enter_context(nc.sbuf_tensor(name, shape, dt))

        def sem(name):
            return ctx.enter_context(nc.semaphore(name))

        split_cols = KD * H * P + KD * S + S + 2 * 2 * P
        with ExitStack() as earlier:
            def early(name, shape, dt=F32R):
                return earlier.enter_context(nc.sbuf_tensor(name, shape, dt))

            early("before_split", [P, SPLIT_AT], F32)
            w_query = [early(f"w_query{u}", [P, KD, H * P]) for u in range(2)]
            xT = [early(f"xT{u}", [P, KD, S]) for u in range(2)]
            keyT = [early(f"keyT{u}", [P, S]) for u in range(2)]
            qT = [[early(f"qT{v}{u}", [P, 2, P]) for u in range(2)] for v in range(2)]
        WREG = sb("expert_weights", [P, E * WCOLS])
        at = [0, STAGE_EXPERTS * WCOLS]

        def stage(n, *dims):
            v = WREG[:, at[0]:at[0] + n]
            at[0] += n
            assert at[0] <= at[1]
            names = "abc"[:len(dims)]
            if len(dims) == 1:
                return v
            spec = " ".join(names)
            return v.rearrange(f"p ({spec}) -> p {spec}", **dict(zip(names, dims)))

        wq_nope = stage(H * D, H, D)
        wq_rope = stage(PAIRS * D, PAIRS, D)
        wkvb = stage(2 * H * LAT, 2 * H, LAT)
        wo_raw = stage(2 * H * VDIM, KD, H * VDIM)
        wkva = stage(D, D)
        wo_t = stage(H * D, H, D)
        at[0], at[1] = HEAD_EXPERTS * WCOLS, E * WCOLS
        o_all = stage(TILES * H * LAT, TILES, H * LAT)
        probs = [stage(2 * S, 2, S) for _ in range(2)]
        probsT = [stage(S, TILES, P) for _ in range(2)]
        assert at[0] <= SPLIT_AT
        at[0] = SPLIT_AT + 2 * split_cols
        x_in = stage(TILES * D, TILES, D)
        k_all = stage(TILES * P, TILES, P)
        w_value_out = stage(PAIRS * D, PAIRS, D)
        oT = [stage(PAIRS * P, PAIRS, P) for _ in range(2)]
        rope_a = stage(2 * ROPE, 2, ROPE)
        rope_b = stage(2 * ROPE, 2, ROPE)
        assert at[0] >= LATE_EXPERTS * WCOLS
        acc = stage(TILES * D, TILES, D)
        wsgu = stage(KD * 2 * FS, KD, 2 * FS)
        wsd = stage(len(SHC) * D, len(SHC), D)

        cst = sb("cst", [P, NCONST])

        def const(name, *dims):
            a, n = CONSTS[name]
            v = cst[:, a:a + n]
            if dims:
                v = v.rearrange("p (a b) -> p a b", a=dims[0], b=dims[1])
            return v

        ident = const("ident")
        cos2, sin2 = const("cos2", TILES, ROPE), const("sin2", TILES, ROPE)
        tri = const("tri", E, E)
        ident_bf = sb("ident_bf", [P, P], BF16)
        mask_bf = sb("mask_bf", [P, P], BF16)
        before_bf = sb("before_bf", [P, P], BF16)
        ones_bf = sb("ones_bf", [P, P], BF16)
        kvw = sb("kvw", [P, LAT])
        wkvaT = [sb(f"wkvaT{u}", [P, KD, P], F32R) for u in range(2)]
        wr_raw = sb("wr_raw", [E, D])
        wrT = sb("wrT", [P, KD, E])
        q_raw = [sb(f"q_raw{u}", [P, 2, P]) for u in range(2)]
        kv_raw = sb("kv_raw", [P, TILES, P])
        k_a = sb("k_a", [P, TILES, ROPE])
        k_b = sb("k_b", [P, TILES, ROPE])
        k_c = sb("k_c", [P, TILES, LAT])
        key = sb("key", [P, TILES, P])
        neg_max = [sb(f"neg_max{i}", [P, 2]) for i in range(TILES)]
        row_sum = [sb(f"row_sum{i}", [P, 2]) for i in range(TILES)]
        row_inv = [sb(f"row_inv{i}", [P, 2]) for i in range(TILES)]
        x_res = sb("x_res", [P, TILES, D])
        stat = sb("stat", [P, 8 * TILES])
        bn6 = sb("bn6", [P, TILES, 6])
        mv = sb("mv", [P, TILES, 2])
        ln_s = sb("ln_s", [P, 3, TILES])
        x1 = sb("x1", [P, TILES, D])
        x1T = sb("x1T", [P, KD, S])
        sh_s = [sb(f"sh_s{u}", [P, FS]) for u in range(2)]
        sh_hT = sb("sh_hT", [P, len(SHC), P])
        rt_e = sb("rt_e", [P, TILES, E])
        rt_p = sb("rt_p", [P, TILES, E])
        rt_m = sb("rt_m", [P, 4, TILES])
        top = sb("top", [P, TILES, 8])
        top_ix = sb("top_ix", [P, TILES, 8], U32)
        top_f = sb("top_f", [P, TILES, 8])
        onehot = sb("onehot", [P, TILES, TOPK, E], BF16)
        picked = sb("picked", [P, TILES, TOPK, E])
        chosen = sb("chosen", [P, TILES, E], BF16)
        run = sb("run", [P, E], BF16)
        run_add = sb("run_add", [P, E])
        slot_e = sb("slot_e", [P, TILES, E])
        slot_inv = sb("slot_inv", [P, TILES, E])
        slot = sb("slot", [P, TILES, TOPK])
        slot_u = sb("slot_u", [P, TILES * TOPK], U32)
        ids_now = sb("ids_now", [P, TILES])
        entry = sb("entry", [P, TILES, TOPK, 2])
        bl = sb("bl", [P, 5, E])
        bl_gt = picked[:, 0, :, :].rearrange("p k e -> p (k e)").rearrange("p (e j) -> p e j", j=CAPB)
        bl_tri = x_res[:, :, :].rearrange("p i d -> p (i d)").rearrange("p (a b) -> p a b", b=E)
        bcol = sb("bcol", [P, 8])
        row_u = sb("row_u", [P, 1], U32)
        rows = sb("rows", [P, P, 2])
        exp_i = sb("exp_i", [1, P], I32)
        tok_u = sb("tok_u", [P, NBLK + AHEAD + 2], U32)
        slot_w = sb("slot_w", [P, NBLK])
        first_ix = sb("first_ix", [P, AHEAD], U32)
        block_ix = sb("block_ix", [P, 8, 2], U32)
        xg = [x1[:, r, :] for r in range(4)]
        xgT = [x1T[:, 0, u * D:(u + 1) * D] for u in range(2)]
        hid = [sh_s[u][:, 0:F] for u in range(2)]
        hidT = [kv_raw[0:FH, 2 * u:2 * u + 2, :].rearrange("p a b -> p (a b)") for u in range(2)]
        silu_g = [sh_s[u][:, F:2 * F] for u in range(2)]
        y_out = ([t[:, :, :].rearrange("p i c -> p (i c)") for t in (k_a, k_b)] +
                 [key[:, 2 * u:2 * u + 2, :].rearrange("p i c -> p (i c)") for u in range(2)])
        sums = [[WREG[:, (2 * q + j) * TILES * D:(2 * q + j + 1) * TILES * D].rearrange("p (i d) -> p i d", d=D)
                 for j in range(2)] for q in range(B)]
        out_mv = sb("out_mv", [P, B, TILES, 2])
        out_s = sb("out_s", [P, B, 3, TILES])
        credit = sb("credit", [P, 10])

        bank = [ctx.enter_context(nc.psum_tensor(f"bank{i}", [P, 512], F32)) for i in range(8)]

        s_const = sem("const_loaded")
        s_raw_nope = sem("raw_nope_and_kv_b_loaded")
        s_raw_rope = sem("raw_rope_and_kv_a_loaded")
        s_raw_wo = sem("raw_wo_loaded")
        s_small = sem("small_weights_loaded")
        s_zero = sem("zero_source_ready")
        s_table0 = sem("table_emptied")
        s_bf = sem("bf_consts_ready")
        s_prep_mm = sem("prep_round_in_psum")
        s_split_h = sem("prep_high_parts_stored")
        s_split = sem("prep_both_parts_stored")
        s_prep_even = sem("prep_even_round_stored")
        s_prep_odd = sem("prep_odd_round_stored")
        s_x = sem("x_loaded")
        s_xt_mm = sem("xT_in_psum")
        s_xt_h = sem("xT_high_parts_stored")
        s_xt_l = sem("xT_low_parts_stored")
        s_kv_mm = sem("kv_in_psum")
        s_kv = sem("kv_copied")
        s_ms = sem("kv_mean_square_ready")
        s_rms = sem("kv_rms_ready")
        s_key = sem("key_ready")
        s_key_mm = sem("keyT_in_psum")
        s_keyT_h = sem("keyT_high_part_stored")
        s_keyT = sem("keyT_stored")
        s_proj = sem("q_in_psum")
        s_qcopy = sem("q_copied")
        s_rope = sem("q_rotated")
        s_rope_c = sem("rope_step")
        s_qt_mm = sem("qT_in_psum")
        s_qT_h = sem("qT_high_part_stored")
        s_qT = sem("qT_stored")
        s_score = sem("scores_in_psum")
        s_max = sem("max_ready")
        s_exp = sem("exp_done")
        s_pt0 = sem("probsT0_in_psum")
        s_pt1 = sem("probsT1_in_psum")
        s_pt0s = sem("probsT0_stored")
        s_pt1s = sem("probsT1_stored")
        s_pv = sem("pv_done")
        s_inv = sem("row_inverse_ready")
        s_norm = sem("head_output_stored")
        s_ot_mm = sem("oT_in_psum")
        s_ota = sem("oT_low_stored")
        s_otb = sem("oT_high_stored")
        s_y = sem("attention_y_in_psum")
        s_res = sem("residual_added")
        s_var = sem("ln_variance_ready")
        s_std = sem("ln_std_ready")
        s_x1 = sem("x1_ready")
        s_x1_st = sem("x1_rows_stored")
        s_x1t_mm = sem("x1T_in_psum")
        s_x1t_a = sem("x1T_half0_stored")
        s_x1t_d = sem("x1T_half1_stored")
        s_log = sem("logits_in_psum")
        s_logd = sem("logits_shifted")
        s_rexp = sem("router_exp_ready")
        s_cho = sem("chosen_ready")
        s_pos = sem("places_in_psum")
        s_slot = sem("slots_ready")
        s_scat = sem("ids_scattered")
        s_gu = sem("shared_gate_up_in_psum")
        s_silu = sem("shared_silu_ready")
        s_sh = sem("shared_hidden_ready")
        s_sht_mm = sem("shared_hiddenT_in_psum")
        s_sht = sem("shared_hiddenT_stored")
        s_sd = sem("shared_down_in_psum")
        s_acc = sem("acc_ready")
        s_acc_st = sem("acc_rows_stored")
        s_run = sem("counts_final")
        s_cnt = sem("counts_in_psum")
        s_row = sem("block_rows_ready")
        s_xr = sem("residual_x_loaded")
        s_rows = sem("block_slots_gathered")
        s_bt = sem("block_tables_in_psum")
        s_blk = sem("block_tables_ready")
        s_w = sem("expert_weights_loaded")
        s_g = [sem(f"tokens_gathered{u}") for u in range(4)]
        s_ix = sem("block_indices_copied")
        s_mx_mm = sem("block_xT_in_psum")
        s_mxT = sem("block_xT_stored")
        s_mgu = sem("block_gate_up_in_psum")
        s_msilu = sem("block_silu_ready")
        s_mh = sem("block_hidden_ready")
        s_mht_mm = sem("block_hiddenT_in_psum")
        s_mhT = sem("block_hiddenT_stored")
        s_mdn = sem("block_down_in_psum")
        s_my = sem("block_y_copied")
        s_add = [sem(f"results_added{u}") for u in range(2)]
        s_spare = sem("spare_rows_zeroed")
        s_cld = [sem(f"sums_loaded{q}") for q in range(B)]
        s_sum = sem("sums_ready")
        s_cvar = sem("out_variance_ready")
        s_cstd = sem("out_std_ready")
        s_cbias = sem("out_shift_ready")
        s_cout = sem("out_tiles_ready")
        s_cout_a = sem("out_first_tiles_ready")
        s_cst = sem("out_stored")
        s_slots_read = sem("places_read")
        s_link_key = sem("vector_step_keys")
        s_link = sem("vector_step")
        s_link2 = sem("vector_step_blocks")
        s_link3 = sem("vector_step_combine")

        N_SMALL = 7
        PREP_ROUNDS = 22
        SPLIT_ROUNDS = 9
        EARLY_GROUPS = HEAD_EXPERTS // GROUP + 2
        LOADS = (E // GROUP) * 6
        SCAT = TILES * TOPK * 16
        KEY_LINKS = 5
        LINKS = 15

        w_view = WREG[:, :].rearrange("p (e c) -> p e c", e=E)

        def load_experts(eng, g):
            e0 = g * GROUP
            for k in range(KD):
                for j, w in enumerate((w_gate, w_up)):
                    at0 = k * 2 * F + j * F
                    eng.dma_start(w_view[:, e0:e0 + GROUP, at0:at0 + F],
                                  w[e0:e0 + GROUP, k * P:(k + 1) * P, :].rearrange("e p f -> p e f")).then_inc(s_w, 16)
            for j in range(2):
                at0 = KD * 2 * F + j * D
                eng.dma_start(w_view[0:FH, e0:e0 + GROUP, at0:at0 + D],
                              w_down[e0:e0 + GROUP, j * FH:(j + 1) * FH, :].rearrange("e p d -> p e d")).then_inc(s_w, 16)

        def split_views(r, part):
            wq_ = w_query[part][:, :, :].rearrange("p k (h c) -> p k h c", c=P)
            if r < 4:
                heads = slice(8 * (r % 2), 8 * (r % 2) + 8)
                return [(wq_[:, r // 2, heads, ROPE:P], bank[r][:, :].rearrange("p (h c) -> p h c", c=LAT))]
            if r < 8:
                heads = slice(8 * (r % 2), 8 * (r % 2) + 8)
                return [(wq_[:, (r - 4) // 2, heads, 0:ROPE].rearrange("p h (t j) -> p h j t", t=2),
                         bank[r][:, :].rearrange("p (h j t) -> p h j t", h=8, t=2))]
            kv = bank[0][:, 0:KD * P].rearrange("p (k c) -> p k c", k=KD)
            return [(wkvaT[part][:, :, ROPE:P], kv[:, :, 0:LAT]),
                    (wkvaT[part][:, :, 0:ROPE].rearrange("p k (t j) -> p k j t", t=2),
                     kv[:, :, LAT:P].rearrange("p k (j t) -> p k j t", t=2))]

        block = ctx.enter_context(nc.Block())

        @block.sync
        def _(sp):
            wq_h = wq.rearrange("(h r) d -> h r d", r=QK)
            sp.dma_start(wkvb, wkv_b.rearrange("(h r) c -> r h c", r=P)).then_inc(s_raw_nope, 16)
            sp.dma_start(wq_nope, wq_h[:, 0:NOPE, :].rearrange("h r d -> r h d")).then_inc(s_raw_nope, 16)
            sp.dma_start(cst[:, :], consts).then_inc(s_const, 16)
            for o in range(2):
                sp.dma_start(wq_rope[o * ROPE:(o + 1) * ROPE, :, :],
                             wq.rearrange("(a o r) d -> o r a d", o=2, r=QK)[o, NOPE:QK, :, :]).then_inc(s_raw_rope, 16)
            sp.dma_start(wkva, wkv_a).then_inc(s_raw_rope, 16)
            sp.dma_start(wo_raw, wo.rearrange("(k p) n -> p k n", p=P)).then_inc(s_raw_wo, 16)
            sp.dma_start(kvw[:, :], kv_w.rearrange("(a c) -> a c", a=1).to_broadcast([P, LAT])).then_inc(s_small, 16)
            sp.dma_start(wr_raw[:, :], w_router).then_inc(s_small, 16)
            sp.dma_start(wsgu[:, :, 0:FS], ws_gate.rearrange("(k p) f -> p k f", p=P)).then_inc(s_small, 16)
            sp.dma_start(wsgu[:, :, FS:2 * FS], ws_up.rearrange("(k p) f -> p k f", p=P)).then_inc(s_small, 16)
            for c, (f0, fn) in enumerate(SHC):
                sp.dma_start(wsd[0:fn, c, :], ws_down[f0:f0 + fn, :]).then_inc(s_small, 16)
            sp.dma_start(table_dram, empty_table).then_inc(s_table0, 16)
            sp.wait_ge(s_zero, 1)
            zeros = x1[:, 0:1, :]
            sp.dma_start(x1_dram[B * S:ROWS, :], x1[:, 0, :]).then_inc(s_spare, 16)
            sp.dma_start(sum_dram[0][B * S:ROWS, :], x1[:, 0, :]).then_inc(s_spare, 16)
            sp.dma_start(sum_dram[1].rearrange("(i p) d -> p i d", p=P),
                         zeros.broadcast_to([P, ROWS // P, D])).then_inc(s_spare, 16)

            def load_x(b):
                sp.dma_start(x_in, x[bass.ds(b, 1), :, :].squeeze(0).rearrange("(i p) d -> p i d", p=P)).then_inc(s_x, 16)

            def load_residual(b):
                sp.dma_start(x_res[:, :, :],
                             x[bass.ds(b, 1), :, :].squeeze(0).rearrange("(i p) d -> p i d", p=P)).then_inc(s_xr, 16)

            def store_x1(b):
                sp.wait_ge(s_x1, b + 1)
                sp.dma_start(x1_dram[bass.ds(b * S, S), :].rearrange("(i p) d -> p i d", p=P),
                             x1[:, :, :]).then_inc(s_x1_st, 16)

            def store_acc(b):
                sp.wait_ge(s_acc, TILES * (b + 1))
                sp.dma_start(sum_dram[0][bass.ds(b * S, S), :].rearrange("(i p) d -> p i d", p=P),
                             acc).then_inc(s_acc_st, 16)

            load_x(0)
            sp.wait_ge(s_prep_mm, PREP_ROUNDS)
            sp.wait_ge(s_prep_even, (PREP_ROUNDS - SPLIT_ROUNDS) // 2)
            sp.wait_ge(s_prep_odd, (PREP_ROUNDS - SPLIT_ROUNDS + 1) // 2)
            for g in range(HEAD_EXPERTS // GROUP):
                load_experts(sp, g)
            load_residual(0)
            with sp.Fori(0, B - 1) as b:
                sp.wait_ge(s_xt_mm, 2 * (b + 1))
                load_x(b + 1)
                sp.wait_ge(s_res, TILES * (b + 1))
                load_residual(b + 1)
                store_x1(b)
                store_acc(b)
            sp.wait_ge(s_res, TILES * B)
            for g in range(HEAD_EXPERTS // GROUP, EARLY_GROUPS):
                load_experts(sp, g)
            store_x1(B - 1)
            for g in range(EARLY_GROUPS, LATE_EXPERTS // GROUP):
                load_experts(sp, g)
            store_acc(B - 1)
            sp.wait_ge(s_acc_st, 16 * B)
            for g in range(LATE_EXPERTS // GROUP, E // GROUP):
                load_experts(sp, g)

            for u in range(2):
                sp.wait_ge(s_add[u], 16 * (NBLK // 2))
            sp.wait_ge(s_mdn, NBLK)

            for q in range(B):
                for j in range(2):
                    sp.dma_start(sums[q][j], sum_dram[j][q * S:(q + 1) * S, :].rearrange("(i p) d -> p i d", p=P)).then_inc(s_cld[q], 16)
            for q in range(B):
                sp.wait_ge(s_cout, q + 1)
                sp.wait_ge(s_cout_a, q + 1)
                sp.dma_start(out_rows[q * S:(q + 1) * S, :].rearrange("(i p) d -> p i d", p=P), sums[q][0]).then_inc(s_cst, 16)
            sp.wait_ge(s_cst, 16 * B)
            sp.wait_ge(s_x1_st, 16 * B)
            sp.wait_ge(s_acc_st, 16 * B)
            sp.wait_ge(s_table0, 16)
            sp.wait_ge(s_spare, 48)
            sp.wait_ge(s_scat, SCAT * B)

        @block.tensor
        def _(pe):
            def stored(r):
                if r < SPLIT_ROUNDS:
                    pe.wait_ge(s_split, r + 1)
                else:
                    pe.wait_ge(s_prep_odd if r % 2 else s_prep_even, (r - SPLIT_ROUNDS) // 2 + 1)

            def round_free(r):
                if r >= 8:
                    stored(r - 8)

            PARTS = ((0, 0), (0, 1), (1, 0))

            pe.wait_ge(s_raw_nope, 32)
            for k in range(KD):
                for g in range(2):
                    for j in range(8):
                        h = 8 * g + j
                        mm = pe.matmul(bank[2 * k + g][:, j * LAT:(j + 1) * LAT], wq_nope[:, h, k * P:(k + 1) * P],
                                       wkvb[:, 2 * h, :], start=True, stop=True)
                    mm.then_inc(s_prep_mm, 1)
            pe.wait_ge(s_const, 16)
            pe.wait_ge(s_raw_rope, 48)
            for k in range(KD):
                for g in range(2):
                    for j in range(4):
                        mm = pe.transpose(bank[4 + 2 * k + g][:, j * P:(j + 1) * P],
                                          wq_rope[:, 4 * g + j, k * P:(k + 1) * P], ident)
                    mm.then_inc(s_prep_mm, 1)
            round_free(8)
            for k in range(KD):
                mm = pe.transpose(bank[0][:, k * P:(k + 1) * P], wkva[:, k * P:(k + 1) * P], ident)
            mm.then_inc(s_prep_mm, 1)
            pe.wait_ge(s_raw_wo, 16)
            for r in range(9, 17):
                round_free(r)
                for j in range(2):
                    h = 2 * (r - 9) + j
                    for k in range(KD):
                        mm = pe.transpose(bank[r % 8][:, (2 * j + k) * P:(2 * j + k + 1) * P],
                                          wo_raw[:, k, h * VDIM:(h + 1) * VDIM], ident)
                mm.then_inc(s_prep_mm, 1)
            stored(15)
            stored(16)
            for r in range(17, 21):
                for j in range(2):
                    for o in range(2):
                        h = 4 * (r - 17) + 2 * j + o
                        mm = pe.matmul(bank[r % 8][o * LAT:(o + 1) * LAT, j * D:(j + 1) * D], wkvb[:, 2 * h + 1, :],
                                       wo_t[:, h, :], start=True, stop=True)
                mm.then_inc(s_prep_mm, 1)
            round_free(21)
            pe.wait_ge(s_small, 16 * N_SMALL)
            for k in range(KD):
                mm = pe.transpose(bank[5][:, k * E:(k + 1) * E], wr_raw[:, k * P:(k + 1) * P], ident[0:E, 0:E])
            mm.then_inc(s_prep_mm, 1)
            stored(PREP_ROUNDS - 2)
            stored(PREP_ROUNDS - 1)
            pe.wait_ge(s_bf, 4)

            S_BANK = [(bank[0], bank[1]), (bank[2], bank[3])]
            O_BANK, Q_BANK, QT_BANK = bank[4:6], bank[6], bank[7]

            def project(n, pair, i):
                pe.wait_ge(s_qcopy, n)
                for k in range(KD):
                    for a, c in PARTS:
                        mm = pe.matmul(Q_BANK[:, 0:2 * P], xT[a][:, k, i * P:(i + 1) * P],
                                       w_query[c][:, k, bass.ds(pair * 2 * P, 2 * P)],
                                       start=(k == 0 and a + c == 0), stop=(k == KD - 1 and a == 1))
                mm.then_inc(s_proj, 1)

            def turn_query(n, slot_):
                pe.wait_ge(s_rope, n + 1)
                pe.wait_ge(s_qT, n)
                for h in range(2):
                    mm = pe.transpose(QT_BANK[:, h * P:(h + 1) * P], q_raw[slot_][:, h, :], ident)
                mm.then_inc(s_qt_mm, 1)

            def scores(n, i):
                u = i % 2
                keys = (i + 1) * P
                pe.wait_ge(s_qT, n + 1)
                pe.wait_ge(s_pt0s, n)
                pe.wait_ge(s_pt1s, n)
                for h in range(2):
                    for a, c in PARTS:
                        pe.matmul(S_BANK[u][h][:, 0:keys], qT[u][a][:, h, :], keyT[c][:, 0:keys],
                                  start=(a + c == 0), stop=False)
                    mm = pe.matmul(S_BANK[u][h][:, i * P:keys], ident_bf[:, :], mask_bf[:, :], start=False, stop=True)
                    mm.then_inc(s_score, 1)

            def turn_probs(n, i, h):
                pe.wait_ge(s_exp, 2 * n + h + 1)
                for j in range(i + 1):
                    mm = pe.transpose(S_BANK[i % 2][h][:, j * P:(j + 1) * P], probs[i % 2][:, h, j * P:(j + 1) * P], ident)
                mm.then_inc(s_pt1 if h else s_pt0, 1)

            def values(n, i, h):
                if h == 0:
                    pe.wait_ge(s_norm, n)
                    pe.wait_ge(s_pt0s, n + 2)
                else:
                    pe.wait_ge(s_pt1s, n + 2)
                for j in range(i + 1):
                    mm = pe.matmul(O_BANK[i % 2][:, h * LAT:(h + 1) * LAT], probsT[h][:, j, :], k_all[:, j, ROPE:P],
                                   start=(j == 0), stop=(j == i))
                if h == 1:
                    mm.then_inc(s_pv, 1)

            def step(b, p, i, first_local):
                n = UNITS * b + TILES * p + i
                last = first_local + i
                turn_probs(n, i, 0)
                turn_probs(n, i, 1)
                if last + 4 < UNITS:
                    project(n + 4, p + 1, i)
                if last + 3 < UNITS:
                    turn_query(n + 3, (i + 3) % 2)
                if last + 2 < UNITS:
                    scores(n + 2, (i + 2) % TILES)
                values(n, i, 0)
                values(n, i, 1)

            def turn_x():
                for k in range(KD):
                    for i in range(TILES):
                        mm = pe.transpose(bank[6 + k][:, i * P:(i + 1) * P], x_in[:, i, k * P:(k + 1) * P], ident)
                    mm.then_inc(s_xt_mm, 1)

            def project_kv(b):
                pe.wait_ge(s_xt_h, KD * (b + 1))
                pe.wait_ge(s_xt_l, KD * (b + 1))
                pe.wait_ge(s_res, TILES * b)
                for i in range(TILES):
                    for k in range(KD):
                        for a, c in PARTS:
                            mm = pe.matmul(bank[4][:, i * P:(i + 1) * P], xT[a][:, k, i * P:(i + 1) * P],
                                           wkvaT[c][:, k, :], start=(k == 0 and a + c == 0),
                                           stop=(k == KD - 1 and a == 1))
                mm.then_inc(s_kv_mm, 1)

            def turn_key(b):
                pe.wait_ge(s_key, b + 1)
                for i in range(TILES):
                    mm = pe.transpose(bank[4][:, i * P:(i + 1) * P], key[:, i, :], ident)
                mm.then_inc(s_key_mm, 1)

            def first_queries(n0):
                project(n0, 0, 0)
                project(n0 + 1, 0, 1)

            def more_queries(n0):
                turn_query(n0, 0)
                project(n0 + 2, 0, 2)
                turn_query(n0 + 1, 1)
                project(n0 + 3, 0, 3)

            def first_scores(b):
                n0 = UNITS * b
                pe.wait_ge(s_keyT, b + 1)
                scores(n0, 0)
                scores(n0 + 1, 1)
                turn_query(n0 + 2, 0)

            def units(b):
                with pe.Fori(0, PAIRS - 1) as p:
                    for i in range(TILES):
                        step(b, p, i, 0)
                for i in range(TILES):
                    step(b, PAIRS - 1, i, UNITS - TILES)

            def turn_out(b, i):
                m = TILES * b + i
                u = i % 2
                if i >= 2:
                    pe.wait_ge(s_ota, m - 1)
                    pe.wait_ge(s_otb, m - 1)
                for kk in range(PAIRS):
                    mm = pe.transpose(bank[2 * u + kk // 4][:, (kk % 4) * P:(kk % 4 + 1) * P],
                                      o_all[:, i, kk * P:(kk + 1) * P], ident)
                    if kk % 4 == 3:
                        mm.then_inc(s_ot_mm, 1)

            def project_out(b, i):
                m = TILES * b + i
                pe.wait_ge(s_ota, m + 1)
                pe.wait_ge(s_otb, m + 1)
                if i >= 2:
                    pe.wait_ge(s_res, m - 1)
                for kk in range(PAIRS):
                    mm = pe.matmul(bank[4 + i % 2][:, 0:D], oT[i % 2][:, kk, :], w_value_out[:, kk, :],
                                   start=(kk == 0), stop=(kk == PAIRS - 1))
                mm.then_inc(s_y, 1)

            def gate_up(b, i):
                m = TILES * b + i
                if i >= 2:
                    pe.wait_ge(s_sh, m - 1)
                for half in range(2):
                    for k in range(KD):
                        mm = pe.matmul(bank[2 * (i % 2) + half][:, 0:FS], x1T[:, k, i * P:(i + 1) * P],
                                       wsgu[:, k, half * FS:(half + 1) * FS], start=(k == 0), stop=(k == KD - 1))
                mm.then_inc(s_gu, 1)

            def turn_hidden(b, i):
                m = TILES * b + i
                pe.wait_ge(s_sh, m + 1)
                pe.wait_ge(s_sht, m)
                for c, (f0, fn) in enumerate(SHC):
                    mm = pe.transpose(bank[4][0:fn, c * P:(c + 1) * P], sh_s[i % 2][:, f0:f0 + fn], ident)
                mm.then_inc(s_sht_mm, 1)

            def down(b, i):
                m = TILES * b + i
                pe.wait_ge(s_sht, m + 1)
                pe.wait_ge(s_acc, m)
                for c, (f0, fn) in enumerate(SHC):
                    mm = pe.matmul(bank[5][:, 0:D], sh_hT[0:fn, c, :], wsd[0:fn, c, :],
                                   start=(c == 0), stop=(c == len(SHC) - 1))
                mm.then_inc(s_sd, 1)

            def finish(b, more):
                n1 = UNITS * (b + 1)
                pe.wait_ge(s_norm, UNITS * (b + 1) + 1)
                turn_out(b, 0)
                turn_out(b, 1)
                if more:
                    pe.wait_ge(s_x, 16 * (b + 2))
                    turn_x()
                project_out(b, 0)
                turn_out(b, 2)
                project_out(b, 1)
                turn_out(b, 3)
                project_out(b, 2)
                project_out(b, 3)
                if more:
                    project_kv(b + 1)
                    first_queries(n1)
                pe.wait_ge(s_x1, b + 1)
                for k in range(KD):
                    for i in range(TILES):
                        mm = pe.transpose(bank[k][:, i * P:(i + 1) * P], x1[:, i, k * P:(k + 1) * P], ident)
                    mm.then_inc(s_x1t_mm, 1)
                if more:
                    turn_query(n1, 0)
                    project(n1 + 2, 0, 2)
                pe.wait_ge(s_x1t_a, b + 1)
                pe.wait_ge(s_x1t_d, b + 1)
                for i in range(TILES):
                    for k in range(KD):
                        mm = pe.matmul(bank[5][:, i * E:(i + 1) * E], x1T[:, k, i * P:(i + 1) * P], wrT[:, k, :],
                                       start=(k == 0), stop=(k == KD - 1))
                mm.then_inc(s_log, 1)
                gate_up(b, 0)
                if more:
                    gate_up(b, 1)
                    turn_query(n1 + 1, 1)
                    project(n1 + 3, 0, 3)
                    turn_key(b + 1)
                pe.wait_ge(s_cho, b + 1)
                o = bank[5][:, 0:TILES * E].rearrange("p (i e) -> p i e", e=E)
                pe.matmul(o, ones_bf[:, :], run[:, :].unsqueeze(1).broadcast_to([P, TILES, E]), start=True, stop=False)
                for j in range(TILES - 1):
                    later = TILES - 1 - j
                    pe.matmul(o[:, j + 1:, :], ones_bf[:, :],
                              chosen[:, j, :].unsqueeze(1).broadcast_to([P, later, E]), start=False, stop=False)
                mm = pe.matmul(o, before_bf[:, :], chosen[:, :, :], start=False, stop=True)
                mm.then_inc(s_pos, 1)
                if more:
                    pe.wait_ge(s_keyT, b + 2)
                else:
                    gate_up(b, 1)
                turn_hidden(b, 0)
                gate_up(b, 2)
                pe.wait_ge(s_slots_read, b + 1)
                if not more:
                    pe.wait_ge(s_run, 1)
                    pe.matmul(bank[6][:, 0:E], ones_bf[:, :], run[:, :], start=True, stop=True).then_inc(s_cnt, 1)
                down(b, 0)
                turn_hidden(b, 1)
                gate_up(b, 3)
                down(b, 1)
                turn_hidden(b, 2)
                if more:
                    pe.wait_ge(s_sh, TILES * (b + 1) - 1)
                    scores(n1, 0)
                down(b, 2)
                turn_hidden(b, 3)
                if more:
                    scores(n1 + 1, 1)
                down(b, 3)
                if more:
                    turn_query(n1 + 2, 0)
                    pe.wait_ge(s_acc, TILES * (b + 1))

            pe.wait_ge(s_x, 16)
            turn_x()
            project_kv(0)
            first_queries(0)
            more_queries(0)
            turn_key(0)
            first_scores(0)
            with pe.Fori(0, B - 1) as b:
                units(b)
                finish(b, True)
            units(B - 1)
            finish(B - 1, False)

            pe.wait_ge(s_row, 1)
            pe.matmul(bank[7][0:1, 0:P], bcol[:, 0:1], ident, start=True, stop=True).then_inc(s_bt, 1)
            pe.wait_ge(s_acc, TILES * B)
            pe.wait_ge(s_rows, 16)
            for j in range(2):
                mm = pe.transpose(bank[5][:, j * P:(j + 1) * P], rows[:, :, j], ident)
            mm.then_inc(s_bt, 1)

            XT_B, GU_B, HT_B, Y_B = bank[0:2], bank[2:4], bank[4:6], bank[6:8]

            def block_xT(m, turn, r):
                u = r % 2
                pe.wait_ge(s_g[r], 16 * (turn + 1))
                pe.wait_ge(s_mxT, m)
                for k in range(KD):
                    mm = pe.transpose(XT_B[u][:, k * P:(k + 1) * P], xg[r][:, k * P:(k + 1) * P], ident)
                mm.then_inc(s_mx_mm, 1)

            def block_expert(m):
                return pe.value_load(exp_i[0:1, bass.ds(m, 1)], min_val=0, max_val=E - 1)

            def block_gate_up(m, u, e):
                pe.wait_ge(s_mxT, m + 2)
                pe.wait_ge(s_mh, m)
                for k in range(KD):
                    mm = pe.matmul(GU_B[u][:, 0:2 * F], xgT[u][:, k * P:(k + 1) * P],
                                   WREG[:, bass.ds(e * WCOLS + k * 2 * F, 2 * F)], start=(k == 0), stop=(k == KD - 1))
                mm.then_inc(s_mgu, 1)

            def block_hT(m, u):
                pe.wait_ge(s_mh, m + 2)
                pe.wait_ge(s_mhT, m)
                for j in range(2):
                    mm = pe.transpose(HT_B[u][0:FH, j * P:(j + 1) * P], hid[u][:, j * FH:(j + 1) * FH], ident)
                mm.then_inc(s_mht_mm, 1)

            def block_down(m, u, e):
                pe.wait_ge(s_mhT, m + 2)
                pe.wait_ge(s_my, m)
                for j in range(2):
                    mm = pe.matmul(Y_B[u][:, 0:D], hidT[u][:, j * P:(j + 1) * P],
                                   WREG[0:FH, bass.ds(e * WCOLS + KD * 2 * F + j * D, D)],
                                   start=(j == 0), stop=(j == 1))
                mm.then_inc(s_mdn, 1)

            pe.wait_ge(s_blk, 2)
            pe.wait_ge(s_w, 16 * LOADS)
            block_xT(0, 0, 0)
            block_xT(1, 0, 1)
            block_gate_up(0, 0, block_expert(0))

            def block_step(it, r, left):
                m = 8 * it + r
                if left > 1:
                    next_expert = block_expert(m + 1)
                if left > 2:
                    block_xT(m + 2, 2 * it + (r + 2) // 4, (r + 2) % 4)
                block_hT(m, r % 2)
                if left > 1:
                    block_gate_up(m + 1, (r + 1) % 2, next_expert)
                block_down(m, r % 2, block_expert(m))

            with pe.Fori(0, NBLK // 8 - 1) as it:
                for r in range(8):
                    block_step(it, r, NBLK)
            for r in range(8):
                block_step(NBLK // 8 - 1, r, 8 - r)

        @block.scalar
        def _(act):
            def prep(r):
                act.wait_ge(s_prep_mm, r + 1)

            for r in range(SPLIT_ROUNDS):
                prep(r)
                for out_, in_ in split_views(r, 0):
                    ins = act.copy(out_, in_)
                ins.then_inc(s_split_h, 1)
            for r in (10, 12, 14, 16):
                prep(r)
                act.copy(wo_t[:, 2 * (r - 9):2 * (r - 9) + 2, :],
                         bank[r % 8][:, :].rearrange("p (j d) -> p j d", j=2)).then_inc(s_prep_even, 1)
            for r in (18, 20):
                prep(r)
                act.copy(w_value_out[:, 2 * (r - 17):2 * (r - 17) + 2, :],
                         bank[r % 8][:, :].rearrange("p (j d) -> p j d", j=2)).then_inc(s_prep_even, 1)

            def copy_query(n, i):
                act.wait_ge(s_proj, n + 1)
                act.copy(q_raw[i % 2][:, :, :], bank[6][:, 0:2 * P].rearrange("p (h c) -> p h c", h=2)).then_inc(s_qcopy, 1)

            def exps(n, i):
                u = i % 2
                for h in range(2):
                    act.wait_ge(s_max, 2 * n + h + 1)
                    act.activation(probs[u][:, h, 0:(i + 1) * P], bank[2 * u + h][:, 0:(i + 1) * P], ACT.Exp,
                                   bias=neg_max[i][:, h:h + 1], scale=1.0,
                                   accum_out=row_sum[i][:, h:h + 1]).then_inc(s_exp, 1)

            def step(b, p, i, first_local):
                n = UNITS * b + TILES * p + i
                last = first_local + i
                act.wait_ge(s_pt0, n + 1)
                act.copy(probsT[0][:, 0:i + 1, :],
                         bank[2 * (i % 2)][:, 0:(i + 1) * P].rearrange("p (j t) -> p j t", t=P)).then_inc(s_pt0s, 1)
                if last + 1 < UNITS:
                    exps(n + 1, (i + 1) % TILES)
                if last + 4 < UNITS:
                    copy_query(n + 4, i)

            def turn_x(b):
                for k in range(KD):
                    act.wait_ge(s_xt_mm, KD * b + k + 1)
                    act.copy(xT[0][:, k, :], bank[6 + k][:, :]).then_inc(s_xt_h, 1)

            def copy_kv(b):
                act.wait_ge(s_kv_mm, b + 1)
                act.copy(kv_raw[:, :, :], bank[4][:, :].rearrange("p (i c) -> p i c", c=P)).then_inc(s_kv, 1)

            def key_rms(b):
                act.wait_ge(s_ms, b + 1)
                act.activation(stat[:, 8:12], stat[:, 4:8], ACT.Sqrt).then_inc(s_rms, 1)

            def more_queries(b):
                copy_query(UNITS * b + 2, 2)
                copy_query(UNITS * b + 3, 3)
                act.wait_ge(s_key_mm, b + 1)
                act.copy(keyT[0][:, :], bank[4][:, :]).then_inc(s_keyT_h, 1)

            def units(b):
                with act.Fori(0, PAIRS - 1) as p:
                    for i in range(TILES):
                        step(b, p, i, 0)
                for i in range(TILES):
                    step(b, PAIRS - 1, i, UNITS - TILES)

            def finish(b, more):
                n1 = UNITS * (b + 1)
                for i in range(TILES):
                    act.wait_ge(s_ot_mm, 2 * (TILES * b + i) + 1)
                    act.copy(oT[i % 2][:, 0:4, :],
                             bank[2 * (i % 2)][:, :].rearrange("p (j t) -> p j t", t=P)).then_inc(s_ota, 1)
                    if more and i == 2:
                        turn_x(b + 1)
                act.wait_ge(s_var, b + 1)
                act.activation(ln_s[:, 1, :], ln_s[:, 0, :], ACT.Sqrt).then_inc(s_std, 1)
                if more:
                    copy_kv(b + 1)
                    copy_query(n1, 0)
                    key_rms(b + 1)
                    copy_query(n1 + 1, 1)
                act.wait_ge(s_x1t_mm, 2 * b + 1)
                act.copy(x1T[:, 0, :], bank[0][:, :]).then_inc(s_x1t_a, 1)
                act.wait_ge(s_logd, b + 1)
                act.activation(rt_e[:, :, :], rt_p[:, :, :], ACT.Exp).then_inc(s_rexp, 1)

                def silu(i):
                    m = TILES * b + i
                    act.wait_ge(s_gu, m + 1)
                    act.wait_ge(s_sht_mm, m - 1 if i >= 2 else TILES * b)
                    act.activation(sh_s[i % 2][:, :], bank[2 * (i % 2)][:, 0:FS], ACT.Silu).then_inc(s_silu, 1)

                silu(0)
                silu(1)
                if more:
                    more_queries(b + 1)
                silu(2)
                silu(3)
                if more:
                    exps(n1, 0)

            turn_x(0)
            copy_kv(0)
            copy_query(0, 0)
            copy_query(1, 1)
            key_rms(0)
            more_queries(0)
            exps(0, 0)
            with act.Fori(0, B - 1) as b:
                units(b)
                finish(b, True)
            units(B - 1)
            finish(B - 1, False)

            def block_silu(m, u):
                act.wait_ge(s_mgu, m + 1)
                act.activation(silu_g[u], bank[2 + u][:, 0:F], ACT.Silu).then_inc(s_msilu, 1)

            def block_y(a, r):
                m = 4 * a + r
                act.wait_ge(s_mdn, m + 1)
                if not (isinstance(a, int) and a == 0):
                    act.wait_ge(s_add[r % 2], 32 * a + 16 * (r // 2) - 16)
                act.activation(y_out[r], bank[6 + r % 2][:, 0:D], ACT.Copy,
                               scale=slot_w[:, bass.ds(m, 1)]).then_inc(s_my, 1)

            act.wait_ge(s_blk, 2)
            block_silu(0, 0)
            for r in range(4):
                block_silu(r + 1, (r + 1) % 2)
                block_y(0, r)
            with act.Fori(1, NBLK // 4 - 1) as a:
                for r in range(4):
                    block_silu(4 * a + r + 1, (r + 1) % 2)
                    block_y(a, r)
            for r in range(4):
                if r < 3:
                    block_silu(NBLK - 3 + r, (r + 1) % 2)
                block_y(NBLK // 4 - 1, r)

            def rows_out(q):
                act.wait_ge(s_cbias, q + 1)
                for i in range(ACT_TILES):
                    ins = act.activation(sums[q][0][:, i, :], sums[q][0][:, i, :], ACT.Identity,
                                         bias=out_s[:, q, 0, i:i + 1], scale=out_s[:, q, 2, i:i + 1])
                ins.then_inc(s_cout_a, 1)

            for q in range(B):
                act.wait_ge(s_cvar, q + 1)
                act.activation(out_s[:, q, 1, :], out_s[:, q, 0, :], ACT.Sqrt).then_inc(s_cstd, 1)
                if q > 0:
                    rows_out(q - 1)
            rows_out(B - 1)

        @block.vector
        def _(dve):
            class Links:

                def __init__(self, s, per):
                    self.s, self.per, self.n, self.base = s, per, 0, 0

                def start(self, base):
                    self.n, self.base = 0, base

                def __call__(self, ins):
                    self.n += 1
                    ins.then_inc(self.s, 1)
                    dve.wait_ge(self.s, self.base + self.n)

                def end(self):
                    assert self.per is None or self.n == self.per, self.n

            for j, s in enumerate((s_pt0s, s_pt1s, s_norm, s_mxT, s_mh, s_mhT, s_my)):
                dve.memset(credit[:, j:j + 1], 0.0).then_inc(s, 1)
            dve.memset(x1[:, 0, :], 0.0).then_inc(s_zero, 1)
            dve.memset(run[:, :], 0.0)

            def prep(r):
                dve.wait_ge(s_prep_mm, r + 1)

            for r in range(SPLIT_ROUNDS):
                dve.wait_ge(s_split_h, r + 1)
                for (low, in_), (high, _) in zip(split_views(r, 1), split_views(r, 0)):
                    ins = dve.tensor_tensor(low, in_, high.bitcast(F32), ALU.subtract)
                ins.then_inc(s_split, 1)
            dve.wait_ge(s_const, 16)
            dve.tensor_copy(ident_bf[:, :], ident).then_inc(s_bf, 1)
            dve.tensor_copy(mask_bf[:, :], const("mask")).then_inc(s_bf, 1)
            dve.tensor_copy(before_bf[:, :], const("before")).then_inc(s_bf, 1)
            dve.tensor_copy(ones_bf[:, :], const("ones")).then_inc(s_bf, 1)
            dve.tensor_copy(ids_now[:, :], const("ids"))
            for r in (9, 11, 13, 15):
                prep(r)
                dve.tensor_copy(wo_t[:, 2 * (r - 9):2 * (r - 9) + 2, :],
                                bank[r % 8][:, :].rearrange("p (j d) -> p j d", j=2)).then_inc(s_prep_odd, 1)
            for r in (17, 19):
                prep(r)
                dve.tensor_copy(w_value_out[:, 2 * (r - 17):2 * (r - 17) + 2, :],
                                bank[r % 8][:, :].rearrange("p (j d) -> p j d", j=2)).then_inc(s_prep_odd, 1)
            prep(21)
            dve.tensor_copy(wrT[:, :, :], bank[5][:, 0:KD * E].rearrange("p (k e) -> p k e", k=KD)).then_inc(s_prep_odd, 1)

            link = Links(s_link, LINKS)

            def store_qT(n, i):
                q = bank[7][:, 0:2 * P].rearrange("p (h t) -> p h t", h=2)
                high, low = qT[i % 2]
                dve.wait_ge(s_qt_mm, n + 1)
                dve.tensor_copy(high[:, :, :], q).then_inc(s_qT_h, 1)
                dve.wait_ge(s_qT_h, n + 1)
                dve.tensor_tensor(low[:, :, :], q, high[:, :, :].bitcast(F32), ALU.subtract).then_inc(s_qT, 1)

            def store_keyT(b):
                dve.wait_ge(s_keyT_h, b + 1)
                dve.tensor_tensor(keyT[1][:, :], bank[4][:, :], keyT[0][:, :].bitcast(F32), ALU.subtract).then_inc(s_keyT, 1)

            def maxima(n, i):
                u = i % 2
                for h in range(2):
                    dve.wait_ge(s_score, 2 * n + h + 1)
                    dve.tensor_reduce(neg_max[i][:, h:h + 1], bank[2 * u + h][:, 0:(i + 1) * P], AX.X, ALU.max,
                                      negate=True).then_inc(s_max, 1)

            def normalise(b, p, i):
                n = UNITS * b + TILES * p + i
                dve.wait_ge(s_pv, n + 1)
                dve.reciprocal(row_inv[i][:, :], row_sum[i][:, :]).then_inc(s_inv, 1)
                dve.wait_ge(s_inv, n + 1)
                dve.tensor_tensor(o_all[:, i, bass.ds(p * 2 * LAT, 2 * LAT)].rearrange("p (h c) -> p h c", h=2),
                                  bank[4 + i % 2][:, 0:2 * LAT].rearrange("p (h c) -> p h c", h=2),
                                  row_inv[i][:, :].unsqueeze(2).broadcast_to([P, 2, LAT]), ALU.mult).then_inc(s_norm, 1)

            def step(b, p, i, first_local):
                n = UNITS * b + TILES * p + i
                last = first_local + i
                dve.wait_ge(s_pt1, n + 1)
                dve.tensor_copy(probsT[1][:, 0:i + 1, :],
                                bank[2 * (i % 2) + 1][:, 0:(i + 1) * P].rearrange("p (j t) -> p j t", t=P)).then_inc(s_pt1s, 1)
                if last + 3 < UNITS:
                    store_qT(n + 3, i + 3)
                if last + 2 < UNITS:
                    maxima(n + 2, (i + 2) % TILES)

            def bc(ap, shape):
                return ap.broadcast_to(shape)

            key_link = Links(s_link_key, KEY_LINKS)

            def low_xT(b):
                for k in range(KD):
                    dve.wait_ge(s_xt_h, KD * b + k + 1)
                    dve.tensor_tensor(xT[1][:, k, :], bank[6 + k][:, :], xT[0][:, k, :].bitcast(F32),
                                      ALU.subtract).then_inc(s_xt_l, 1)

            def keys_first(b):
                key_link.start(b * KEY_LINKS)
                dve.wait_ge(s_kv, b + 1)
                dve.tensor_tensor(k_a[:, :, :], kv_raw[:, :, 0:ROPE], cos2, ALU.mult)
                dve.tensor_tensor(k_b[:, :, :], kv_raw[:, :, 0:ROPE], sin2, ALU.mult)
                key_link(dve.tensor_tensor(k_c[:, :, :], kv_raw[:, :, ROPE:P], kv_raw[:, :, ROPE:P], ALU.mult))
                dve.tensor_tensor(k_all[:, :, 0:HALF], k_a[:, :, 0:HALF], k_b[:, :, HALF:ROPE], ALU.subtract)
                dve.tensor_tensor(k_all[:, :, HALF:ROPE], k_a[:, :, HALF:ROPE], k_b[:, :, 0:HALF], ALU.add)
                key_link(dve.tensor_reduce(stat[:, 0:4], k_c[:, :, :], AX.X, ALU.add))
                dve.tensor_scalar(stat[:, 4:8], stat[:, 0:4], 1.0 / LAT, EPS_RMS, ALU.mult, ALU.add).then_inc(s_ms, 1)

            def keys_second(b):
                dve.wait_ge(s_rms, b + 1)
                key_link(dve.reciprocal(stat[:, 12:16], stat[:, 8:12]))
                key_link(dve.tensor_tensor(k_c[:, :, :], kv_raw[:, :, ROPE:P],
                                           bc(stat[:, 12:16].unsqueeze(2), [P, TILES, LAT]), ALU.mult))
                key_link(dve.tensor_tensor(k_all[:, :, ROPE:P], k_c[:, :, :],
                                           bc(kvw[:, :].unsqueeze(1), [P, TILES, LAT]), ALU.mult))
                dve.tensor_scalar(key[:, :, :], k_all, SCALE, None, ALU.mult).then_inc(s_key, 1)
                key_link.end()

            def pair(b, p, first_local):
                for i in range(TILES):
                    step(b, p, i, first_local)
                    if i < TILES - 1:
                        normalise(b, p, i)

            def units(b):
                pair(b, 0, 0)
                with dve.Fori(0, PAIRS - 2) as p:
                    normalise(b, p, TILES - 1)
                    pair(b, p + 1, 0)
                normalise(b, PAIRS - 2, TILES - 1)
                pair(b, PAIRS - 1, UNITS - TILES)
                normalise(b, PAIRS - 1, TILES - 1)

            cnt, nblk, before, upto, tmp = (bl[:, j, :] for j in range(5))
            table_link = Links(s_link2, None)

            def count_blocks():
                table_link.start(0)
                dve.wait_ge(s_cnt, 1)
                table_link(dve.tensor_scalar(cnt, bank[6][:, 0:E], float(CAP), None, ALU.min))
                table_link(dve.tensor_tensor(bl_gt, bc(cnt.unsqueeze(2), [P, E, CAPB]),
                                             bc(const("j_128").unsqueeze(1), [P, E, CAPB]), ALU.is_gt))
                table_link(dve.tensor_reduce(nblk, bl_gt, AX.X, ALU.add))

            def blocks_before():
                table_link(dve.tensor_tensor(bl_tri, bc(nblk.unsqueeze(1), [P, E, E]), tri, ALU.mult))
                table_link(dve.tensor_reduce(before, bl_tri, AX.X, ALU.add))
                table_link(dve.tensor_tensor(upto, before, nblk, ALU.add))

            def block_experts():
                table_link(dve.tensor_scalar(tmp, upto, const("part"), None, ALU.is_le))
                table_link(dve.tensor_reduce(bcol[:, 1:2], tmp, AX.X, ALU.add))
                table_link(dve.tensor_scalar(bcol[:, 0:1], bcol[:, 1:2], float(E - 1), None, ALU.min))
                table_link(dve.tensor_scalar(tmp, const("iota_e"), bcol[:, 0:1], None, ALU.is_equal))

            def block_rows():
                table_link(dve.tensor_tensor(tmp, tmp, before, ALU.mult))
                table_link(dve.tensor_reduce(bcol[:, 2:3], tmp, AX.X, ALU.add))
                table_link(dve.tensor_tensor(bcol[:, 3:4], const("part"), bcol[:, 2:3], ALU.subtract))
                table_link(dve.tensor_scalar(bcol[:, 4:5], bcol[:, 3:4], float(CAPB - 1), None, ALU.min))
                table_link(dve.scalar_tensor_tensor(out=bcol[:, 5:6], in0=bcol[:, 0:1], scalar=float(CAPB),
                                                    in1=bcol[:, 4:5], op0=ALU.mult, op1=ALU.add))
                dve.tensor_copy(row_u[:, :], bcol[:, 5:6]).then_inc(s_row, 1)

            def finish(b, more):
                n1 = UNITS * (b + 1)
                link.start(b * LINKS)

                def store_oT(i):
                    dve.wait_ge(s_ot_mm, 2 * (TILES * b + i) + 2)
                    dve.tensor_copy(oT[i % 2][:, 4:8, :],
                                    bank[2 * (i % 2) + 1][:, :].rearrange("p (j t) -> p j t", t=P)).then_inc(s_otb, 1)

                def residual(i):
                    dve.wait_ge(s_y, TILES * b + i + 1)
                    if i == 0:
                        dve.wait_ge(s_x1_st, 16 * b)
                        dve.wait_ge(s_spare, 48)
                        dve.wait_ge(s_xr, 16 * (b + 1))
                    dve.tensor_tensor(x1[:, i, :], bank[4 + i % 2][:, 0:D], x_res[:, i, :], ALU.add).then_inc(s_res, 1)
                    dve.wait_ge(s_res, TILES * b + i + 1)
                    dve.bn_stats(bn6[:, i, :], x1[:, i, :])

                store_oT(0)
                store_oT(1)
                residual(0)
                store_oT(2)
                residual(1)
                store_oT(3)
                residual(2)
                if more:
                    low_xT(b + 1)
                residual(3)
                dve.drain()
                for i in range(TILES):
                    ins = dve.bn_aggr(mv[:, i, :], bn6[:, i, :])
                link(ins)
                dve.tensor_scalar(ln_s[:, 0, :], mv[:, :, 1], EPS_LN, None, ALU.add).then_inc(s_var, 1)
                dve.wait_ge(s_std, b + 1)
                link(dve.reciprocal(ln_s[:, 2, :], ln_s[:, 1, :]))
                for i in range(TILES):
                    ins = dve.tensor_scalar(x1[:, i, :], x1[:, i, :], mv[:, i, 0:1], ln_s[:, 2, i:i + 1],
                                            ALU.subtract, ALU.mult)
                ins.then_inc(s_x1, 1)
                if more:
                    keys_first(b + 1)
                    keys_second(b + 1)
                dve.wait_ge(s_x1t_mm, 2 * b + 2)
                dve.tensor_copy(x1T[:, 1, :], bank[1][:, :]).then_inc(s_x1t_d, 1)
                if more:
                    store_qT(n1, 0)

                logits = bank[5][:, 0:TILES * E].rearrange("p (i e) -> p i e", e=E)
                dve.wait_ge(s_log, b + 1)
                link(dve.tensor_reduce(rt_m[:, 0, :], logits, AX.X, ALU.max))
                dve.tensor_tensor(rt_p[:, :, :], logits, bc(rt_m[:, 0, :].unsqueeze(2), [P, TILES, E]),
                                  ALU.subtract).then_inc(s_logd, 1)
                dve.wait_ge(s_rexp, b + 1)
                link(dve.tensor_reduce(rt_m[:, 1, :], rt_e[:, :, :], AX.X, ALU.add))
                link(dve.reciprocal(rt_m[:, 2, :], rt_m[:, 1, :]))
                dve.tensor_tensor(rt_p[:, :, :], rt_e[:, :, :], bc(rt_m[:, 2, :].unsqueeze(2), [P, TILES, E]), ALU.mult)
                dve.drain()
                for i in range(TILES):
                    dve.max(top[:, i, :], rt_p[:, i, :])
                dve.drain()
                for i in range(TILES):
                    ins = dve.max_index(top_ix[:, i, :], top[:, i, :], rt_p[:, i, :])
                link(ins)
                dve.tensor_reduce(rt_m[:, 3, :], top[:, :, 0:TOPK], AX.X, ALU.add)
                link(dve.tensor_copy(top_f[:, :, :], top_ix[:, :, :]))
                link(dve.tensor_scalar(rt_m[:, 0, :], rt_m[:, 3, :], 1e-20, None, ALU.add))
                dve.reciprocal(rt_m[:, 1, :], rt_m[:, 0, :])
                four = [P, TILES, TOPK, E]
                iota_b = bc(const("iota_e").unsqueeze(1).unsqueeze(1), four)
                link(dve.tensor_tensor(onehot[:, :, :, :], iota_b, bc(top_f[:, :, 0:TOPK].unsqueeze(3), four),
                                       ALU.is_equal))
                dve.tensor_reduce(chosen[:, :, :], onehot[:, :, :, :].rearrange("p i k e -> p i e k"), AX.X,
                                  ALU.max).then_inc(s_cho, 1)
                dve.wait_ge(s_scat, SCAT * b)
                link(dve.tensor_scalar(ids_now[:, :], ids_now[:, :], float(S), None, ALU.add))
                link(dve.tensor_copy(entry[:, :, :, 0], bc(ids_now[:, :].unsqueeze(2), [P, TILES, TOPK])))
                def hidden(i):
                    m = TILES * b + i
                    dve.wait_ge(s_silu, m + 1)
                    dve.tensor_tensor(sh_s[i % 2][:, :], sh_s[i % 2][:, :], bank[1 + 2 * (i % 2)][:, 0:FS],
                                      ALU.mult).then_inc(s_sh, 1)

                if more:
                    hidden(0)
                    hidden(1)
                    store_qT(n1 + 1, 1)
                    store_keyT(b + 1)
                places = bank[5][:, 0:TILES * E].rearrange("p (i e) -> p i e", e=E)
                dve.wait_ge(s_pos, b + 1)
                dve.tensor_scalar(slot_inv[:, :, :], places, float(CAP), DROPPED, ALU.is_ge, ALU.mult)
                dve.tensor_tensor(slot_e[:, :, :], places, bc(const("e_cap").unsqueeze(1), [P, TILES, E]),
                                  ALU.add).then_inc(s_slots_read, 1)
                link(dve.tensor_reduce(run_add[:, :], chosen[:, :, :].rearrange("p i e -> p e i"), AX.X, ALU.add))
                ins = dve.tensor_tensor(run[:, :], run[:, :], run_add[:, :], ALU.add)
                if not more:
                    ins.then_inc(s_run, 1)
                link(dve.tensor_tensor(slot_e[:, :, :], slot_e[:, :, :], slot_inv[:, :, :], ALU.add))
                link(dve.tensor_tensor(picked[:, :, :, :], onehot[:, :, :, :], bc(slot_e[:, :, :].unsqueeze(2), four),
                                       ALU.mult))
                link(dve.tensor_reduce(slot[:, :, :], picked[:, :, :, :], AX.X, ALU.add))
                dve.tensor_copy(slot_u[:, :], slot[:, :, :].rearrange("p i k -> p (i k)")).then_inc(s_slot, 1)
                if not more:
                    hidden(0)
                    hidden(1)

                def store_hT(i):
                    m = TILES * b + i
                    dve.wait_ge(s_sht_mm, m + 1)
                    dve.tensor_copy(sh_hT[:, 0:2, :], bank[4][:, 0:2 * P].rearrange("p (c t) -> p c t", c=2))
                    dve.tensor_copy(sh_hT[0:SHC[2][1], 2, :], bank[4][0:SHC[2][1], 2 * P:3 * P]).then_inc(s_sht, 1)

                def add_shared(i):
                    m = TILES * b + i
                    dve.wait_ge(s_sd, m + 1)
                    if i == 0:
                        dve.wait_ge(s_acc_st, 16 * b)
                    dve.tensor_tensor(acc[:, i, :], bank[5][:, 0:D], x1[:, i, :], ALU.add).then_inc(s_acc, 1)

                store_hT(0)
                hidden(2)
                if not more:
                    count_blocks()
                add_shared(0)
                store_hT(1)
                hidden(3)
                if not more:
                    blocks_before()
                add_shared(1)
                store_hT(2)
                if not more:
                    block_experts()
                add_shared(2)
                store_hT(3)
                if not more:
                    block_rows()
                add_shared(3)
                if more:
                    first_maxima(n1)
                link.end()

            def first_maxima(n0):
                maxima(n0, 0)
                maxima(n0 + 1, 1)
                store_qT(n0 + 2, 2)

            low_xT(0)
            keys_first(0)
            store_qT(0, 0)
            keys_second(0)
            store_qT(1, 1)
            store_keyT(0)
            first_maxima(0)
            with dve.Fori(0, B - 1) as b:
                units(b)
                finish(b, True)
            units(B - 1)
            finish(B - 1, False)

            dve.wait_ge(s_bt, 1)
            dve.tensor_copy(exp_i[:, :], bank[7][0:1, 0:P]).then_inc(s_blk, 1)
            dve.wait_ge(s_bt, 2)
            dve.memset(tok_u[:, NBLK:], 0)
            dve.tensor_copy(tok_u[:, 0:NBLK], bank[5][:, 0:P])
            dve.tensor_copy(slot_w[:, :], bank[5][:, P:2 * P]).then_inc(s_blk, 1)

            def block_xT(m, u):
                dve.wait_ge(s_mx_mm, m + 1)
                dve.tensor_copy(xgT[u], bank[u][:, 0:D]).then_inc(s_mxT, 1)

            def block_hidden(m, u):
                dve.wait_ge(s_msilu, m + 1)
                dve.tensor_tensor(hid[u], silu_g[u], bank[2 + u][:, F:2 * F], ALU.mult).then_inc(s_mh, 1)

            def block_hT(m, u):
                dve.wait_ge(s_mht_mm, m + 1)
                dve.tensor_copy(hidT[u], bank[4 + u][0:FH, 0:2 * P]).then_inc(s_mhT, 1)

            block_xT(0, 0)
            block_xT(1, 1)
            block_hidden(0, 0)
            with dve.Fori(0, NBLK // 2 - 1) as it:
                for u in range(2):
                    m = 2 * it + u
                    block_xT(m + 2, u)
                    block_hT(m, u)
                    block_hidden(m + 1, 1 - u)
            block_hT(NBLK - 2, 0)
            block_hidden(NBLK - 1, 1)
            block_hT(NBLK - 1, 1)

            link = Links(s_link3, None)
            link.start(0)

            def statistics(q):
                dve.wait_ge(s_sum, q + 1)
                for i in range(TILES):
                    ins = dve.bn_stats(bn6[:, i, :], sums[q][0][:, i, :])
                link(ins)
                for i in range(TILES):
                    ins = dve.bn_aggr(out_mv[:, q, i, :], bn6[:, i, :])
                link(ins)
                dve.tensor_scalar(out_s[:, q, 0, :], out_mv[:, q, :, 1], EPS_LN, None, ALU.add).then_inc(s_cvar, 1)

            def rows_out(q):
                dve.wait_ge(s_cstd, q + 1)
                link(dve.reciprocal(out_s[:, q, 2, :], out_s[:, q, 1, :]))
                dve.scalar_tensor_tensor(out=out_s[:, q, 0, :], in0=out_mv[:, q, :, 0], scalar=-1.0,
                                         in1=out_s[:, q, 2, :], op0=ALU.mult, op1=ALU.mult).then_inc(s_cbias, 1)
                for i in range(ACT_TILES, TILES):
                    ins = dve.tensor_scalar(sums[q][0][:, i, :], sums[q][0][:, i, :], out_mv[:, q, i, 0:1],
                                            out_s[:, q, 2, i:i + 1], ALU.subtract, ALU.mult)
                ins.then_inc(s_cout, 1)

            for q in range(B):
                statistics(q)
                if q > 0:
                    rows_out(q - 1)
            rows_out(B - 1)

        @block.gpsimd
        def _(pool):
            pool.wait_ge(s_const, 16)

            def rotate(n, b, i):
                s = i % 2
                c = bc2(cos2[:, i % TILES, :])
                q = q_raw[s]
                pool.wait_ge(s_rope, n)
                pool.wait_ge(s_qcopy, n + 1)
                pool.tensor_tensor(rope_a[:, :, :], q[:, :, 0:ROPE], c, ALU.mult)
                pool.tensor_tensor(rope_b[:, :, :], q[:, :, 0:ROPE], bc2(sin2[:, i % TILES, :]), ALU.mult).then_inc(s_rope_c, 1)
                pool.wait_ge(s_rope_c, n + 1)
                pool.tensor_tensor(q[:, :, 0:HALF], rope_a[:, :, 0:HALF], rope_b[:, :, HALF:ROPE], ALU.subtract)
                pool.tensor_tensor(q[:, :, HALF:ROPE], rope_a[:, :, HALF:ROPE], rope_b[:, :, 0:HALF], ALU.add).then_inc(s_rope, 1)

            def bc2(ap):
                return ap.unsqueeze(1).broadcast_to([P, 2, ROPE])

            def scatter_ready(b):
                pool.wait_ge(s_slot, b + 1)
                pool.tensor_tensor(entry[:, :, :, 1], top[:, :, 0:TOPK],
                                   rt_m[:, 1, :].unsqueeze(2).broadcast_to([P, TILES, TOPK]), ALU.mult)
                pool.drain()

            def scatter(c):
                pool.indirect_dma_start(table_dram, bass.IndirectOffsetOnAxis(slot_u[:, c:c + 1], 0),
                                        entry[:, c // TOPK, c % TOPK, :], None, bounds_check=E * CAP - 1,
                                        oob_is_err=False).then_inc(s_scat, 16)

            def units(b, first_pair):
                with pool.Fori(first_pair, PAIRS - 1) as p:
                    for i in range(TILES):
                        rotate(UNITS * b + TILES * p + i + 4, b, i)

            PAIRS_BETWEEN = 3
            per_turn = TILES * TOPK // (PAIRS_BETWEEN * TILES)
            pool.wait_ge(s_table0, 16)
            for i in range(TILES):
                rotate(i, 0, i)
            units(0, 0)
            with pool.Fori(1, B) as b:
                for i in range(TILES):
                    rotate(UNITS * b + i, b, i)
                scatter_ready(b - 1)
                for t in range(PAIRS_BETWEEN * TILES):
                    rotate(UNITS * b + t + 4, b, t)
                    for c in range(per_turn):
                        scatter(per_turn * t + c)
                units(b, PAIRS_BETWEEN)
            scatter_ready(B - 1)
            for c in range(TILES * TOPK):
                scatter(c)

            pool.wait_ge(s_row, 1)
            pool.wait_ge(s_scat, SCAT * B)
            pool.indirect_dma_start(rows[:, :, :].rearrange("p c a -> p (c a)"), None,
                                    table_dram.rearrange("(r c) a -> r (c a)", c=P),
                                    bass.IndirectOffsetOnAxis(row_u[:, 0:1], 0)).then_inc(s_rows, 16)
            pool.wait_ge(s_x1_st, 16 * B)
            pool.wait_ge(s_acc_st, 16 * B)
            pool.wait_ge(s_spare, 48)
            pool.wait_ge(s_blk, 2)

            def gather(m, index):
                pool.indirect_dma_start(xg[m % 4], None, x1_dram,
                                        bass.IndirectOffsetOnAxis(index, 0)).then_inc(s_g[m % 4], 16)

            pool.tensor_copy(first_ix[:, :], tok_u[:, 0:AHEAD])
            pool.tensor_copy(block_ix[:, 7, :], tok_u[:, 0:AHEAD + 1:AHEAD]).then_inc(s_ix, 1)
            pool.wait_ge(s_ix, 1)
            for m in range(AHEAD):
                if m >= 4:
                    pool.wait_ge(s_mx_mm, m - 3)
                gather(m, first_ix[:, m:m + 1])

            def block_turn(it, r, left):
                m = 8 * it + r
                pool.wait_ge(s_my, m + 2)
                pool.wait_ge(s_add[r % 2], 64 * it + 16 * (r // 2))
                pool.wait_ge(s_ix, m + 1)
                pool.tensor_copy(block_ix[:, r, :], tok_u[:, bass.ds(m + 1, 2, AHEAD)]).then_inc(s_ix, 1)
                now = (r - 1) % 8
                if left > AHEAD:
                    gather(r + AHEAD, block_ix[:, now, 1:2])
                pool.indirect_dma_start(sum_dram[r % 2], bass.IndirectOffsetOnAxis(block_ix[:, now, 0:1], 0),
                                        y_out[r % 4], None, compute_op=ALU.add).then_inc(s_add[r % 2], 16)

            with pool.Fori(0, NBLK // 8 - 1) as it:
                for r in range(8):
                    block_turn(it, r, NBLK)
            for r in range(8):
                block_turn(NBLK // 8 - 1, r, 8 - r)

            for q in range(B):
                pool.wait_ge(s_cld[q], 32)
                pool.tensor_tensor(sums[q][0], sums[q][0], sums[q][1], ALU.add).then_inc(s_sum, 1)


_INS = ["L0_attn_x", "L0_attn_wq", "L0_attn_wkv_a", "L0_attn_wkv_b", "L0_attn_wo", "L0_attn_kv_norm_w",
        "L0_ffn_wg_router", "L0_ffn_w_gate", "L0_ffn_w_up", "L0_ffn_w_down", "L0_ffn_ws_gate", "L0_ffn_ws_up",
        "L0_ffn_ws_down"]


def shape_constants():
    import numpy as np

    freqs = 1.0 / 10000.0 ** (np.arange(0, ROPE, 2, dtype=np.float32) / ROPE)
    ang = np.outer(np.arange(S, dtype=np.float32), freqs)
    p = np.arange(P)

    def rope(t):
        t = t.reshape(TILES, P, HALF).transpose(1, 0, 2)
        return np.concatenate([t, t], axis=2).reshape(P, TILES * ROPE)

    def rows(v):
        return np.broadcast_to(v, (P, v.size))

    e = np.arange(E)
    parts = {
        "ident": np.eye(P),
        "mask": np.where(p[None, :] > p[:, None], -1e30, 0.0),
        "before": (p[:, None] < p[None, :]),
        "ones": np.ones((P, P)),
        "cos2": rope(np.cos(ang)),
        "sin2": rope(np.sin(ang)),
        "iota_e": rows(e),
        "e_cap": rows(e * CAP),
        "j_128": rows(np.arange(CAPB) * P),
        "part": p[:, None],
        "ids": p[:, None] + P * np.arange(TILES)[None, :] - S,
        "tri": rows((e[None, :] < e[:, None]).reshape(-1)),
    }
    return np.concatenate([parts[k].astype(np.float32) for k in CONSTS], axis=1)


def kernel(**inputs):
    import numpy as np
    import concourse.bacc as bacc
    from concourse.bass_utils import run_bass_kernel_spmd

    nc = bacc.Bacc("TRN2", target_bir_lowering=False, num_devices=1)
    arrays, args = {}, []
    for name in _INS:
        arrays[name] = np.ascontiguousarray(inputs[name])
    arrays["shape_constants"] = np.ascontiguousarray(shape_constants())
    empty = np.zeros((E * CAP, 2), np.float32)
    empty[:, 0] = B * S + np.arange(E * CAP) % P
    arrays["empty_table"] = empty
    for name, a in arrays.items():
        args.append(nc.dram_tensor(name, a.shape, mybir.dt.from_np(a.dtype), kind="ExternalInput").ap())
    out = nc.dram_tensor("out", (B, S, D), F32, kind="ExternalOutput").ap()
    layer_kernel(nc, *args, out)
    r = run_bass_kernel_spmd(nc, [arrays], core_ids=[0])
    return r.results[0]["out"]
```
